# Optimizing a Trainium2 kernel written in Bass

```python
import numpy as np
import jax
import jax.numpy as jnp

def _softmax(x, axis=-1):
    return jax.nn.softmax(x, axis=axis)

def _gelu(x):
    return jax.nn.gelu(x, approximate=True)

def _silu(x):
    return jax.nn.silu(x)

def _sigmoid(x):
    return jax.nn.sigmoid(x)

def _layernorm(x, axis=-1, eps=1e-05):
    m = jnp.mean(x, axis=axis, keepdims=True)
    v = jnp.var(x, axis=axis, keepdims=True)
    return (x - m) / jnp.sqrt(v + eps)

def _scatter_add(tgt, idx, src, axis=0):
    return tgt.at[idx].add(src)

def _segment_sum(src, seg, n):
    return jax.ops.segment_sum(src, seg, n)
kernel_name = 'mk_xattn_ffn_d4_seqx_r4_b090d6'

def setup_inputs(seed: int=0):
    np.random.seed(seed)
    _w = jnp.asarray

    def _rec_inputs():
        import jax
        import jax.numpy as jnp
        _rk = jax.random.key(seed)
        x = 7.22e-05 + 1 * jax.random.normal(jax.random.fold_in(_rk, 1), (2, 1024, 256), jnp.float32)
        _lenS = 1024 - jax.random.randint(jax.random.fold_in(_rk, 7), (2,), 0, max(1, 1024 // 4) + 1, jnp.int32)
        _lenS2 = 77 - jax.random.randint(jax.random.fold_in(_rk, 8), (2,), 0, max(1, 77 // 4) + 1, jnp.int32)
        _ctx_1024P = jax.random.normal(jax.random.fold_in(_rk, 11), (2, 16, 256), jnp.float32)
        _ctx_1024c = jax.random.dirichlet(jax.random.fold_in(_rk, 511), 0.3 * jnp.ones((16,), jnp.float32), (2, 77))
        _ctx_1024t = jnp.einsum('bsk,bkd->bsd', _ctx_1024c, _ctx_1024P)
        _ctx_1024t = _ctx_1024t * jax.lax.rsqrt(jnp.mean(jnp.square(_ctx_1024t)) + 1e-12) * 0.953939
        ctx_1024 = 4.13588e-05 + 0.999923 * (_ctx_1024t + 0.3 * jax.random.normal(jax.random.fold_in(_rk, 611), (2, 77, 256), jnp.float32))
        fside_Bx16xSxS2_0 = -6.00028e-06 + 0.100001 * jax.random.normal(jax.random.fold_in(_rk, 12), (2, 16, 1024, 77), jnp.float32)
        _validS = jnp.arange(1024)[None, :] < _lenS[:, None]
        _validS2 = jnp.arange(77)[None, :] < _lenS2[:, None]
        _causal = jnp.tril(jnp.ones((1024, 1024), dtype=bool))
        mask_Bx1xS2_ik0 = jnp.where(jnp.broadcast_to(_validS2[:, None, :], (2, 1, 77)), 0, 1).astype(jnp.int32)
        mask_Bx1xSxS2_bf0 = jnp.logical_not(jnp.ones((2, 1, 1024, 77), dtype=bool))
        return (x, ctx_1024, fside_Bx16xSxS2_0, mask_Bx1xS2_ik0, mask_Bx1xSxS2_bf0)
    x, ctx_1024, fside_Bx16xSxS2_0, mask_Bx1xS2_ik0, mask_Bx1xSxS2_bf0 = _rec_inputs()

    def _L0_xattn_setup():
        import jax, jax.numpy as jnp
        import numpy as np
        EMBED_DIM = 256
        HIDDEN_DIM = 16 * 64
        SCALE = 64 ** (-0.5)
        key = jax.random.key(seed)
        ks = jax.random.split(key, 12)
        B, S = (4, 512)
        std_in = EMBED_DIM ** (-0.5)
        std_h = HIDDEN_DIM ** (-0.5)
        return {'query': jax.random.normal(ks[0], (B, S, EMBED_DIM), jnp.float32), 'key': jax.random.normal(ks[1], (B, S, EMBED_DIM), jnp.float32), 'value': jax.random.normal(ks[2], (B, S, EMBED_DIM), jnp.float32), 'Wq': jax.random.normal(ks[3], (HIDDEN_DIM, EMBED_DIM), jnp.float32) * std_in, 'bq': jnp.zeros((HIDDEN_DIM,), jnp.float32), 'Wk': jax.random.normal(ks[4], (HIDDEN_DIM, EMBED_DIM), jnp.float32) * std_in, 'bk': jnp.zeros((HIDDEN_DIM,), jnp.float32), 'Wv': jax.random.normal(ks[5], (HIDDEN_DIM, EMBED_DIM), jnp.float32) * std_in, 'bv': jnp.zeros((HIDDEN_DIM,), jnp.float32), 'Wo': jax.random.normal(ks[6], (EMBED_DIM, HIDDEN_DIM), jnp.float32) * std_h, 'bo': jnp.zeros((EMBED_DIM,), jnp.float32)}
    _L0_xattn_all = _L0_xattn_setup()
    _L0_xattn_in = {k: v for k, v in _L0_xattn_all.items() if k in ('Wq', 'bq', 'Wk', 'bk', 'Wv', 'bv', 'Wo', 'bo')}
    del _L0_xattn_all

    def _L0_ffn_setup():
        import jax, jax.numpy as jnp
        import numpy as np

        def _ste(w, w_q):
            return w + jax.lax.stop_gradient(w_q - w)

        def quantize_w8_per(w, axis):
            amax = jnp.clip(jnp.max(jnp.abs(w), axis=axis, keepdims=True), 1e-08, None)
            scale = 127.0 / amax
            w_q = jnp.clip(jnp.round(w * scale), -128.0, 127.0) / scale
            return _ste(w, w_q)

        def quantize_a16(x):
            amax = jnp.clip(jnp.max(jnp.abs(x)), 1e-08, None)
            scale = 32767.0 / amax
            x_q = jnp.clip(jnp.round(x * scale), -32768.0, 32767.0) / scale
            return _ste(x, x_q)
        key = jax.random.key(seed)
        k1, k2, k3 = jax.random.split(key, 3)
        d_model, d_ff = (256, 1024)
        x = jax.random.normal(k1, (4, 512, d_model), dtype=jnp.float32)
        W_in = jax.random.normal(k2, (d_model, d_ff), dtype=jnp.float32) / np.sqrt(d_model)
        b_in = jnp.zeros((d_ff,), dtype=jnp.float32)
        W_out = jax.random.normal(k3, (d_ff, d_model), dtype=jnp.float32) / np.sqrt(d_ff)
        b_out = jnp.zeros((d_model,), dtype=jnp.float32)
        return {'x': x, 'W_in': W_in, 'b_in': b_in, 'W_out': W_out, 'b_out': b_out}
    _L0_ffn_all = _L0_ffn_setup()
    _L0_ffn_in = {k: v for k, v in _L0_ffn_all.items() if k in ('W_in', 'b_in', 'W_out', 'b_out')}
    del _L0_ffn_all

    def _L1_xattn_setup():
        import jax, jax.numpy as jnp
        import numpy as np
        import math
        H = 16
        D = 256
        FF = 1024
        DK = D // H
        EPS = 1e-05

        def layer_norm(x, g, b):
            mu = jnp.mean(x, axis=-1, keepdims=True)
            var = jnp.var(x, axis=-1, keepdims=True)
            return (x - mu) * jax.lax.rsqrt(var + EPS) * g + b
        key = jax.random.key(seed)
        ks = jax.random.split(key, 16)
        B, S = (2, 512)
        s = 1.0 / math.sqrt(D)
        return {'x_q': jax.random.normal(ks[0], (B, S, D), jnp.float32), 'x_kv': jax.random.normal(ks[1], (B, S, D), jnp.float32), 'bias': jax.random.normal(ks[2], (B, H, S, S), jnp.float32) * 0.1, 'Wq': jax.random.normal(ks[3], (D, D), jnp.float32) * s, 'Wk': jax.random.normal(ks[4], (D, D), jnp.float32) * s, 'Wv': jax.random.normal(ks[5], (D, D), jnp.float32) * s, 'Wo': jax.random.normal(ks[6], (D, D), jnp.float32) * s, 'W1': jax.random.normal(ks[7], (FF, D), jnp.float32) * s, 'b1': jnp.zeros((FF,), jnp.float32), 'W2': jax.random.normal(ks[8], (D, FF), jnp.float32) * (1.0 / math.sqrt(FF)), 'b2': jnp.zeros((D,), jnp.float32), 'g1': jnp.ones((D,), jnp.float32), 'be1': jnp.zeros((D,), jnp.float32), 'g2': jnp.ones((D,), jnp.float32), 'be2': jnp.zeros((D,), jnp.float32)}
    _L1_xattn_all = _L1_xattn_setup()
    _L1_xattn_in = {k: v for k, v in _L1_xattn_all.items() if k in ('Wq', 'Wk', 'Wv', 'Wo', 'W1', 'b1', 'W2', 'b2', 'g1', 'be1', 'g2', 'be2')}
    del _L1_xattn_all

    def _L1_ffn_setup():
        import jax, jax.numpy as jnp
        import numpy as np
        D = 256
        H = 16
        DK = D // H
        E = 8
        DFF = 4 * D
        TOPK = 2
        EPS = 1e-05

        def _layernorm(x, g, b):
            m = jnp.mean(x, axis=-1, keepdims=True)
            v = jnp.mean(jnp.square(x - m), axis=-1, keepdims=True)
            return (x - m) * jax.lax.rsqrt(v + EPS) * g + b
        key = jax.random.key(seed)
        ks = jax.random.split(key, 16)
        s_in = 1.0 / np.sqrt(D)
        s_ff = 1.0 / np.sqrt(DFF)
        return {'x': jax.random.normal(ks[0], (2, 512, D), dtype=jnp.float32), 'ln1_g': jnp.ones((D,), jnp.float32), 'ln1_b': jnp.zeros((D,), jnp.float32), 'w_qkv': jax.random.normal(ks[1], (D, 3 * D), jnp.float32) * s_in, 'b_qkv': jnp.zeros((3 * D,), jnp.float32), 'w_o': jax.random.normal(ks[2], (D, D), jnp.float32) * s_in, 'b_o': jnp.zeros((D,), jnp.float32), 'ln2_g': jnp.ones((D,), jnp.float32), 'ln2_b': jnp.zeros((D,), jnp.float32), 'gate_w': jax.random.normal(ks[3], (D, E), jnp.float32) * s_in, 'gate_b': jnp.zeros((E,), jnp.float32), 'W1': jax.random.normal(ks[4], (E, D, DFF), jnp.float32) * s_in, 'b1': jnp.zeros((E, DFF), jnp.float32), 'W2': jax.random.normal(ks[5], (E, DFF, D), jnp.float32) * s_ff, 'b2': jnp.zeros((E, D), jnp.float32)}
    _L1_ffn_all = _L1_ffn_setup()
    _L1_ffn_in = {k: v for k, v in _L1_ffn_all.items() if k in ('ln1_g', 'ln1_b', 'w_qkv', 'b_qkv', 'w_o', 'b_o', 'ln2_g', 'ln2_b', 'gate_w', 'gate_b', 'W1', 'b1', 'W2', 'b2')}
    del _L1_ffn_all

    def _L2_xattn_setup():
        import jax, jax.numpy as jnp
        import numpy as np
        D_MODEL = 256
        NEG_BIG = -1000000000.0
        key = jax.random.key(seed)
        kq, kk, kv, km = jax.random.split(key, 4)
        B, S, D = (4, 512, D_MODEL)
        q = jax.random.normal(kq, (B, S, D), dtype=jnp.float32)
        k = jax.random.normal(kk, (B, S, D), dtype=jnp.float32)
        v = jax.random.normal(kv, (B, S, D), dtype=jnp.float32)
        mask = jax.random.randint(km, (B, 1, S), 0, 2, dtype=jnp.int32)
        return {'q': q, 'k': k, 'v': v, 'mask': mask}
    _L2_xattn_all = _L2_xattn_setup()
    _L2_xattn_in = {k: v for k, v in _L2_xattn_all.items() if k in ()}
    del _L2_xattn_all

    def _L2_ffn_setup():
        import jax, jax.numpy as jnp
        import numpy as np
        B, S, D, H, E = (4, 512, 256, 1024, 8)
        THRESHOLD = 0.5
        key = jax.random.key(seed)
        ks = jax.random.split(key, 7)
        s_in = 1.0 / np.sqrt(D)
        s_h = 1.0 / np.sqrt(H)
        return {'x': jax.random.normal(ks[0], (B, S, D), dtype=jnp.float32), 'Wg': jax.random.uniform(ks[1], (D, E), jnp.float32, -s_in, s_in), 'bg': jax.random.uniform(ks[2], (E,), jnp.float32, -s_in, s_in), 'W1': jax.random.uniform(ks[3], (E, D, H), jnp.float32, -s_in, s_in), 'b1': jax.random.uniform(ks[4], (E, H), jnp.float32, -s_in, s_in), 'W2': jax.random.uniform(ks[5], (E, H, D), jnp.float32, -s_h, s_h), 'b2': jax.random.uniform(ks[6], (E, D), jnp.float32, -s_h, s_h)}
    _L2_ffn_all = _L2_ffn_setup()
    _L2_ffn_in = {k: v for k, v in _L2_ffn_all.items() if k in ('Wg', 'bg', 'W1', 'b1', 'W2', 'b2')}
    del _L2_ffn_all

    def _L3_xattn_setup():
        import jax, jax.numpy as jnp
        import numpy as np
        D_MODEL = 256
        NUM_HEAD = 16
        DK = D_MODEL // NUM_HEAD
        B, S = (4, 512)
        NEG = -1000000000.0
        key = jax.random.key(seed)
        ks = jax.random.split(key, 12)
        sc = 1.0 / np.sqrt(D_MODEL)
        return {'q': jax.random.normal(ks[0], (B, S, D_MODEL), jnp.float32), 'k': jax.random.normal(ks[1], (B, S, D_MODEL), jnp.float32), 'v': jax.random.normal(ks[2], (B, S, D_MODEL), jnp.float32), 'mask': jnp.zeros((B, 1, S, S), dtype=bool), 'wq': jax.random.normal(ks[3], (D_MODEL, D_MODEL), jnp.float32) * sc, 'bq': jnp.zeros((D_MODEL,), jnp.float32), 'wk': jax.random.normal(ks[4], (D_MODEL, D_MODEL), jnp.float32) * sc, 'bk': jnp.zeros((D_MODEL,), jnp.float32), 'wv': jax.random.normal(ks[5], (D_MODEL, D_MODEL), jnp.float32) * sc, 'bv': jnp.zeros((D_MODEL,), jnp.float32), 'wo': jax.random.normal(ks[6], (D_MODEL, D_MODEL), jnp.float32) * sc, 'bo': jnp.zeros((D_MODEL,), jnp.float32)}
    _L3_xattn_all = _L3_xattn_setup()
    _L3_xattn_in = {k: v for k, v in _L3_xattn_all.items() if k in ('wq', 'bq', 'wk', 'bk', 'wv', 'bv', 'wo', 'bo')}
    del _L3_xattn_all

    def _L3_ffn_setup():
        import jax, jax.numpy as jnp
        import numpy as np
        B, S, H, FFN, E = (2, 512, 256, 1024, 8)
        key = jax.random.key(seed)
        k0, k1, k2, k3 = jax.random.split(key, 4)
        return {'hidden_states': jax.random.normal(k0, (B, S, H), dtype=jnp.float32), 'Wr': jax.random.normal(k1, (H, E), dtype=jnp.float32) * 0.02, 'br': jnp.zeros((E,), dtype=jnp.float32), 'W1': jax.random.normal(k2, (E, H, FFN), dtype=jnp.float32) * 0.02, 'W2': jax.random.normal(k3, (E, FFN, H), dtype=jnp.float32) * 0.02}
    _L3_ffn_all = _L3_ffn_setup()
    _L3_ffn_in = {k: v for k, v in _L3_ffn_all.items() if k in ('Wr', 'br', 'W1', 'W2')}
    del _L3_ffn_all
    return {'x': x, 'ctx_1024': ctx_1024, 'fside_Bx16xSxS2_0': fside_Bx16xSxS2_0, 'mask_Bx1xS2_ik0': mask_Bx1xS2_ik0, 'mask_Bx1xSxS2_bf0': mask_Bx1xSxS2_bf0, 'L0_xattn_Wq': _L0_xattn_in['Wq'], 'L0_xattn_bq': _L0_xattn_in['bq'], 'L0_xattn_Wk': _L0_xattn_in['Wk'], 'L0_xattn_bk': _L0_xattn_in['bk'], 'L0_xattn_Wv': _L0_xattn_in['Wv'], 'L0_xattn_bv': _L0_xattn_in['bv'], 'L0_xattn_Wo': _L0_xattn_in['Wo'], 'L0_xattn_bo': _L0_xattn_in['bo'], 'L0_ffn_W_in': _L0_ffn_in['W_in'], 'L0_ffn_b_in': _L0_ffn_in['b_in'], 'L0_ffn_W_out': _L0_ffn_in['W_out'], 'L0_ffn_b_out': _L0_ffn_in['b_out'], 'L1_xattn_Wq': _L1_xattn_in['Wq'], 'L1_xattn_Wk': _L1_xattn_in['Wk'], 'L1_xattn_Wv': _L1_xattn_in['Wv'], 'L1_xattn_Wo': _L1_xattn_in['Wo'], 'L1_xattn_W1': _L1_xattn_in['W1'], 'L1_xattn_b1': _L1_xattn_in['b1'], 'L1_xattn_W2': _L1_xattn_in['W2'], 'L1_xattn_b2': _L1_xattn_in['b2'], 'L1_xattn_g1': _L1_xattn_in['g1'], 'L1_xattn_be1': _L1_xattn_in['be1'], 'L1_xattn_g2': _L1_xattn_in['g2'], 'L1_xattn_be2': _L1_xattn_in['be2'], 'L1_ffn_ln1_g': _L1_ffn_in['ln1_g'], 'L1_ffn_ln1_b': _L1_ffn_in['ln1_b'], 'L1_ffn_w_qkv': _L1_ffn_in['w_qkv'], 'L1_ffn_b_qkv': _L1_ffn_in['b_qkv'], 'L1_ffn_w_o': _L1_ffn_in['w_o'], 'L1_ffn_b_o': _L1_ffn_in['b_o'], 'L1_ffn_ln2_g': _L1_ffn_in['ln2_g'], 'L1_ffn_ln2_b': _L1_ffn_in['ln2_b'], 'L1_ffn_gate_w': _L1_ffn_in['gate_w'], 'L1_ffn_gate_b': _L1_ffn_in['gate_b'], 'L1_ffn_W1': _L1_ffn_in['W1'], 'L1_ffn_b1': _L1_ffn_in['b1'], 'L1_ffn_W2': _L1_ffn_in['W2'], 'L1_ffn_b2': _L1_ffn_in['b2'], 'L2_ffn_Wg': _L2_ffn_in['Wg'], 'L2_ffn_bg': _L2_ffn_in['bg'], 'L2_ffn_W1': _L2_ffn_in['W1'], 'L2_ffn_b1': _L2_ffn_in['b1'], 'L2_ffn_W2': _L2_ffn_in['W2'], 'L2_ffn_b2': _L2_ffn_in['b2'], 'L3_xattn_wq': _L3_xattn_in['wq'], 'L3_xattn_bq': _L3_xattn_in['bq'], 'L3_xattn_wk': _L3_xattn_in['wk'], 'L3_xattn_bk': _L3_xattn_in['bk'], 'L3_xattn_wv': _L3_xattn_in['wv'], 'L3_xattn_bv': _L3_xattn_in['bv'], 'L3_xattn_wo': _L3_xattn_in['wo'], 'L3_xattn_bo': _L3_xattn_in['bo'], 'L3_ffn_Wr': _L3_ffn_in['Wr'], 'L3_ffn_br': _L3_ffn_in['br'], 'L3_ffn_W1': _L3_ffn_in['W1'], 'L3_ffn_W2': _L3_ffn_in['W2']}

def reference(x, ctx_1024, fside_Bx16xSxS2_0, mask_Bx1xS2_ik0, mask_Bx1xSxS2_bf0, L0_xattn_Wq, L0_xattn_bq, L0_xattn_Wk, L0_xattn_bk, L0_xattn_Wv, L0_xattn_bv, L0_xattn_Wo, L0_xattn_bo, L0_ffn_W_in, L0_ffn_b_in, L0_ffn_W_out, L0_ffn_b_out, L1_xattn_Wq, L1_xattn_Wk, L1_xattn_Wv, L1_xattn_Wo, L1_xattn_W1, L1_xattn_b1, L1_xattn_W2, L1_xattn_b2, L1_xattn_g1, L1_xattn_be1, L1_xattn_g2, L1_xattn_be2, L1_ffn_ln1_g, L1_ffn_ln1_b, L1_ffn_w_qkv, L1_ffn_b_qkv, L1_ffn_w_o, L1_ffn_b_o, L1_ffn_ln2_g, L1_ffn_ln2_b, L1_ffn_gate_w, L1_ffn_gate_b, L1_ffn_W1, L1_ffn_b1, L1_ffn_W2, L1_ffn_b2, L2_ffn_Wg, L2_ffn_bg, L2_ffn_W1, L2_ffn_b1, L2_ffn_W2, L2_ffn_b2, L3_xattn_wq, L3_xattn_bq, L3_xattn_wk, L3_xattn_bk, L3_xattn_wv, L3_xattn_bv, L3_xattn_wo, L3_xattn_bo, L3_ffn_Wr, L3_ffn_br, L3_ffn_W1, L3_ffn_W2):
    import jax
    import jax.numpy as jnp

    def _L0_xattn_ref(query, key, value, Wq, bq, Wk, bk, Wv, bv, Wo, bo):
        import jax, jax.numpy as jnp
        import numpy as np
        EMBED_DIM = 256
        HIDDEN_DIM = 16 * 64
        SCALE = 64 ** (-0.5)
        q = jnp.einsum('bsd,hd->bsh', query, Wq) + bq
        k = jnp.einsum('bsd,hd->bsh', key, Wk) + bk
        v = jnp.einsum('bsd,hd->bsh', value, Wv) + bv
        scores = jnp.einsum('bqh,bkh->bqk', q, k) * SCALE
        attn = jax.nn.softmax(scores, axis=1)
        out = jnp.einsum('bqk,bkh->bqh', attn, v)
        return jnp.einsum('bqh,dh->bqd', out, Wo) + bo

    def _L0_ffn_ref(x, W_in, b_in, W_out, b_out):
        import jax, jax.numpy as jnp
        import numpy as np

        def _ste(w, w_q):
            return w + jax.lax.stop_gradient(w_q - w)

        def quantize_w8_per(w, axis):
            amax = jnp.clip(jnp.max(jnp.abs(w), axis=axis, keepdims=True), 1e-08, None)
            scale = 127.0 / amax
            w_q = jnp.clip(jnp.round(w * scale), -128.0, 127.0) / scale
            return _ste(w, w_q)

        def quantize_a16(x):
            amax = jnp.clip(jnp.max(jnp.abs(x)), 1e-08, None)
            scale = 32767.0 / amax
            x_q = jnp.clip(jnp.round(x * scale), -32768.0, 32767.0) / scale
            return _ste(x, x_q)
        W_in_sim = quantize_w8_per(W_in, axis=0)
        W_out_sim = quantize_w8_per(W_out, axis=1)
        x_sim = quantize_a16(x)
        hidden = jax.nn.gelu(x_sim @ W_in_sim + b_in, approximate=False)
        hidden_sim = quantize_a16(hidden)
        out = hidden_sim @ W_out_sim + b_out
        return out

    def _L1_xattn_ref(x_q, x_kv, bias, Wq, Wk, Wv, Wo, W1, b1, W2, b2, g1, be1, g2, be2):
        import jax, jax.numpy as jnp
        import numpy as np
        import math
        H = 16
        D = 256
        FF = 1024
        DK = D // H
        EPS = 1e-05

        def layer_norm(x, g, b):
            mu = jnp.mean(x, axis=-1, keepdims=True)
            var = jnp.var(x, axis=-1, keepdims=True)
            return (x - mu) * jax.lax.rsqrt(var + EPS) * g + b
        B, S, _ = x_q.shape

        def split(x):
            return x.reshape(B, -1, H, DK).transpose(0, 2, 1, 3)
        q = split(x_q @ Wq.T)
        k = split(x_kv @ Wk.T)
        v = split(x_kv @ Wv.T)
        scores = jnp.einsum('bhqd,bhkd->bhqk', q, k) / math.sqrt(DK) + bias
        p = jax.nn.softmax(scores, axis=-1)
        o = jnp.einsum('bhqk,bhkd->bhqd', p, v)
        o = o.transpose(0, 2, 1, 3).reshape(B, S, D)
        x = x_q + o @ Wo.T
        h = jax.nn.gelu(layer_norm(x, g1, be1) @ W1.T + b1, approximate=False)
        x = x + h @ W2.T + b2
        return layer_norm(x, g2, be2)

    def _L1_ffn_ref(x, ln1_g, ln1_b, w_qkv, b_qkv, w_o, b_o, ln2_g, ln2_b, gate_w, gate_b, W1, b1, W2, b2):
        import jax, jax.numpy as jnp
        import numpy as np
        D = 256
        H = 16
        DK = D // H
        E = 8
        DFF = 4 * D
        TOPK = 2
        EPS = 1e-05

        def _layernorm(x, g, b):
            m = jnp.mean(x, axis=-1, keepdims=True)
            v = jnp.mean(jnp.square(x - m), axis=-1, keepdims=True)
            return (x - m) * jax.lax.rsqrt(v + EPS) * g + b
        B, S, _ = x.shape
        h = _layernorm(x, ln1_g, ln1_b)
        qkv = h @ w_qkv + b_qkv
        q, k, v = jnp.split(qkv, 3, axis=-1)
        q = q.reshape(B, S, H, DK)
        k = k.reshape(B, S, H, DK)
        v = v.reshape(B, S, H, DK)
        scores = jnp.einsum('bqhd,bkhd->bhqk', q, k) / np.sqrt(DK)
        attn = jax.nn.softmax(scores, axis=-1)
        o = jnp.einsum('bhqk,bkhd->bqhd', attn, v).reshape(B, S, D)
        x = x + o @ w_o + b_o
        h = _layernorm(x, ln2_g, ln2_b).reshape(B * S, D)
        logits = h @ gate_w + gate_b
        topv, topi = jax.lax.top_k(logits, TOPK)
        gw = jax.nn.softmax(topv, axis=-1)
        ew = jnp.sum(jax.nn.one_hot(topi, E, dtype=h.dtype) * gw[..., None], axis=1)
        hid = jax.nn.relu(jnp.einsum('td,edf->etf', h, W1) + b1[:, None, :])
        out_e = jnp.einsum('etf,efd->etd', hid, W2) + b2[:, None, :]
        moe = jnp.einsum('etd,te->td', out_e, ew)
        return x + moe.reshape(B, S, D)

    def _L2_xattn_ref(q, k, v, mask):
        import jax, jax.numpy as jnp
        import numpy as np
        D_MODEL = 256
        NEG_BIG = -1000000000.0
        scale = jnp.asarray(D_MODEL, q.dtype) ** (-0.5)
        logits = jnp.einsum('bqd,bkd->bqk', q, k) * scale
        logits = logits + mask.astype(q.dtype) * NEG_BIG
        weights = jax.nn.softmax(logits, axis=-1)
        return jnp.einsum('bqk,bkd->bqd', weights, v)

    def _L2_ffn_ref(x, Wg, bg, W1, b1, W2, b2):
        import jax, jax.numpy as jnp
        import numpy as np
        B, S, D, H, E = (4, 512, 256, 1024, 8)
        THRESHOLD = 0.5
        b, s, d = x.shape
        x_flat = x.reshape(-1, d)
        probs = jax.nn.sigmoid(x_flat @ Wg + bg)
        mask = (probs > THRESHOLD).astype(x_flat.dtype)
        weights = probs * mask
        h = jax.nn.relu(jnp.einsum('td,edh->eth', x_flat, W1) + b1[:, None, :])
        expert_out = jnp.einsum('eth,ehd->etd', h, W2) + b2[:, None, :]
        combined = jnp.einsum('te,etd->td', weights, expert_out)
        return combined.reshape(b, s, d)

    def _L3_xattn_ref(q, k, v, mask, wq, bq, wk, bk, wv, bv, wo, bo):
        import jax, jax.numpy as jnp
        import numpy as np
        D_MODEL = 256
        NUM_HEAD = 16
        DK = D_MODEL // NUM_HEAD
        B, S = (4, 512)
        NEG = -1000000000.0
        b, s, _ = q.shape
        Q = (q @ wq + bq).reshape(b, s, NUM_HEAD, DK).transpose(0, 2, 1, 3)
        K = (k @ wk + bk).reshape(b, -1, NUM_HEAD, DK).transpose(0, 2, 1, 3)
        V = (v @ wv + bv).reshape(b, -1, NUM_HEAD, DK).transpose(0, 2, 1, 3)
        score = jnp.einsum('bhqd,bhkd->bhqk', Q, K) / np.sqrt(DK)
        score = jnp.where(mask, NEG, score)
        attn = jax.nn.softmax(score, axis=-1)
        x = jnp.einsum('bhqk,bhkd->bhqd', attn, V)
        x = x.transpose(0, 2, 1, 3).reshape(b, s, NUM_HEAD * DK)
        return x @ wo + bo

    def _L3_ffn_ref(hidden_states, Wr, br, W1, W2):
        import jax, jax.numpy as jnp
        import numpy as np
        B, S, H, FFN, E = (2, 512, 256, 1024, 8)
        b, s, h = hidden_states.shape
        x = hidden_states.reshape(-1, h)
        route = jax.nn.sigmoid(x @ Wr + br)
        max_prob = jnp.max(route, axis=1, keepdims=True)
        max_ind = jnp.argmax(route, axis=1)
        out = jnp.zeros_like(x)
        n_experts = Wr.shape[1]
        for e in range(n_experts):
            mask = (max_ind == e)[:, None].astype(x.dtype)
            y = jax.nn.gelu(x @ W1[e], approximate=False) @ W2[e]
            out = out + mask * y
        out = out * max_prob
        return out.reshape(b, s, h)
    x = x + _L0_xattn_ref(_layernorm(x, axis=-1), ctx_1024, ctx_1024, L0_xattn_Wq, L0_xattn_bq, L0_xattn_Wk, L0_xattn_bk, L0_xattn_Wv, L0_xattn_bv, L0_xattn_Wo, L0_xattn_bo)
    x = x + _L0_ffn_ref(_layernorm(x, axis=-1), L0_ffn_W_in, L0_ffn_b_in, L0_ffn_W_out, L0_ffn_b_out)
    x = x + _L1_xattn_ref(_layernorm(x, axis=-1), ctx_1024, fside_Bx16xSxS2_0, L1_xattn_Wq, L1_xattn_Wk, L1_xattn_Wv, L1_xattn_Wo, L1_xattn_W1, L1_xattn_b1, L1_xattn_W2, L1_xattn_b2, L1_xattn_g1, L1_xattn_be1, L1_xattn_g2, L1_xattn_be2)
    x = x + _L1_ffn_ref(_layernorm(x, axis=-1), L1_ffn_ln1_g, L1_ffn_ln1_b, L1_ffn_w_qkv, L1_ffn_b_qkv, L1_ffn_w_o, L1_ffn_b_o, L1_ffn_ln2_g, L1_ffn_ln2_b, L1_ffn_gate_w, L1_ffn_gate_b, L1_ffn_W1, L1_ffn_b1, L1_ffn_W2, L1_ffn_b2)
    x = x + _L2_xattn_ref(_layernorm(x, axis=-1), ctx_1024, ctx_1024, mask_Bx1xS2_ik0)
    x = x + _L2_ffn_ref(_layernorm(x, axis=-1), L2_ffn_Wg, L2_ffn_bg, L2_ffn_W1, L2_ffn_b1, L2_ffn_W2, L2_ffn_b2)
    x = x + _L3_xattn_ref(_layernorm(x, axis=-1), ctx_1024, ctx_1024, mask_Bx1xSxS2_bf0, L3_xattn_wq, L3_xattn_bq, L3_xattn_wk, L3_xattn_bk, L3_xattn_wv, L3_xattn_bv, L3_xattn_wo, L3_xattn_bo)
    x = x + _L3_ffn_ref(_layernorm(x, axis=-1), L3_ffn_Wr, L3_ffn_br, L3_ffn_W1, L3_ffn_W2)
    return x

_drawn_inputs = setup_inputs


def setup_inputs(seed=0):
    import zlib

    import numpy as np

    out = dict(_drawn_inputs(seed))
    spreads = {'L0_xattn_bq': (0.0, 0.8),
     'L0_xattn_bk': (0.0, 0.1),
     'L0_xattn_bv': (0.0, 0.309),
     'L0_xattn_bo': (0.0, 0.1),
     'L0_ffn_b_in': (0.0, 0.1),
     'L0_ffn_b_out': (0.0, 0.1),
     'L1_xattn_b1': (0.0, 0.1),
     'L1_xattn_b2': (0.0, 0.1),
     'L1_xattn_g1': (1.0, 0.2),
     'L1_xattn_be1': (0.0, 0.1),
     'L1_xattn_g2': (1.0, 0.2),
     'L1_xattn_be2': (0.0, 0.1),
     'L1_ffn_ln1_g': (1.0, 0.2),
     'L1_ffn_ln1_b': (0.0, 0.1),
     'L1_ffn_b_qkv': (0.0, 0.1),
     'L1_ffn_b_o': (0.0, 0.1),
     'L1_ffn_ln2_g': (1.0, 0.2),
     'L1_ffn_ln2_b': (0.0, 0.1),
     'L1_ffn_gate_b': (0.0, 0.1),
     'L1_ffn_b1': (0.0, 0.442),
     'L1_ffn_b2': (0.0, 0.331),
     'L3_xattn_bq': (0.0, 0.8),
     'L3_xattn_bk': (0.0, 0.8),
     'L3_xattn_bv': (0.0, 0.282),
     'L3_xattn_bo': (0.0, 0.268),
     'L3_ffn_br': (0.0, 0.624)}
    factors = {'fside_Bx16xSxS2_0': 5.146,
     'L2_ffn_bg': 4.422,
     'L2_ffn_b1': 8.0,
     'L2_ffn_b2': 8.0,
     'L3_ffn_Wr': 2.986,
     'L3_ffn_W1': 2.844,
     'L3_ffn_W2': 2.775}
    for name, (base, spread) in spreads.items():
        noise = np.random.default_rng([zlib.crc32(name.encode()), seed]).standard_normal(out[name].shape)
        drawn = base * np.exp(spread * noise) if base else spread * noise
        out[name] = jnp.asarray(drawn.astype(out[name].dtype))
    for name, factor in factors.items():
        out[name] = (out[name] * factor).astype(out[name].dtype)
    return out
```

```python
from contextlib import ExitStack

import concourse.bass as bass
from concourse import mybir

ALU = mybir.AluOpType
ACT = mybir.ActivationFunctionType
F32 = mybir.dt.float32
BF16 = mybir.dt.bfloat16
I32 = mybir.dt.int32
U8 = mybir.dt.uint8
AX = mybir.AxisListType.X

P = 128
BATCH, SEQ, D = 2, 1024, 256
TOK = BATCH * SEQ
NT = TOK // P
KD = D // P
KEYS = 77
HEADS, DK = 16, 16
FF = 1024
FB = FF // P
EXPERTS = 8
CH = 512
NCH = TOK // CH
EPS = 1e-5
NEG = -1e9
SEM_RANGES = (range(140, 190), range(190, 240))
ROUND = 12582912.0


class Core:

    def __init__(self, nc, ctx, dram):
        self.nc, self.dram = nc, dram
        sb = lambda name, shape, dt=F32: ctx.enter_context(nc.sbuf_tensor(name, shape, dt))
        self.x = sb("x_resid", [P, NT, D])
        self.xn = sb("x_norm", [P, NT, D])
        self.xnT = sb("x_normT", [P, KD, TOK])
        self.ctxT = sb("ctxT_sb", [P, KD, BATCH * KEYS])
        self.ident = sb("ident", [P, P])
        self.ident_bf = sb("ident_bf", [P, P], BF16)
        self.ps = ctx.enter_context(nc.psum_tensor("banks", [P, 8, CH], F32))
        self.side, self.taken = 0, 0

    def semaphore(self, ctx, name):
        s = self.nc.alloc_semaphore(name=name, num=SEM_RANGES[self.side][self.taken])
        ctx.callback(self.nc.release_semaphore, s)
        self.taken += 1
        return s

    def stage(self, ctx):
        self.side, self.taken = 1 - self.side, 0
        self.nc.gpsimd.sem_clear(SEM_RANGES[self.side])
        return ctx.enter_context(self.nc.Block())


def bcast(ap, n):
    return ap.unsqueeze(0).broadcast_to([n] + list(ap.shape))


def load_inputs(core):
    nc, dram = core.nc, core.dram
    with ExitStack() as ctx:
        loaded = core.semaphore(ctx, "in_loaded")
        ident_ready = core.semaphore(ctx, "in_ident")
        block = core.stage(ctx)

        @block.sync
        def _(sp):
            sp.dma_start(core.x[:], dram["x"].rearrange("b (t p) d -> p (b t) d", p=P)).then_inc(loaded, 16)
            sp.dma_start(core.ident[:], dram["identity"]).then_inc(loaded, 16)
            sp.dma_start(core.ctxT[:], dram["ctxT"].rearrange("(k p) n -> p k n", p=P)).then_inc(loaded, 16)
            sp.wait_ge(loaded, 48)

        @block.vector
        def _(dve):
            dve.wait_ge(loaded, 48)
            dve.tensor_copy(core.ident_bf[:], core.ident[:]).then_inc(ident_ready, 1)
            dve.wait_ge(ident_ready, 1)


def layer_norm(core, name, src, dst, dstT=None, gainT=None, shiftT=None, gain=None, shift=None, absmax=None):
    nc = core.nc
    with ExitStack() as ctx:
        sb = lambda n, shape, dt=F32: ctx.enter_context(nc.sbuf_tensor(f"{name}_{n}", shape, dt))
        sem = lambda n: core.semaphore(ctx, f"{name}_{n}")
        stats, moments = sb("stats", [P, NT, 6]), sb("moments", [P, NT, 2])
        std, rstd = sb("std", [P, NT]), sb("rstd", [P, NT])
        stats_done, moments_done, std_done, rstd_done = sem("stats"), sem("moments"), sem("std"), sem("rstd")
        tile_normed, transposed, evacuated, gains_in = sem("normed"), sem("transposed"), sem("evac"), sem("gains")
        affine_done = sem("affine")
        if gainT is not None:
            gT, sT = sb("gainT", [P, KD]), sb("shiftT", [P, KD])
        if gain is not None:
            g_bc, s_bc = sb("gain", [P, D]), sb("shift", [P, D])
        block = core.stage(ctx)

        @block.sync
        def _(sp):
            if gainT is not None:
                sp.dma_start(gT[:], gainT).then_inc(gains_in, 16)
                sp.dma_start(sT[:], shiftT).then_inc(gains_in, 16)
                sp.wait_ge(gains_in, 32)
            if gain is not None:
                sp.dma_start(g_bc[:], bcast(gain, P)).then_inc(gains_in, 16)
                sp.dma_start(s_bc[:], bcast(shift, P)).then_inc(gains_in, 16)
                sp.wait_ge(gains_in, 32)

        def evacuate(eng, is_act, g, k):
            out, in_ = dstT[:, k, g * CH:(g + 1) * CH], core.ps[:, 2 * g + k, :]
            if gainT is not None:
                if is_act:
                    return eng.activation(out, in_, ACT.Identity, bias=sT[:, k:k + 1], scale=gT[:, k:k + 1])
                return eng.tensor_scalar(out, in_, gT[:, k:k + 1], sT[:, k:k + 1], ALU.mult, ALU.add)
            return eng.copy(out, in_) if is_act else eng.tensor_copy(out, in_)

        @block.vector
        def _(dve):
            for t in range(NT):
                dve.bn_stats(stats[:, t, :], src[:, t, :]).then_inc(stats_done, 1)
            for t in range(NT):
                dve.wait_ge(stats_done, t + 1)
                dve.bn_aggr(moments[:, t, :], stats[:, t, :]).then_inc(moments_done, 1)
            dve.wait_ge(moments_done, NT)
            dve.tensor_scalar(moments[:, :, 1], moments[:, :, 1], EPS, None, ALU.add).then_inc(moments_done, 1)
            dve.wait_ge(std_done, 1)
            dve.reciprocal(rstd[:], std[:]).then_inc(rstd_done, 1)
            dve.wait_ge(rstd_done, 1)
            for t in range(NT):
                dve.tensor_scalar(dst[:, t, :], src[:, t, :], moments[:, t, 0:1], rstd[:, t:t + 1],
                                  ALU.subtract, ALU.mult).then_inc(tile_normed, 1)
            if gain is not None:
                dve.wait_ge(gains_in, 32)
                dve.wait_ge(tile_normed, NT)
                dve.tensor_tensor(dst[:], dst[:], g_bc[:].unsqueeze(1).broadcast_to([P, NT, D]), ALU.mult).then_inc(affine_done, 1)
                dve.wait_ge(affine_done, 1)
                dve.tensor_tensor(dst[:], dst[:], s_bc[:].unsqueeze(1).broadcast_to([P, NT, D]), ALU.add).then_inc(affine_done, 1)
            if absmax is not None:
                dve.wait_ge(tile_normed, NT)
                dve.tensor_reduce(absmax[:, 0:1], dst[:], mybir.AxisListType.XY, ALU.max, apply_absolute_value=True).then_inc(affine_done, 1)
            if dstT is not None:
                if gainT is not None:
                    dve.wait_ge(gains_in, 32)
                for g in range(NCH):
                    dve.wait_ge(transposed, 2 * g + 2)
                    evacuate(dve, False, g, 1).then_inc(evacuated, 1)

        @block.scalar
        def _(act):
            act.wait_ge(moments_done, NT + 1)
            act.activation(std[:], moments[:, :, 1], ACT.Sqrt).then_inc(std_done, 1)
            if dstT is not None:
                if gainT is not None:
                    act.wait_ge(gains_in, 32)
                for g in range(NCH):
                    act.wait_ge(transposed, 2 * g + 1)
                    evacuate(act, True, g, 0).then_inc(evacuated, 1)

        if dstT is not None:
            @block.tensor
            def _(pe):
                for g in range(NCH):
                    pe.wait_ge(tile_normed, 4 * g + 4)
                    for k in range(KD):
                        for j in range(4):
                            mm = pe.transpose(core.ps[:, 2 * g + k, j * P:(j + 1) * P],
                                              dst[:, 4 * g + j, k * P:(k + 1) * P], core.ident[:])
                        mm.then_inc(transposed, 1)


def transpose_tokens(core, name, src, dstT):
    nc = core.nc
    with ExitStack() as ctx:
        transposed = core.semaphore(ctx, f"{name}_transposed")
        evacuated = core.semaphore(ctx, f"{name}_evac")
        block = core.stage(ctx)

        @block.tensor
        def _(pe):
            for g in range(NCH):
                for k in range(KD):
                    for j in range(4):
                        mm = pe.transpose(core.ps[:, 2 * g + k, j * P:(j + 1) * P],
                                          src[:, 4 * g + j, k * P:(k + 1) * P], core.ident[:])
                    mm.then_inc(transposed, 1)

        @block.vector
        def _(dve):
            for g in range(NCH):
                dve.wait_ge(transposed, 2 * g + 2)
                dve.tensor_copy(dstT[:, 1, g * CH:(g + 1) * CH], core.ps[:, 2 * g + 1, :]).then_inc(evacuated, 1)

        @block.scalar
        def _(act):
            for g in range(NCH):
                act.wait_ge(transposed, 2 * g + 1)
                act.copy(dstT[:, 0, g * CH:(g + 1) * CH], core.ps[:, 2 * g, :]).then_inc(evacuated, 1)


def query_softmax_attention(core):
    nc, dram, ps = core.nc, core.dram, core.ps
    W = BATCH * KEYS
    SCALE = 64 ** -0.5
    with ExitStack() as ctx:
        sb = lambda n, shape, dt=F32: ctx.enter_context(nc.sbuf_tensor(f"a0_{n}", shape, dt))
        sem = lambda n: core.semaphore(ctx, f"a0_{n}")
        wkT, wvT = sb("wkT", [P, KD, FF]), sb("wvT", [P, KD, FF])
        wq, woT = sb("wq", [P, FB, D]), sb("woT", [P, FB, D])
        bq, bk, bv = sb("bq", [P, FB]), sb("bk", [P, FB]), sb("bv", [P, FB])
        bo = sb("bo", [P, D])
        kT, vT = sb("kT", [P, FB, W]), sb("vT", [P, FB, W])
        gT = sb("gT", [P, KD, W])
        cT = sb("cT", [KEYS, BATCH])
        vo = sb("vo", [KEYS, BATCH, D])
        ET = sb("ET", [KEYS, BATCH, SEQ])
        mx, tmp, nb = sb("mx", [KEYS, BATCH]), sb("tmp", [KEYS, BATCH]), sb("nb", [KEYS, BATCH])
        sums, rs = sb("sums", [KEYS, BATCH]), sb("rs", [KEYS, BATCH])
        loaded, kv_mm, k_sb, v_sb, g_mm, g_sb = sem("loaded"), sem("kv_mm"), sem("k_sb"), sem("v_sb"), sem("g_mm"), sem("g_sb")
        s_mm, chain, bias_ready, exp_done, v_ready, y_mm, y_sb = (
            sem("s_mm"), sem("chain"), sem("bias"), sem("exp"), sem("v"), sem("y_mm"), sem("y_sb"))
        block = core.stage(ctx)

        @block.sync
        def _(sp):
            for dst, key, pat in ((wkT, "L0_WkT", "(k p) f -> p k f"), (wvT, "L0_WvT", "(k p) f -> p k f"),
                                  (wq, "L0_Wq", "(f p) d -> p f d"), (woT, "L0_WoT", "(f p) d -> p f d")):
                sp.dma_start(dst[:], dram[key].rearrange(pat, p=P)).then_inc(loaded, 16)
            for dst, key in ((bq, "L0_bq"), (bk, "L0_bk"), (bv, "L0_bv")):
                sp.dma_start(dst[:], dram[key]).then_inc(loaded, 16)
            sp.dma_start(bo[:], bcast(dram["L0_bo"], P)).then_inc(loaded, 16)
            sp.wait_ge(loaded, 128)

        @block.tensor
        def _(pe):
            pe.wait_ge(loaded, 128)
            for i, w in enumerate((wkT, wvT)):
                for f in range(FB):
                    for k in range(KD):
                        mm = pe.matmul(ps[:, 4 * i + f // 2, (f % 2) * W:(f % 2 + 1) * W], w[:, k, f * P:(f + 1) * P],
                                       core.ctxT[:, k, :], start=(k == 0), stop=(k == KD - 1))
                mm.then_inc(kv_mm, 1)
            pe.wait_ge(k_sb, FB // 2)
            for m in range(KD):
                for f in range(FB):
                    mm = pe.matmul(ps[:, m, 0:W], wq[:, f, m * P:(m + 1) * P], kT[:, f, :], start=(f == 0), stop=(f == FB - 1))
            mm.then_inc(g_mm, 1)
            for b in range(BATCH):
                for f in range(FB):
                    mm = pe.matmul(ps[0:KEYS, 2 + b, 0:1], kT[:, f, b * KEYS:(b + 1) * KEYS], bq[:, f:f + 1],
                                   start=(f == 0), stop=(f == FB - 1))
            mm.then_inc(g_mm, 1)
            pe.wait_ge(v_sb, FB // 2)
            for b in range(BATCH):
                for f in range(FB):
                    mm = pe.matmul(ps[0:KEYS, 4 + b, 0:D], vT[:, f, b * KEYS:(b + 1) * KEYS], woT[:, f, :],
                                   start=(f == 0), stop=(f == FB - 1))
            mm.then_inc(g_mm, 1)
            pe.wait_ge(g_sb, 3)
            for b in range(BATCH):
                for c in range(2):
                    for k in range(KD):
                        mm = pe.matmul(ps[0:KEYS, 2 * b + c, :], gT[:, k, b * KEYS:(b + 1) * KEYS],
                                       core.xnT[:, k, b * SEQ + c * CH:b * SEQ + (c + 1) * CH], start=(k == 0), stop=(k == KD - 1))
                mm.then_inc(s_mm, 1)
            for b in range(BATCH):
                pe.wait_ge(exp_done, b + 1)
                pe.wait_ge(v_ready, b + 1)
                for t in range(NT // BATCH):
                    n = b * 8 + t
                    if n >= 4:
                        pe.wait_ge(y_sb, n - 3)
                    pe.matmul(ps[:, 4 + n % 4, 0:D], ET[:, b, t * P:(t + 1) * P], vo[:, b, :], start=True, stop=True).then_inc(y_mm, 1)

        @block.scalar
        def _(act):
            act.wait_ge(kv_mm, 1)
            for f in range(FB):
                ins = act.activation(kT[:, f, :], ps[:, f // 2, (f % 2) * W:(f % 2 + 1) * W], ACT.Identity, bias=bk[:, f:f + 1])
                if f % 2:
                    ins.then_inc(k_sb, 1)
            for b in range(BATCH):
                act.wait_ge(bias_ready, b + 1)
                act.activation(ET[:, b, :], ps[0:KEYS, 2 * b:2 * b + 2, :], ACT.Exp, bias=nb[:, b:b + 1], scale=SCALE,
                               accum_out=sums[:, b:b + 1]).then_inc(exp_done, 1)

        @block.vector
        def _(dve):
            count = [0]

            def link(ins):
                count[0] += 1
                ins.then_inc(chain, 1)
                dve.wait_ge(chain, count[0])

            dve.wait_ge(loaded, 128)
            link(dve.tensor_tensor(core.x[:], core.x[:], bo[:].unsqueeze(1).broadcast_to([P, NT, D]), ALU.add))
            dve.wait_ge(kv_mm, 2)
            for f in range(FB):
                ins = dve.tensor_scalar(vT[:, f, :], ps[:, 4 + f // 2, (f % 2) * W:(f % 2 + 1) * W], bv[:, f:f + 1], None, ALU.add)
                if f % 2:
                    ins.then_inc(v_sb, 1)
            dve.wait_ge(g_mm, 1)
            dve.tensor_copy(gT[:], ps[:, 0:KD, 0:W]).then_inc(g_sb, 1)
            dve.wait_ge(g_mm, 2)
            dve.tensor_copy(cT[:], ps[0:KEYS, 2:4, 0]).then_inc(g_sb, 1)
            dve.wait_ge(g_mm, 3)
            dve.tensor_copy(vo[:], ps[0:KEYS, 4:6, 0:D]).then_inc(g_sb, 1)
            dve.wait_ge(g_sb, 3)
            for b in range(BATCH):
                col = slice(b, b + 1)
                dve.wait_ge(s_mm, b + 1)
                link(dve.tensor_reduce(mx[:, col], ps[0:KEYS, 2 * b:2 * b + 2, :], mybir.AxisListType.XY, ALU.max))
                link(dve.tensor_scalar(tmp[:, col], mx[:, col], cT[:, col], -1.0, ALU.add, ALU.mult))
                link(dve.tensor_scalar(tmp[:, col], tmp[:, col], cT[:, col], None, ALU.add))
                dve.tensor_scalar(nb[:, col], tmp[:, col], SCALE, None, ALU.mult).then_inc(bias_ready, 1)
            for b in range(BATCH):
                dve.wait_ge(exp_done, b + 1)
                link(dve.reciprocal(rs[:, b:b + 1], sums[:, b:b + 1]))
                dve.tensor_scalar(vo[:, b, :], vo[:, b, :], rs[:, b:b + 1], None, ALU.mult).then_inc(v_ready, 1)
            for n in range(NT):
                dve.wait_ge(y_mm, n + 1)
                dve.tensor_tensor(core.x[:, n, :], core.x[:, n, :], ps[:, 4 + n % 4, 0:D], ALU.add).then_inc(y_sb, 1)


def quantised_ffn(core, xmax):
    nc, dram, ps = core.nc, core.dram, core.ps
    with ExitStack() as ctx:
        sb = lambda n, shape, dt=F32: ctx.enter_context(nc.sbuf_tensor(f"q_{n}", shape, dt))
        sem = lambda n: core.semaphore(ctx, f"q_{n}")
        w_inT = sb("w_inT", [P, FB, D])
        w_out = sb("w_out", [P, FB, D])
        w_in = sb("w_in", [P, KD, FF])
        b_in, b_out = sb("b_in", [P, FB]), sb("b_out", [P, D])
        amax, scale, inv = sb("amax", [P, 2 * FB]), sb("scale", [P, 2 * FB]), sb("inv", [P, 2 * FB])
        xs, hs = sb("xs", [P, 4]), sb("hs", [P, 4])
        hid = sb("hid", [P, FB, TOK])
        hmaxes, hmax = sb("hmaxes", [P, FB * NCH]), sb("hmax", [P, 1])
        loaded, chain, wq_done, wT_mm, wT_sb, xq_done = sem("loaded"), sem("chain"), sem("wq"), sem("wT_mm"), sem("wT_sb"), sem("xq")
        xT_mm, xT_sb, h_mm, h_sb, xred, hred, hmax_done, hq_done, y_mm, y_sb, scales_done = (
            sem("xT_mm"), sem("xT_sb"), sem("h_mm"), sem("h_sb"), sem("xred"), sem("hred"), sem("hmax"),
            sem("hq"), sem("y_mm"), sem("y_sb"), sem("scales"))
        block = core.stage(ctx)

        @block.sync
        def _(sp):
            sp.dma_start(w_inT[:], dram["L0_WinT"].rearrange("(f p) d -> p f d", p=P)).then_inc(loaded, 16)
            sp.dma_start(w_out[:], dram["L0_Wout"].rearrange("(f p) d -> p f d", p=P)).then_inc(loaded, 16)
            sp.dma_start(b_in[:], dram["L0_bin"]).then_inc(loaded, 16)
            sp.dma_start(b_out[:], bcast(dram["L0_bout"], P)).then_inc(loaded, 16)
            sp.wait_ge(loaded, 64)

        @block.gpsimd
        def _(pool):
            pool.partition_all_reduce(xs[:, 0:1], xmax[:, 0:1], P, bass.bass_isa.ReduceOp.max).then_inc(xred, 1)
            pool.wait_ge(hmax_done, FB * NCH + 1)
            pool.partition_all_reduce(hs[:, 0:1], hmax[:, 0:1], P, bass.bass_isa.ReduceOp.max).then_inc(hred, 1)

        @block.vector
        def _(dve):
            count = [0]

            def link(ins):
                count[0] += 1
                ins.then_inc(chain, 1)
                dve.wait_ge(chain, count[0])

            def scales_of(s, top):
                link(dve.tensor_scalar(s[:, 0:1], s[:, 0:1], 1e-8, None, ALU.max))
                link(dve.reciprocal(s[:, 1:2], s[:, 0:1]))
                link(dve.tensor_scalar(s[:, 2:3], s[:, 1:2], top, None, ALU.mult))
                link(dve.tensor_scalar(s[:, 3:4], s[:, 0:1], 1.0 / top, None, ALU.mult))

            def quantise(v, s):
                link(dve.tensor_scalar(v, v, s, 32767.0, ALU.mult, ALU.min))
                link(dve.tensor_scalar(v, v, -32768.0, ROUND, ALU.max, ALU.add))
                return dve.tensor_scalar(v, v, ROUND, None, ALU.subtract)

            dve.wait_ge(loaded, 64)
            link(dve.tensor_tensor(core.x[:], core.x[:], b_out[:].unsqueeze(1).broadcast_to([P, NT, D]), ALU.add))
            for i, w in enumerate((w_inT, w_out)):
                link(dve.tensor_reduce(amax[:, i * FB:(i + 1) * FB], w[:], AX, ALU.max, apply_absolute_value=True))
            link(dve.tensor_scalar(amax[:], amax[:], 1e-8, None, ALU.max))
            link(dve.reciprocal(scale[:], amax[:]))
            link(dve.tensor_scalar(scale[:], scale[:], 127.0, None, ALU.mult))
            link(dve.tensor_scalar(inv[:], amax[:], 1.0 / 127.0, None, ALU.mult))
            for i, w in enumerate((w_inT, w_out)):
                for f in range(FB):
                    n = i * FB + f
                    link(dve.tensor_scalar(w[:, f, :], w[:, f, :], scale[:, n:n + 1], 127.0, ALU.mult, ALU.min))
                    link(dve.tensor_scalar(w[:, f, :], w[:, f, :], -128.0, ROUND, ALU.max, ALU.add))
                    if i == 0:
                        dve.tensor_scalar(w[:, f, :], w[:, f, :], ROUND, None, ALU.subtract).then_inc(wq_done, 1)
                    else:
                        dve.tensor_scalar(w[:, f, :], w[:, f, :], ROUND, inv[:, n:n + 1], ALU.subtract, ALU.mult).then_inc(wq_done, 1)
            dve.wait_ge(xred, 1)
            scales_of(xs, 32767.0)
            quantise(core.xn[:], xs[:, 2:3]).then_inc(xq_done, 1)
            dve.tensor_scalar(scale[:, 0:FB], inv[:, 0:FB], xs[:, 3:4], None, ALU.mult).then_inc(scales_done, 1)
            for k in range(KD):
                dve.wait_ge(wT_mm, k + 1)
                dve.tensor_copy(w_in[:, k, :].rearrange("p (c n) -> p c n", n=CH), ps[:, 2 * k:2 * k + 2, :]).then_inc(wT_sb, 1)
            for g in range(NCH):
                dve.wait_ge(xT_mm, g + 1)
                dve.tensor_copy(core.xnT[:, :, g * CH:(g + 1) * CH], ps[:, 4 + 2 * (g % 2):6 + 2 * (g % 2), :]).then_inc(xT_sb, 1)
            for n in range(FB * NCH):
                c, f = n // FB, n % FB
                dve.wait_ge(h_sb, n + 1)
                dve.tensor_reduce(hmaxes[:, n:n + 1], hid[:, f, c * CH:(c + 1) * CH], AX, ALU.max, apply_absolute_value=True).then_inc(hmax_done, 1)
            dve.wait_ge(hmax_done, FB * NCH)
            dve.tensor_reduce(hmax[:], hmaxes[:], AX, ALU.max).then_inc(hmax_done, 1)
            dve.wait_ge(hred, 1)
            scales_of(hs, 32767.0)
            for c in range(NCH):
                quantise(hid[:, :, c * CH:(c + 1) * CH], hs[:, 2:3]).then_inc(hq_done, 1)
            for t in range(NT):
                dve.wait_ge(y_mm, t + 1)
                dve.scalar_tensor_tensor(core.x[:, t, :], ps[:, 4 + t % 4, 0:D], hs[:, 3:4], core.x[:, t, :],
                                         ALU.mult, ALU.add).then_inc(y_sb, 1)

        @block.tensor
        def _(pe):
            pe.wait_ge(wq_done, FB)
            for k in range(KD):
                for f in range(FB):
                    mm = pe.transpose(ps[:, 2 * k + f // 4, (f % 4) * P:(f % 4 + 1) * P], w_inT[:, f, k * P:(k + 1) * P], core.ident[:])
                mm.then_inc(wT_mm, 1)
            pe.wait_ge(xq_done, 1)
            for g in range(NCH):
                if g >= 2:
                    pe.wait_ge(xT_sb, g - 1)
                for k in range(KD):
                    for j in range(4):
                        mm = pe.transpose(ps[:, 4 + 2 * (g % 2) + k, j * P:(j + 1) * P],
                                          core.xn[:, 4 * g + j, k * P:(k + 1) * P], core.ident[:])
                mm.then_inc(xT_mm, 1)
            pe.wait_ge(wT_sb, KD)
            for n in range(FB * NCH):
                c, f = n // FB, n % FB
                pe.wait_ge(xT_sb, c + 1)
                if n >= 4:
                    pe.wait_ge(h_sb, n - 3)
                for k in range(KD):
                    mm = pe.matmul(ps[:, n % 4, :], w_in[:, k, f * P:(f + 1) * P], core.xnT[:, k, c * CH:(c + 1) * CH],
                                   start=(k == 0), stop=(k == KD - 1))
                mm.then_inc(h_mm, 1)
            pe.wait_ge(wq_done, 2 * FB)
            for t in range(NT):
                pe.wait_ge(hq_done, t // 4 + 1)
                if t >= 4:
                    pe.wait_ge(y_sb, t - 3)
                for f in range(FB):
                    mm = pe.matmul(ps[:, 4 + t % 4, 0:D], hid[:, f, t * P:(t + 1) * P], w_out[:, f, :], start=(f == 0), stop=(f == FB - 1))
                mm.then_inc(y_mm, 1)

        @block.scalar
        def _(act):
            act.wait_ge(scales_done, 1)
            act.wait_ge(loaded, 64)
            for n in range(FB * NCH):
                c, f = n // FB, n % FB
                act.wait_ge(h_mm, n + 1)
                act.activation(hid[:, f, c * CH:(c + 1) * CH], ps[:, n % 4, :], ACT.Gelu, bias=b_in[:, f:f + 1],
                               scale=scale[:, f:f + 1]).then_inc(h_sb, 1)


def headed_cross_attention(core, name, wqT, wkT, wvT, woT, out, bias=None, mask=None, bq=None, bk=None, bv=None):
    nc, dram, ps = core.nc, core.dram, core.ps
    W = BATCH * KEYS
    HW = 4 * KEYS
    with ExitStack() as ctx:
        sb = lambda n, shape, dt=F32: ctx.enter_context(nc.sbuf_tensor(f"{name}_{n}", shape, dt))
        sem = lambda n: core.semaphore(ctx, f"{name}_{n}")
        w = {n: sb(n, [P, KD, D]) for n in ("wq", "wk", "wv", "wo")}
        qT, kT = sb("qT", [P, KD, TOK]), sb("kT", [P, KD, W])
        kbd = sb("kbd", [P, BATCH, KD, 8, KEYS])
        vh = sb("vh", [KEYS, BATCH, HEADS, DK + 1])
        head_of = sb("head_of", [P, 8])
        s = sb("s", [P, 2, HEADS, KEYS])
        mx = sb("mx", [P, 2, HEADS])
        pT = sb("pT", [KEYS, 2, HEADS, P])
        rs, on, oT = sb("rs", [P, 2, HEADS]), sb("on", [P, 2, D]), sb("oT", [P, 2, KD, P])
        if bias is not None:
            bt = sb("bt", [P, 3, HEADS, KEYS])
        else:
            mt, bt = sb("mt", [P, NT, KEYS], U8), sb("bt", [P, NT, KEYS])
        if bq is not None:
            bqT, bkT, bv_bc = sb("bqT", [P, KD]), sb("bkT", [P, KD]), sb("bv", [KEYS, D])
        loaded, bias_in = sem("loaded"), [sem(f"bias{i}") for i in range(3)]
        q_mm, q_sb, kv_mm, k_sb, kbd_done, v_sb, ones_done, limit_done = (
            sem("q_mm"), sem("q_sb"), sem("kv_mm"), sem("k_sb"), sem("kbd"), sem("v_sb"), sem("ones"), sem("limit"))
        s_mm, s_sb, chain, s_ready, exp_done, pT_mm, pT_sb, o_mm, o_sb, oT_mm, oT_sb, y_mm, y_sb = (
            sem(x) for x in ("s_mm", "s_sb", "chain", "s_ready", "exp", "pT_mm", "pT_sb", "o_mm", "o_sb", "oT_mm", "oT_sb", "y_mm", "y_sb"))
        loads = 5 + (3 if bq is not None else 0) + (1 if mask is not None else 0)
        block = core.stage(ctx)

        @block.sync
        def _(sp):
            for n, a in (("wq", wqT), ("wk", wkT), ("wv", wvT), ("wo", woT)):
                sp.dma_start(w[n][:], a.rearrange("(k p) d -> p k d", p=P)).then_inc(loaded, 16)
            sp.dma_start(head_of[:], dram["head_of"]).then_inc(loaded, 16)
            if bq is not None:
                sp.dma_start(bqT[:], bq).then_inc(loaded, 16)
                sp.dma_start(bkT[:], bk).then_inc(loaded, 16)
                sp.dma_start(bv_bc[:], bcast(bv, KEYS)).then_inc(loaded, 16)
            if mask is not None:
                sp.dma_start(mt[:], mask.rearrange("(t p) k -> p t k", p=P)).then_inc(loaded, 16)
            sp.wait_ge(loaded, 16 * loads)
            if bias is not None:
                for t in range(NT):
                    if t >= 3:
                        sp.wait_ge(s_sb, t - 2)
                    sp.dma_start(bt[:, t % 3, :, :], bias[t]).then_inc(bias_in[t % 3], 16)

        @block.gpsimd
        def _(pool):
            pool.memset(vh[:, :, :, DK:DK + 1], 1.0).then_inc(ones_done, 1)

        @block.vector
        def _(dve):
            count = [0]

            def link(ins):
                count[0] += 1
                ins.then_inc(chain, 1)
                dve.wait_ge(chain, count[0])

            dve.wait_ge(loaded, 16 * loads)
            if mask is not None:
                link(dve.tensor_scalar(bt[:], mt[:], -3e38, 3e38, ALU.mult, ALU.add))
                link(dve.scalar_tensor_tensor(bt[:], mt[:], NEG, bt[:], ALU.mult, ALU.add))
            dve.wait_ge(kv_mm, 1)
            for k in range(KD):
                if bk is not None:
                    link(dve.tensor_scalar(kT[:, k, :], ps[:, k, 0:W], bkT[:, k:k + 1], 0.25, ALU.add, ALU.mult))
                else:
                    link(dve.tensor_scalar(kT[:, k, :], ps[:, k, 0:W], 0.25, None, ALU.mult))
            for b in range(BATCH):
                for k in range(KD):
                    for h in range(8):
                        dve.tensor_scalar(kbd[:, b, k, h, :], kT[:, k, b * KEYS:(b + 1) * KEYS], head_of[:, h:h + 1], None,
                                          ALU.mult).then_inc(kbd_done, 1)
            dve.wait_ge(kv_mm, 2)
            for b in range(BATCH):
                vin = ps[0:KEYS, 2 + b, 0:D].rearrange("p (h d) -> p h d", d=DK)
                if bv is not None:
                    dve.tensor_tensor(vh[:, b, :, 0:DK], vin, bv_bc[:].rearrange("p (h d) -> p h d", d=DK), ALU.add).then_inc(v_sb, 1)
                else:
                    dve.tensor_copy(vh[:, b, :, 0:DK], vin).then_inc(v_sb, 1)

            def scores(t):
                i = t % 2
                dve.wait_ge(s_mm, t + 1)
                if t >= 2:
                    dve.wait_ge(pT_mm, 4 * (t - 1))
                raw = ps[:, 0:4, 0:HW].rearrange("p c (h k) -> p c h k", k=KEYS)
                si = s[:, i, :, :].rearrange("p (c h) k -> p c h k", c=4)
                if bias is not None:
                    dve.wait_ge(bias_in[t % 3], 16 * (t // 3 + 1))
                    ins = dve.tensor_tensor(si, raw, bt[:, t % 3, :, :].rearrange("p (c h) k -> p c h k", c=4), ALU.add)
                else:
                    ins = dve.tensor_tensor(si, raw, bt[:, t, :].unsqueeze(1).unsqueeze(1).broadcast_to([P, 4, 4, KEYS]), ALU.min)
                ins.then_inc(s_sb, 1)
                dve.wait_ge(s_sb, t + 1)
                link(dve.tensor_reduce(mx[:, i, :], s[:, i, :, :], AX, ALU.max))
                dve.tensor_tensor(s[:, i, :, :], s[:, i, :, :], mx[:, i, :].unsqueeze(2).broadcast_to([P, HEADS, KEYS]),
                                  ALU.subtract).then_inc(s_ready, 1)

            def outputs(t):
                i = t % 2
                dve.wait_ge(o_mm, t + 1)
                o = ps[:, 6, 0:HEADS * (DK + 1)].rearrange("p (h d) -> p h d", d=DK + 1)
                link(dve.reciprocal(rs[:, i, :], o[:, :, DK]))
                if t >= 2:
                    dve.wait_ge(oT_mm, t - 1)
                dve.tensor_tensor(on[:, i, :].rearrange("p (h d) -> p h d", d=DK), o[:, :, 0:DK],
                                  rs[:, i, :].unsqueeze(2).broadcast_to([P, HEADS, DK]), ALU.mult).then_inc(o_sb, 1)
                dve.wait_ge(y_mm, t + 1)
                dve.tensor_tensor(out[:, t, :], out[:, t, :], ps[:, 7, 0:D], ALU.add).then_inc(y_sb, 1)

            for t in range(NT):
                scores(t)
                if t:
                    outputs(t - 1)
            outputs(NT - 1)

        @block.scalar
        def _(act):
            act.wait_ge(loaded, 16 * loads)
            for n in range(KD * NCH):
                act.wait_ge(q_mm, n + 1)
                out_, in_ = qT[:, n // NCH, (n % NCH) * CH:(n % NCH + 1) * CH], ps[:, 4 + n % 4, :]
                if bq is not None:
                    act.activation(out_, in_, ACT.Identity, bias=bqT[:, n // NCH:n // NCH + 1]).then_inc(q_sb, 1)
                else:
                    act.copy(out_, in_).then_inc(q_sb, 1)
            for t in range(NT):
                i = t % 2
                act.wait_ge(s_ready, t + 1)
                act.activation(s[:, i, :, :], s[:, i, :, :], ACT.Exp).then_inc(exp_done, 1)
                if t >= 2:
                    act.wait_ge(o_mm, t - 1)
                for q in range(4):
                    act.wait_ge(pT_mm, 4 * t + q + 1)
                    act.copy(pT[:, i, 4 * q:4 * q + 4, :], ps[0:KEYS, 4 + q % 2, :].rearrange("p (h n) -> p h n", n=P)).then_inc(pT_sb, 1)
                act.wait_ge(oT_mm, t + 1)
                act.copy(oT[:, i, :, :], ps[:, 7, D:2 * D].rearrange("p (k n) -> p k n", n=P)).then_inc(oT_sb, 1)

        @block.tensor
        def _(pe):
            pe.wait_ge(loaded, 16 * loads)
            for k2 in range(KD):
                for k in range(KD):
                    mm = pe.matmul(ps[:, k2, 0:W], w["wk"][:, k, k2 * P:(k2 + 1) * P], core.ctxT[:, k, :], start=(k == 0), stop=(k == KD - 1))
            mm.then_inc(kv_mm, 1)
            for b in range(BATCH):
                for k in range(KD):
                    mm = pe.matmul(ps[0:KEYS, 2 + b, 0:D], core.ctxT[:, k, b * KEYS:(b + 1) * KEYS], w["wv"][:, k, :], start=(k == 0), stop=(k == KD - 1))
            mm.then_inc(kv_mm, 1)
            for n in range(KD * NCH):
                k2, c = n // NCH, n % NCH
                if n >= 4:
                    pe.wait_ge(q_sb, n - 3)
                for k in range(KD):
                    mm = pe.matmul(ps[:, 4 + n % 4, :], w["wq"][:, k, k2 * P:(k2 + 1) * P], core.xnT[:, k, c * CH:(c + 1) * CH],
                                   start=(k == 0), stop=(k == KD - 1))
                mm.then_inc(q_mm, 1)
            pe.wait_ge(q_sb, KD * NCH)
            pe.wait_ge(kbd_done, BATCH * HEADS)
            pe.wait_ge(v_sb, BATCH)
            pe.wait_ge(ones_done, 1)

            def scores(t):
                if t:
                    pe.wait_ge(s_sb, t)
                for c in range(4):
                    mm = pe.matmul(ps[:, c, 0:HW], qT[:, c // 2, t * P:(t + 1) * P],
                                   kbd[:, t // 8, c // 2, 4 * (c % 2):4 * (c % 2) + 4, :], start=True, stop=True)
                mm.then_inc(s_mm, 1)

            scores(0)
            for t in range(NT):
                i = t % 2
                pe.wait_ge(exp_done, t + 1)
                for q in range(4):
                    if 4 * t + q >= 2:
                        pe.wait_ge(pT_sb, 4 * t + q - 1)
                    for j in range(4):
                        mm = pe.transpose(ps[0:KEYS, 4 + q % 2, j * P:(j + 1) * P], s[:, i, 4 * q + j, :], core.ident[:])
                    mm.then_inc(pT_mm, 1)
                if t + 1 < NT:
                    scores(t + 1)
                pe.wait_ge(pT_sb, 4 * t + 4)
                if t:
                    pe.wait_ge(o_sb, t)
                for h in range(HEADS):
                    mm = pe.matmul(ps[:, 6, h * (DK + 1):(h + 1) * (DK + 1)], pT[:, i, h, :], vh[:, t // 8, h, :], start=True, stop=True)
                mm.then_inc(o_mm, 1)
                pe.wait_ge(o_sb, t + 1)
                if t:
                    pe.wait_ge(y_sb, t)
                for k in range(KD):
                    mm = pe.transpose(ps[:, 7, D + k * P:D + (k + 1) * P], on[:, i, k * P:(k + 1) * P], core.ident[:])
                mm.then_inc(oT_mm, 1)
                pe.wait_ge(oT_sb, t + 1)
                for k in range(KD):
                    mm = pe.matmul(ps[:, 7, 0:D], oT[:, i, k, :], w["wo"][:, k, :], start=(k == 0), stop=(k == KD - 1))
                mm.then_inc(y_mm, 1)


def plain_cross_attention(core):
    nc, dram, ps = core.nc, core.dram, core.ps
    with ExitStack() as ctx:
        sb = lambda n, shape, dt=F32: ctx.enter_context(nc.sbuf_tensor(f"a2_{n}", shape, dt))
        sem = lambda n: core.semaphore(ctx, f"a2_{n}")
        ctx_sb = sb("ctx", [KEYS, BATCH, D])
        mi, mf = sb("mi", [P, BATCH, KEYS], I32), sb("mf", [P, BATCH, KEYS])
        s, p = sb("s", [P, NT, KEYS]), sb("p", [P, NT, KEYS])
        mx, sums, rs = sb("mx", [P, NT]), sb("sums", [P, NT]), sb("rs", [P, NT])
        pT = sb("pT", [KEYS, NT, P])
        loaded, s_mm, chain, s_ready, exp_done, rs_done, pT_mm, pT_sb, y_mm, y_sb = (
            sem(x) for x in ("loaded", "s_mm", "chain", "s_ready", "exp", "rs", "pT_mm", "pT_sb", "y_mm", "y_sb"))
        block = core.stage(ctx)
        PER = 4

        @block.sync
        def _(sp):
            sp.dma_start(ctx_sb[:], dram["ctx"].rearrange("b k d -> k b d")).then_inc(loaded, 16)
            sp.dma_start(mi[:], bcast(dram["mask_ik"], P)).then_inc(loaded, 16)
            sp.wait_ge(loaded, 32)

        @block.tensor
        def _(pe):
            for t in range(NT):
                for k in range(KD):
                    mm = pe.matmul(ps[:, t // PER, (t % PER) * KEYS:(t % PER + 1) * KEYS], core.xnT[:, k, t * P:(t + 1) * P],
                                   core.ctxT[:, k, (t // 8) * KEYS:(t // 8 + 1) * KEYS], start=(k == 0), stop=(k == KD - 1))
                if t % PER == PER - 1:
                    mm.then_inc(s_mm, 1)
            pe.wait_ge(loaded, 32)
            pe.wait_ge(exp_done, NT)
            for g in range(NT // 4):
                for j in range(4):
                    mm = pe.transpose(ps[0:KEYS, 4 + g, j * P:(j + 1) * P], p[:, 4 * g + j, :], core.ident[:])
                mm.then_inc(pT_mm, 1)
            for t in range(NT):
                pe.wait_ge(pT_sb, t // 4 + 1)
                if t >= 4:
                    pe.wait_ge(y_sb, t - 3)
                pe.matmul(ps[:, t % 4, 0:D], pT[:, t, :], ctx_sb[:, t // 8, :], start=True, stop=True).then_inc(y_mm, 1)

        @block.scalar
        def _(act):
            for t in range(NT):
                act.wait_ge(s_ready, t // 8 + 1)
                act.activation(p[:, t, :], s[:, t, :], ACT.Exp, accum_out=sums[:, t:t + 1]).then_inc(exp_done, 1)
            for g in range(NT // 4):
                act.wait_ge(pT_mm, g + 1)
                act.copy(pT[:, 4 * g:4 * g + 4, :], ps[0:KEYS, 4 + g, :].rearrange("p (t n) -> p t n", n=P)).then_inc(pT_sb, 1)

        @block.vector
        def _(dve):
            count = [0]

            def link(ins):
                count[0] += 1
                ins.then_inc(chain, 1)
                dve.wait_ge(chain, count[0])

            dve.wait_ge(loaded, 32)
            link(dve.tensor_scalar(mf[:], mi[:], NEG, None, ALU.mult))
            for b in range(BATCH):
                dve.wait_ge(s_mm, 2 * b + 2)
                sb_ = s[:, 8 * b:8 * b + 8, :]
                for c in range(2):
                    link(dve.scalar_tensor_tensor(s[:, 8 * b + 4 * c:8 * b + 4 * c + 4, :],
                                                  ps[:, 2 * b + c, 0:PER * KEYS].rearrange("p (t k) -> p t k", k=KEYS),
                                                  D ** -0.5, mf[:, b, :].unsqueeze(1).broadcast_to([P, 4, KEYS]), ALU.mult, ALU.add))
                link(dve.tensor_reduce(mx[:, 8 * b:8 * b + 8], sb_, AX, ALU.max))
                dve.tensor_tensor(sb_, sb_, mx[:, 8 * b:8 * b + 8].unsqueeze(2).broadcast_to([P, 8, KEYS]), ALU.subtract).then_inc(s_ready, 1)
            dve.wait_ge(exp_done, NT)
            link(dve.reciprocal(rs[:], sums[:]))
            for t in range(NT):
                dve.wait_ge(y_mm, t + 1)
                dve.scalar_tensor_tensor(core.x[:, t, :], ps[:, t % 4, 0:D], rs[:, t:t + 1], core.x[:, t, :],
                                         ALU.mult, ALU.add).then_inc(y_sb, 1)


def expert_weights(core, name, kind, wg, bg, ew, b2, acc):
    nc, dram, ps = core.nc, core.dram, core.ps
    with ExitStack() as ctx:
        sb = lambda n, shape, dt=F32: ctx.enter_context(nc.sbuf_tensor(f"{name}_{n}", shape, dt))
        sem = lambda n: core.semaphore(ctx, f"{name}_{n}")
        wg_sb, bg_sb, b2_sb = sb("wg", [P, KD, EXPERTS]), sb("bg", [P, EXPERTS]), sb("b2", [EXPERTS, D])
        rank = sb("rank", [P, EXPERTS])
        lg, t1, t2 = (sb(n, [P, NT, EXPERTS]) for n in ("lg", "t1", "t2"))
        m1, m2, r1, e2 = (sb(n, [P, NT]) for n in ("m1", "m2", "r1", "e2"))
        w8, ewT = sb("w8", [P, NT, EXPERTS]), sb("ewT", [EXPERTS, NT, P])
        loaded, g_mm, chain, act_in, act_out, w_done, wT_mm, wT_sb, y_mm, y_sb = (
            sem(x) for x in ("loaded", "g_mm", "chain", "act_in", "act_out", "w", "wT_mm", "wT_sb", "y_mm", "y_sb"))
        loads = 3 + (b2 is not None)
        block = core.stage(ctx)
        per_token = lambda v: v[:].unsqueeze(2).broadcast_to([P, NT, EXPERTS])
        per_expert = lambda v: v[:].unsqueeze(1).broadcast_to([P, NT, EXPERTS])

        @block.sync
        def _(sp):
            sp.dma_start(wg_sb[:], wg.rearrange("(k p) e -> p k e", p=P)).then_inc(loaded, 16)
            sp.dma_start(bg_sb[:], bcast(bg, P)).then_inc(loaded, 16)
            sp.dma_start(rank[:], bcast(dram["rank"], P)).then_inc(loaded, 16)
            if b2 is not None:
                sp.dma_start(b2_sb[:], b2).then_inc(loaded, 16)
            sp.wait_ge(loaded, 16 * loads)

        @block.tensor
        def _(pe):
            pe.wait_ge(loaded, 16 * loads)
            for t in range(NT):
                for k in range(KD):
                    mm = pe.matmul(ps[:, 0, t * EXPERTS:(t + 1) * EXPERTS], core.xnT[:, k, t * P:(t + 1) * P], wg_sb[:, k, :],
                                   start=(k == 0), stop=(k == KD - 1))
            mm.then_inc(g_mm, 1)
            if b2 is not None:
                pe.wait_ge(w_done, 2)
                for g in range(NT // 4):
                    for j in range(4):
                        mm = pe.transpose(ps[0:EXPERTS, 1 + g, j * P:(j + 1) * P], w8[:, 4 * g + j, :], core.ident[:])
                mm.then_inc(wT_mm, 1)
                pe.wait_ge(wT_sb, 1)
                for t in range(NT):
                    if t >= 2:
                        pe.wait_ge(y_sb, t - 1)
                    pe.matmul(ps[:, 6 + t % 2, 0:D], ewT[:, t, :], b2_sb[:], start=True, stop=True).then_inc(y_mm, 1)

        @block.scalar
        def _(act):
            act.wait_ge(act_in, 1)
            if kind == "top2":
                act.activation(e2[:], m2[:], ACT.Exp).then_inc(act_out, 1)
            else:
                act.activation(t1[:], lg[:], ACT.Sigmoid).then_inc(act_out, 1)

        @block.vector
        def _(dve):
            count = [0]

            def link(ins):
                count[0] += 1
                ins.then_inc(chain, 1)
                dve.wait_ge(chain, count[0])

            def first_best(values, best, onehot):
                link(dve.tensor_reduce(best[:], values[:], AX, ALU.max))
                link(dve.tensor_tensor(onehot[:], values[:], per_token(best), ALU.is_equal))
                link(dve.tensor_tensor(onehot[:], onehot[:], per_expert(rank), ALU.mult))
                link(dve.tensor_reduce(r1[:], onehot[:], AX, ALU.max))
                link(dve.tensor_tensor(onehot[:], onehot[:], per_token(r1), ALU.is_equal))

            dve.wait_ge(loaded, 16 * loads)
            dve.wait_ge(g_mm, 1)
            logits = ps[:, 0, 0:NT * EXPERTS].rearrange("p (t e) -> p t e", e=EXPERTS)
            link(dve.tensor_tensor(lg[:], logits, per_expert(bg_sb), ALU.add))
            if kind == "top2":
                first_best(lg, m1, t1)
                link(dve.scalar_tensor_tensor(lg[:], t1[:], -3e38, lg[:], ALU.mult, ALU.add))
                first_best(lg, m2, t2)
                dve.tensor_tensor(m2[:], m2[:], m1[:], ALU.subtract).then_inc(act_in, 1)
                dve.wait_ge(act_out, 1)
                link(dve.tensor_scalar(m1[:], e2[:], 1.0, None, ALU.add))
                link(dve.reciprocal(m1[:], m1[:]))
                link(dve.tensor_tensor(m2[:], e2[:], m1[:], ALU.mult))
                link(dve.tensor_tensor(t1[:], t1[:], per_token(m1), ALU.mult))
                link(dve.tensor_tensor(t2[:], t2[:], per_token(m2), ALU.mult))
                dve.tensor_tensor(w8[:], t1[:], t2[:], ALU.add).then_inc(w_done, 1)
            elif kind == "threshold":
                dve.sem_inc(act_in, 1)
                dve.wait_ge(act_out, 1)
                dve.scalar_tensor_tensor(w8[:], t1[:], 0.5, t1[:], ALU.is_gt, ALU.mult).then_inc(w_done, 1)
            else:
                dve.sem_inc(act_in, 1)
                dve.wait_ge(act_out, 1)
                first_best(t1, m1, t2)
                dve.tensor_tensor(w8[:], t2[:], per_token(m1), ALU.mult).then_inc(w_done, 1)
            dve.wait_ge(w_done, 1)
            dve.tensor_copy(ew[:].rearrange("p e t -> p t e"), w8[:]).then_inc(w_done, 1)
            if b2 is not None:
                dve.wait_ge(wT_mm, 1)
                dve.tensor_copy(ewT[:].rearrange("e (g t) p -> e g (t p)", g=4), ps[0:EXPERTS, 1:5, :]).then_inc(wT_sb, 1)
                for t in range(NT):
                    dve.wait_ge(y_mm, t + 1)
                    dve.tensor_tensor(acc[:, t, :], acc[:, t, :], ps[:, 6 + t % 2, 0:D], ALU.add).then_inc(y_sb, 1)


def feed_forward(core, name, experts, w1, b1, w2, func, acc, ew=None):
    nc, dram, ps = core.nc, core.dram, core.ps
    with ExitStack() as ctx:
        sb = lambda n, shape, dt=F32: ctx.enter_context(nc.sbuf_tensor(f"{name}_{n}", shape, dt))
        sem = lambda n: core.semaphore(ctx, f"{name}_{n}")
        B = min(2, experts)
        w1_sb = [sb(f"w1_{u}", [P, KD, FF]) for u in range(B)]
        w2_sb = [sb(f"w2_{u}", [P, FB, D]) for u in range(B)]
        b1_sb = [sb(f"b1_{u}", [P, FB]) for u in range(B)]
        hid = sb("hid", [P, FB, CH])
        w_in = [sem(f"w_in{u}") for u in range(B)]
        w_free, h_mm, h_sb, y_mm, y_sb = sem("w_free"), sem("h_mm"), sem("h_sb"), sem("y_mm"), sem("y_sb")
        HB, YB = 4, 4
        LOADS = 48 if b1 is not None else 32
        block = core.stage(ctx)

        @block.sync
        def _(sp):
            with sp.Fori(0, experts // B) as i:
                for u in range(B):
                    e = i * B + u
                    sp.wait_ge(w_free, e + 1)
                    sp.dma_start(w1_sb[u][:], w1[bass.ds(e, 1)].rearrange("e (k p) f -> p (e k) f", p=P)).then_inc(w_in[u], 16)
                    sp.dma_start(w2_sb[u][:], w2[bass.ds(e, 1)].rearrange("e (f p) d -> p (e f) d", p=P)).then_inc(w_in[u], 16)
                    if b1 is not None:
                        sp.dma_start(b1_sb[u][:], b1[:, bass.ds(e, 1), :].rearrange("p e f -> p (e f)")).then_inc(w_in[u], 16)

        @block.tensor
        def _(pe):
            pe.sem_inc(w_free, B)
            with pe.Fori(0, experts // B) as i:
                for u in range(B):
                    e = i * B + u
                    pe.wait_ge(w_in[u], LOADS * i + LOADS)
                    for c in range(NCH):
                        for f in range(FB):
                            pe.wait_ge(h_sb, e * (NCH * FB) + (c * FB + f + 1))
                            for k in range(KD):
                                mm = pe.matmul(ps[:, f % HB, :], w1_sb[u][:, k, f * P:(f + 1) * P],
                                               core.xnT[:, k, c * CH:(c + 1) * CH], start=(k == 0), stop=(k == KD - 1))
                            mm.then_inc(h_mm, 1)
                        pe.wait_ge(h_sb, e * (NCH * FB) + (c * FB + FB + HB))
                        for t in range(4):
                            pe.wait_ge(y_sb, e * NT + (4 * c + t + 1))
                            for f in range(FB):
                                mm = pe.matmul(ps[:, HB + t, 0:D], hid[:, f, t * P:(t + 1) * P], w2_sb[u][:, f, :],
                                               start=(f == 0), stop=(f == FB - 1))
                            mm.then_inc(y_mm, 1)
                    pe.wait_ge(y_mm, e * NT + NT)
                    pe.sem_inc(w_free, 1)

        @block.scalar
        def _(act):
            act.sem_inc(h_sb, HB)
            with act.Fori(0, experts // B) as i:
                for u in range(B):
                    e = i * B + u
                    act.wait_ge(w_in[u], LOADS * i + LOADS)
                    for c in range(NCH):
                        for f in range(FB):
                            act.wait_ge(h_mm, e * (NCH * FB) + (c * FB + f + 1))
                            bias = b1_sb[u][:, f:f + 1] if b1 is not None else 0.0
                            act.activation(hid[:, f, :], ps[:, f % HB, :], func, bias=bias).then_inc(h_sb, 1)

        @block.vector
        def _(dve):
            dve.sem_inc(y_sb, YB)
            with dve.Fori(0, experts // B) as i:
                for u in range(B):
                    e = i * B + u
                    for t in range(NT):
                        dve.wait_ge(y_mm, e * NT + (t + 1))
                        y = ps[:, HB + t % 4, 0:D]
                        if ew is not None:
                            ins = dve.scalar_tensor_tensor(acc[:, t, :], y, ew[:, bass.ds(e, 1), t], acc[:, t, :], ALU.mult, ALU.add)
                        else:
                            ins = dve.tensor_tensor(acc[:, t, :], acc[:, t, :], y, ALU.add)
                        ins.then_inc(y_sb, 1)


PARTS = 3
PROD = ((0, 0), (0, 1), (1, 0), (1, 1), (0, 2), (2, 0))
SR = len(PROD) * DK


def self_attention(core, acc):
    nc, dram, ps = core.nc, core.dram, core.ps
    KT = SEQ // P
    NP = BATCH * HEADS // 2
    with ExitStack() as ctx:
        sb = lambda n, shape, dt=F32: ctx.enter_context(nc.sbuf_tensor(f"sa_{n}", shape, dt))
        sem = lambda n: core.semaphore(ctx, f"sa_{n}")
        parts = dram["scratch_parts"]
        maxima = dram["scratch_max"]
        vh = sb("vh", [P, NT, HEADS, DK + 1])
        on = sb("on", [P, NT, D])

        with ExitStack() as c2:
            sb2 = lambda n, shape, dt=F32: c2.enter_context(nc.sbuf_tensor(f"sp_{n}", shape, dt))
            sem2 = lambda n: core.semaphore(c2, f"sp_{n}")
            wqkv = sb2("wqkv", [P, KD, 3 * D])
            bqk, bv = sb2("bqk", [P, 4]), sb2("bv", [P, D])
            q32 = sb2("q32", [P, 2, CH])
            r32 = sb2("r32", [P, 2, CH])
            part = [sb2(f"part{i}", [P, 2, CH], BF16) for i in range(PARTS)]
            loaded, mm_done, q_sb, chain, split, stored, v_mm, v_sb, ones = (
                sem2("loaded"), sem2("mm"), sem2("q_sb"), sem2("chain"), sem2("split"), [sem2("stored0"), sem2("stored1")], sem2("v_mm"), sem2("v_sb"), sem2("ones"))
            NQ = 4 * NCH
            block = core.stage(c2)

            @block.sync
            def _(sp):
                sp.dma_start(wqkv[:], dram["L1f_wqkv"].rearrange("(k p) d -> p k d", p=P)).then_inc(loaded, 16)
                sp.dma_start(bqk[:], dram["L1f_bqk"]).then_inc(loaded, 16)
                sp.dma_start(bv[:], bcast(dram["L1f_bv"], P)).then_inc(loaded, 16)
                for n in range(NQ):
                    j, c = n // NCH, n % NCH
                    sp.wait_ge(split, n + 1)
                    for i in range(PARTS):
                        sp.dma_start(parts[j // 2, i, (j % 2) * P:(j % 2 + 1) * P, c * CH:(c + 1) * CH], part[i][:, n % 2, :]).then_inc(stored[n % 2], 16)
                sp.wait_ge(loaded, 48)
                for u in range(2):
                    sp.wait_ge(stored[u], NQ // 2 * 48)

            @block.tensor
            def _(pe):
                pe.wait_ge(loaded, 48)
                for n in range(NQ):
                    j, c = n // NCH, n % NCH
                    if n >= 4:
                        pe.wait_ge(q_sb, n - 3)
                    for k in range(KD):
                        mm = pe.matmul(ps[:, n % 4, :], wqkv[:, k, j * P:(j + 1) * P], core.xnT[:, k, c * CH:(c + 1) * CH],
                                       start=(k == 0), stop=(k == KD - 1))
                    mm.then_inc(mm_done, 1)
                for t in range(NT):
                    if t >= 4:
                        pe.wait_ge(v_sb, t - 3)
                    for k in range(KD):
                        mm = pe.matmul(ps[:, 4 + t % 4, 0:D], core.xnT[:, k, t * P:(t + 1) * P], wqkv[:, k, 2 * D:3 * D],
                                       start=(k == 0), stop=(k == KD - 1))
                    mm.then_inc(v_mm, 1)

            @block.gpsimd
            def _(pool):
                pool.memset(vh[:, :, :, DK:DK + 1], 1.0).then_inc(ones, 1)

            @block.scalar
            def _(act):
                act.wait_ge(loaded, 48)
                for n in range(NQ):
                    j = n // NCH
                    act.wait_ge(mm_done, n + 1)
                    if n >= 2:
                        act.wait_ge(split, n - 1)
                    act.activation(q32[:, n % 2, :], ps[:, n % 4, :], ACT.Identity, bias=bqk[:, j:j + 1]).then_inc(q_sb, 1)

            @block.vector
            def _(dve):
                count = [0]

                def link(ins):
                    count[0] += 1
                    ins.then_inc(chain, 1)
                    dve.wait_ge(chain, count[0])

                for n in range(NQ):
                    u = n % 2
                    dve.wait_ge(q_sb, n + 1)
                    if n >= 2:
                        dve.wait_ge(stored[u], 48 * (n // 2))
                    link(dve.tensor_copy(part[0][:, u, :], q32[:, u, :]))
                    link(dve.tensor_tensor(r32[:, u, :], q32[:, u, :], part[0][:, u, :], ALU.subtract))
                    link(dve.tensor_copy(part[1][:, u, :], r32[:, u, :]))
                    dve.tensor_tensor(part[2][:, u, :], r32[:, u, :], part[1][:, u, :], ALU.subtract).then_inc(split, 1)
                dve.wait_ge(loaded, 48)
                for t in range(NT):
                    dve.wait_ge(v_mm, t + 1)
                    dve.tensor_tensor(vh[:, t, :, 0:DK], ps[:, 4 + t % 4, 0:D].rearrange("p (h d) -> p h d", d=DK),
                                      bv[:].rearrange("p (h d) -> p h d", d=DK), ALU.add).then_inc(v_sb, 1)

        with ExitStack() as c3:
            sb3 = lambda n, shape, dt=F32: c3.enter_context(nc.sbuf_tensor(f"sh_{n}", shape, dt))
            sem3 = lambda n: core.semaphore(c3, f"sh_{n}")
            qs = [sb3(f"qs{u}", [SR + PARTS, 2, SEQ], BF16) for u in range(2)]
            ks = [sb3(f"ks{u}", [SR + PARTS, 2, SEQ], BF16) for u in range(2)]
            mhalf, m32 = sb3("mhalf", [P, 2, 2 * KT]), sb3("m32", [P, 2 * KT])
            mpart = [sb3(f"mpart{i}", [P, 2 * KT]) for i in range(PARTS)]
            mbf = [sb3(f"mbf{i}", [P, 2 * KT], BF16) for i in range(2)]
            mT = sb3("mT", [2 * KT, PARTS, P], BF16)
            pT = sb3("pT", [P, 4, 2, CH])
            oT_sb_, rs = sb3("oT", [P, CH]), sb3("rs", [P, 4, 4])
            stack_in = [sem3("stack_in0"), sem3("stack_in1")]
            max_in, max_out, ones_in = [sem3("max_in0"), sem3("max_in1")], sem3("max_out"), sem3("ones_in")
            a_mm, a_max, chain, m_split, mT_mm, mT_sb, b_mm, exp_done, pv_mm, oT_done, on_mm, on_done, stack_free = (
                sem3(x) for x in ("a_mm", "a_max", "chain", "m_split", "mT_mm", "mT_sb", "b_mm", "exp", "pv_mm", "oT", "on_mm", "on", "stack_free"))
            block = core.stage(c3)
            A_BANK, B_BANK, O_BANK, T_BANK = 0, 2, 6, 7
            NA = 2 * KT * 2

            @block.sync
            def _(sp):
                def load_stack(s, u):
                    b, hp = s // (HEADS // 2), s % (HEADS // 2)
                    rows = lambda w_, i: parts[w_, i, hp * 2 * DK:(hp + 1) * 2 * DK, b * SEQ:(b + 1) * SEQ].rearrange("(h p) n -> p h n", p=DK)
                    if s >= 2:
                        sp.wait_ge(stack_free, s - 1)
                    for j, (i, k) in enumerate(PROD):
                        sp.dma_start(qs[u][j * DK:(j + 1) * DK, :, :], rows(0, i)).then_inc(stack_in[u], 16)
                        sp.dma_start(ks[u][j * DK:(j + 1) * DK, :, :], rows(1, k)).then_inc(stack_in[u], 16)

                load_stack(0, 0)
                for s in range(NP):
                    u = s % 2
                    if s + 1 < NP:
                        load_stack(s + 1, 1 - u)
                    sp.wait_ge(mT_sb, s + 1)
                    sp.dma_start(maxima[:, s].rearrange("i h (t n) -> (h t) i n", n=P), mT[:]).then_inc(max_out, 16)
                    sp.wait_ge(max_out, 16 * (s + 1))
                    sp.dma_start(qs[u][SR:SR + PARTS, :, :], maxima[:, s]).then_inc(max_in[u], 16)

            @block.gpsimd
            def _(pool):
                for u in range(2):
                    pool.memset(ks[u][SR:SR + PARTS, :, :], 1.0).then_inc(ones_in, 1)

            def first_pass(pe, s, c):
                u, h, t, half = s % 2, c // (2 * KT), c // 2 % KT, c % 2
                n = s * NA + c
                if n >= 2:
                    pe.wait_ge(a_max, n - 1)
                pe.matmul(ps[:, A_BANK + n % 2, :], qs[u][0:SR, h, t * P:(t + 1) * P], ks[u][0:SR, h, half * CH:(half + 1) * CH],
                          start=True, stop=True).then_inc(a_mm, 1)

            @block.tensor
            def _(pe):
                pe.wait_ge(ones_in, 2)
                pe.wait_ge(stack_in[0], 16 * 2 * len(PROD))
                for c in range(NA):
                    first_pass(pe, 0, c)
                for s in range(NP):
                    u = s % 2
                    pe.wait_ge(m_split, s + 1)
                    if s:
                        pe.wait_ge(on_done, s)
                    for i in range(PARTS):
                        mm = pe.transpose(ps[0:2 * KT, T_BANK, i * P:(i + 1) * P], mpart[i][:], core.ident[:])
                    mm.then_inc(mT_mm, 1)
                    pe.wait_ge(max_in[u], 16 * (s // 2 + 1))
                    if s + 1 < NP:
                        pe.wait_ge(stack_in[1 - u], 16 * 2 * len(PROD) * ((s + 1) // 2 + 1))

                    def weighted(k):
                        pe.wait_ge(exp_done, s * 2 * KT + 2 * k + 2)
                        if k == 0 and s:
                            pe.wait_ge(oT_done, s)
                        b = s // (HEADS // 2)
                        for h in range(2):
                            head = 2 * (s % (HEADS // 2)) + h
                            for half in range(2):
                                g = 2 * h + half
                                mm = pe.matmul(ps[32 * g:32 * g + DK + 1, O_BANK, :], vh[:, b * KT + k, head, :],
                                               pT[:, (2 * k + h) % 4, half, :], start=(k == 0), stop=(k == KT - 1))
                        mm.then_inc(pv_mm, 1)

                    for k in range(KT):
                        for h in range(2):
                            n = s * 2 * KT + 2 * k + h
                            if n >= 2:
                                pe.wait_ge(exp_done, n - 1)
                            for half in range(2):
                                mm = pe.matmul(ps[:, B_BANK + 2 * (n % 2) + half, :], ks[u][:, h, k * P:(k + 1) * P],
                                               qs[u][:, h, half * CH:(half + 1) * CH], start=True, stop=True)
                            mm.then_inc(b_mm, 1)
                            if s + 1 < NP:
                                for c in range(2):
                                    first_pass(pe, s + 1, (2 * k + h) * 2 + c)
                        if k:
                            weighted(k - 1)
                    weighted(KT - 1)
                    pe.wait_ge(pv_mm, (s + 1) * KT)
                    pe.sem_inc(stack_free, 1)
                    pe.wait_ge(oT_done, s + 1)
                    for j in range(4):
                        mm = pe.transpose(ps[:, T_BANK, j * P:(j + 1) * P], oT_sb_[:, j * P:(j + 1) * P], core.ident[:])
                    mm.then_inc(on_mm, 1)

            @block.scalar
            def _(act):
                for s in range(NP):
                    for n in range(s * 2 * KT, (s + 1) * 2 * KT):
                        act.wait_ge(b_mm, n + 1)
                        if n >= 4:
                            act.wait_ge(pv_mm, n // 2 - 1)
                        act.activation(pT[:, n % 4, :, :], ps[:, B_BANK + 2 * (n % 2):B_BANK + 2 * (n % 2) + 2, :], ACT.Exp,
                                       scale=DK ** -0.5).then_inc(exp_done, 1)
                    act.wait_ge(pv_mm, (s + 1) * KT)
                    act.copy(oT_sb_[:], ps[:, O_BANK, :]).then_inc(oT_done, 1)

            @block.vector
            def _(dve):
                count = [0]

                def link(ins):
                    count[0] += 1
                    ins.then_inc(chain, 1)
                    dve.wait_ge(chain, count[0])

                def maxima_of(s):
                    for c in range(NA):
                        n = s * NA + c
                        h, t, half = c // (2 * KT), c // 2 % KT, c % 2
                        dve.wait_ge(a_mm, n + 1)
                        dve.tensor_reduce(mhalf[:, half, h * KT + t:h * KT + t + 1], ps[:, A_BANK + n % 2, :], AX, ALU.max).then_inc(a_max, 1)
                    dve.wait_ge(a_max, (s + 1) * NA)
                    link(dve.tensor_tensor(m32[:], mhalf[:, 0, :], mhalf[:, 1, :], ALU.max))
                    link(dve.tensor_scalar(m32[:], m32[:], -1.0, None, ALU.mult))
                    link(dve.tensor_copy(mbf[0][:], m32[:]))
                    link(dve.tensor_copy(mpart[0][:], mbf[0][:]))
                    link(dve.tensor_tensor(m32[:], m32[:], mpart[0][:], ALU.subtract))
                    link(dve.tensor_copy(mbf[1][:], m32[:]))
                    link(dve.tensor_copy(mpart[1][:], mbf[1][:]))
                    dve.tensor_tensor(mpart[2][:], m32[:], mpart[1][:], ALU.subtract).then_inc(m_split, 1)

                def maxima_rows(s):
                    dve.wait_ge(mT_mm, s + 1)
                    if s:
                        dve.wait_ge(max_out, 16 * s)
                    dve.tensor_copy(mT[:], ps[0:2 * KT, T_BANK, 0:PARTS * P].rearrange("p (i n) -> p i n", n=P)).then_inc(mT_sb, 1)

                def finish(s):
                    b, hp = s // (HEADS // 2), s % (HEADS // 2)
                    dve.wait_ge(on_mm, s + 1)
                    o = ps[:, T_BANK, :].rearrange("p (j g d) -> p j g d", g=4, d=32)
                    link(dve.reciprocal(rs[:], o[:, :, :, DK]))
                    for h in range(2):
                        dst = on[:, b * KT:(b + 1) * KT, (2 * hp + h) * DK:(2 * hp + h + 1) * DK].rearrange("p (g j) d -> p j g d", g=2)
                        ins = dve.tensor_tensor(dst, o[:, :, 2 * h:2 * h + 2, 0:DK],
                                                rs[:, :, 2 * h:2 * h + 2].unsqueeze(3).broadcast_to([P, 4, 2, DK]), ALU.mult)
                    ins.then_inc(on_done, 1)

                maxima_of(0)
                maxima_rows(0)
                for s in range(NP):
                    if s + 1 < NP:
                        maxima_of(s + 1)
                    finish(s)
                    if s + 1 < NP:
                        maxima_rows(s + 1)
        transpose_tokens(core, "sat", on, core.xnT)
        token_projection(core, "sao", dram["L1f_wo"], dram["L1f_bo"], acc)


def token_projection(core, name, w, b, acc):
    nc, ps = core.nc, core.ps
    with ExitStack() as ctx:
        w_sb = ctx.enter_context(nc.sbuf_tensor(f"{name}_w", [P, KD, D], F32))
        b_sb = ctx.enter_context(nc.sbuf_tensor(f"{name}_b", [P, D], F32))
        loaded, bias_done, y_mm, y_sb = (core.semaphore(ctx, f"{name}_{n}") for n in ("loaded", "bias", "y_mm", "y_sb"))
        block = core.stage(ctx)

        @block.sync
        def _(sp):
            sp.dma_start(w_sb[:], w.rearrange("(k p) d -> p k d", p=P)).then_inc(loaded, 16)
            sp.dma_start(b_sb[:], bcast(b, P)).then_inc(loaded, 16)
            sp.wait_ge(loaded, 32)

        @block.tensor
        def _(pe):
            pe.wait_ge(loaded, 32)
            for t in range(NT):
                if t >= 4:
                    pe.wait_ge(y_sb, t - 3)
                for k in range(KD):
                    mm = pe.matmul(ps[:, t % 4, 0:D], core.xnT[:, k, t * P:(t + 1) * P], w_sb[:, k, :], start=(k == 0), stop=(k == KD - 1))
                mm.then_inc(y_mm, 1)

        @block.vector
        def _(dve):
            dve.wait_ge(loaded, 32)
            dve.tensor_tensor(acc[:], acc[:], b_sb[:].unsqueeze(1).broadcast_to([P, NT, D]), ALU.add).then_inc(bias_done, 1)
            dve.wait_ge(bias_done, 1)
            for t in range(NT):
                dve.wait_ge(y_mm, t + 1)
                dve.tensor_tensor(acc[:, t, :], acc[:, t, :], ps[:, t % 4, 0:D], ALU.add).then_inc(y_sb, 1)


def add_to(core, name, dst, src, row=None):
    nc = core.nc
    with ExitStack() as ctx:
        done = core.semaphore(ctx, f"{name}_done")
        if row is not None:
            row_sb = ctx.enter_context(nc.sbuf_tensor(f"{name}_row", [P, D], F32))
            src = row_sb[:].unsqueeze(1).broadcast_to([P, NT, D])
        loaded = core.semaphore(ctx, f"{name}_loaded")
        block = core.stage(ctx)

        @block.sync
        def _(sp):
            if row is not None:
                sp.dma_start(row_sb[:], bcast(row, P)).then_inc(loaded, 16)
                sp.wait_ge(loaded, 16)

        @block.vector
        def _(dve):
            if row is not None:
                dve.wait_ge(loaded, 16)
            dve.tensor_tensor(dst[:], dst[:], src if row is not None else src[:], ALU.add).then_inc(done, 1)


def store_output(core):
    nc = core.nc
    with ExitStack() as ctx:
        stored = core.semaphore(ctx, "out_stored")
        block = core.stage(ctx)

        @block.sync
        def _(sp):
            sp.dma_start(core.dram["out"].rearrange("b (t p) d -> p (b t) d", p=P), core.x[:]).then_inc(stored, 16)
            sp.wait_ge(stored, 16)


def program(nc, dram, stages=range(1, 9)):
    with ExitStack() as ctx:
        core = Core(nc, ctx, dram)
        x, xn, xnT = core.x, core.xn, core.xnT
        load_inputs(core)
        if 1 in stages:
            layer_norm(core, "n0", x, xn, xnT)
            query_softmax_attention(core)
        if 2 in stages:
            with nc.sbuf_tensor("xmax", [P, 1], F32) as xmax:
                layer_norm(core, "n1", x, xn, absmax=xmax)
                quantised_ffn(core, xmax)
        if 3 in stages:
            layer_norm(core, "n2", x, xn, xnT)
            headed_cross_attention(core, "a1", dram["L1_WqT"], dram["L1_WkT"], dram["L1_WvT"], dram["L1_WoT"], xn, bias=dram["bias"])
            with nc.sbuf_tensor("l1_h", [P, NT, D], F32) as h:
                layer_norm(core, "n3", xn, h, xnT, gainT=dram["L1_g1"], shiftT=dram["L1_be1"])
            add_to(core, "b2", xn, None, row=dram["L1_b2"])
            feed_forward(core, "f1", 1, dram["L1_W1T"], dram["L1_b1"], dram["L1_W2T"], ACT.Gelu, xn)
            layer_norm(core, "n4", xn, xn, gain=dram["L1_g2"], shift=dram["L1_be2"])
            add_to(core, "r1", x, xn)
        if 4 in stages:
            layer_norm(core, "n5", x, xn)
            with nc.sbuf_tensor("l1f_h", [P, NT, D], F32) as h:
                layer_norm(core, "n6", xn, h, xnT, gainT=dram["L1f_ln1_g"], shiftT=dram["L1f_ln1_b"])
            self_attention(core, xn)
            with nc.sbuf_tensor("l1f_h2", [P, NT, D], F32) as h:
                layer_norm(core, "n7", xn, h, xnT, gainT=dram["L1f_ln2_g"], shiftT=dram["L1f_ln2_b"])
            add_to(core, "r2", x, xn)
            with nc.sbuf_tensor("ew1", [P, EXPERTS, NT], F32) as ew:
                expert_weights(core, "g1", "top2", dram["L1f_gate_w"], dram["L1f_gate_b"], ew, dram["L1f_b2"], x)
                feed_forward(core, "m1", EXPERTS, dram["L1f_W1"], dram["L1f_b1"], dram["L1f_W2"], ACT.Relu, x, ew)
        if 5 in stages:
            layer_norm(core, "n8", x, xn, xnT)
            plain_cross_attention(core)
        if 6 in stages:
            layer_norm(core, "n9", x, xn, xnT)
            with nc.sbuf_tensor("ew2", [P, EXPERTS, NT], F32) as ew:
                expert_weights(core, "g2", "threshold", dram["L2_Wg"], dram["L2_bg"], ew, dram["L2_b2"], x)
                feed_forward(core, "m2", EXPERTS, dram["L2_W1"], dram["L2_b1"], dram["L2_W2"], ACT.Relu, x, ew)
        if 7 in stages:
            layer_norm(core, "n10", x, xn, xnT)
            add_to(core, "bo3", x, None, row=dram["L3_bo"])
            headed_cross_attention(core, "a3", dram["L3_wq"], dram["L3_wk"], dram["L3_wv"], dram["L3_wo"], x, mask=dram["mask_bf"],
                                   bq=dram["L3_bq"], bk=dram["L3_bk"], bv=dram["L3_bv"])
        if 8 in stages:
            layer_norm(core, "n11", x, xn, xnT)
            with nc.sbuf_tensor("ew3", [P, EXPERTS, NT], F32) as ew:
                expert_weights(core, "g3", "top1", dram["L3_Wr"], dram["L3_br"], ew, None, x)
                feed_forward(core, "m3", EXPERTS, dram["L3_W1"], None, dram["L3_W2"], ACT.Gelu, x, ew)
        store_output(core)



def laid_out(inputs):
    import numpy as np

    g = lambda n: np.asarray(inputs[n])
    t = lambda n: np.ascontiguousarray(np.swapaxes(np.asarray(inputs[n]), -1, -2))
    a = {}
    a["x"] = g("x")
    a["ctx"] = g("ctx_1024")
    a["ctxT"] = np.ascontiguousarray(g("ctx_1024").reshape(BATCH * KEYS, D).T)
    a["bias"] = np.ascontiguousarray(g("fside_Bx16xSxS2_0").reshape(BATCH, HEADS, SEQ // P, P, KEYS).transpose(0, 2, 3, 1, 4)
                                     .reshape(NT, P, HEADS, KEYS))
    a["mask_ik"] = g("mask_Bx1xS2_ik0").reshape(BATCH, KEYS)
    a["mask_bf"] = g("mask_Bx1xSxS2_bf0").reshape(TOK, KEYS)
    for n in ("Wk", "Wv", "Wo"):
        a[f"L0_{n}T"] = t(f"L0_xattn_{n}")
    a["L0_Wq"] = g("L0_xattn_Wq")
    for n in ("bq", "bk", "bv", "bo"):
        a[f"L0_{n}"] = g(f"L0_xattn_{n}")
    a["L0_WinT"], a["L0_Wout"] = t("L0_ffn_W_in"), g("L0_ffn_W_out")
    a["L0_bin"], a["L0_bout"] = g("L0_ffn_b_in"), g("L0_ffn_b_out")
    for n in ("Wq", "Wk", "Wv", "Wo"):
        a[f"L1_{n}T"] = t(f"L1_xattn_{n}")
    a["L1_W1T"], a["L1_W2T"] = t("L1_xattn_W1")[None], t("L1_xattn_W2")[None]
    a["L1_b1"] = g("L1_xattn_b1")[None]
    for n in ("b2", "g1", "be1", "g2", "be2"):
        a[f"L1_{n}"] = g(f"L1_xattn_{n}")
    for n in ("ln1_g", "ln1_b", "ln2_g", "ln2_b", "gate_w", "gate_b", "W1", "b1", "W2", "b2"):
        a[f"L1f_{n}"] = g(f"L1_ffn_{n}")
    a["L1f_wqkv"], a["L1f_bqkv"], a["L1f_wo"], a["L1f_bo"] = (g(f"L1_ffn_{n}") for n in ("w_qkv", "b_qkv", "w_o", "b_o"))
    for n in ("Wg", "bg", "W1", "b1", "W2", "b2"):
        a[f"L2_{n}"] = g(f"L2_ffn_{n}")
    for n in ("wq", "wk", "wv", "wo", "bq", "bk", "bv", "bo"):
        a[f"L3_{n}"] = g(f"L3_xattn_{n}")
    for n in ("Wr", "br", "W1", "W2"):
        a[f"L3_{n}"] = g(f"L3_ffn_{n}")
    a["L1f_bqk"], a["L1f_bv"] = a["L1f_bqkv"][:2 * D], a.pop("L1f_bqkv")[2 * D:]
    for n in ("L0_bq", "L0_bk", "L0_bv", "L0_bin", "L1_g1", "L1_be1", "L1f_ln1_g", "L1f_ln1_b", "L1f_ln2_g", "L1f_ln2_b",
              "L1f_bqk", "L3_bq", "L3_bk"):
        a[n] = a[n].reshape(-1, P).T
    for n in ("L1_b1", "L1f_b1", "L2_b1"):
        a[n] = a[n].reshape(-1, FB, P).transpose(2, 0, 1)
    return {k: np.ascontiguousarray(v) for k, v in a.items()}


def constants():
    import numpy as np
    return {
        "identity": np.eye(P, dtype=np.float32),
        "head_of": (np.arange(P)[:, None] // DK == np.arange(8)[None]).astype(np.float32),
        "rank": np.arange(EXPERTS, 0, -1).astype(np.float32),
    }


def scratch(nc, dram):
    dram["scratch_parts"] = nc.dram_tensor("scratch_parts", (2, PARTS, D, TOK), BF16).ap()
    dram["scratch_max"] = nc.dram_tensor("scratch_max", (PARTS, BATCH * HEADS // 2, 2, SEQ), BF16).ap()


def kernel(**inputs):
    import concourse.bacc as _bacc
    from concourse import mybir as _mybir
    from concourse.bass_utils import run_bass_kernel_spmd as _run

    nc = _bacc.Bacc("TRN2", target_bir_lowering=False, num_devices=1)
    arrays = {**laid_out(inputs), **constants()}
    dram = {n: nc.dram_tensor(n, a.shape, _mybir.dt.from_np(a.dtype), kind="ExternalInput").ap() for n, a in arrays.items()}
    dram["out"] = nc.dram_tensor("out", (BATCH, SEQ, D), F32, kind="ExternalOutput").ap()
    scratch(nc, dram)
    program(nc, dram)
    r = _run(nc, [arrays], core_ids=[0])
    return r.results[0]["out"]
```

```python
from contextlib import ExitStack

import concourse.bass as bass
from concourse import mybir

ALU = mybir.AluOpType
ACT = mybir.ActivationFunctionType
F32 = mybir.dt.float32
BF16 = mybir.dt.bfloat16
I32 = mybir.dt.int32
U8 = mybir.dt.uint8
AX = mybir.AxisListType.X

P = 128
BATCH, SEQ, D = 2, 1024, 256
TOK = BATCH * SEQ
NT = TOK // P
KD = D // P
KEYS = 77
HEADS, DK = 16, 16
FF = 1024
FB = FF // P
EXPERTS = 8
CH = 512
NCH = TOK // CH
EPS = 1e-5
NEG = -1e9
SEM_RANGES = (range(130, 175), range(175, 220))
LONG_SEMS = 220
ROUND = 12582912.0


class Core:

    def __init__(self, nc, ctx, dram):
        self.nc, self.dram = nc, dram
        sb = lambda name, shape, dt=F32: ctx.enter_context(nc.sbuf_tensor(name, shape, dt))
        self.x = sb("x_resid", [P, NT, D])
        self.xn = sb("x_norm", [P, NT, D])
        self.xnT = sb("x_normT", [P, KD, TOK])
        self.ctxT = sb("ctxT_sb", [P, KD, BATCH * KEYS])
        self.ident = sb("ident", [P, P])
        self.ident_bf = sb("ident_bf", [P, P], BF16)
        self.ps = ctx.enter_context(nc.psum_tensor("banks", [P, 8, CH], F32))
        self.side, self.taken, self.long = 0, 0, LONG_SEMS

    def lasting_semaphore(self, name):
        self.long += 1
        return self.nc.alloc_semaphore(name=name, num=self.long - 1)

    def semaphore(self, ctx, name):
        s = self.nc.alloc_semaphore(name=name, num=SEM_RANGES[self.side][self.taken])
        ctx.callback(self.nc.release_semaphore, s)
        self.taken += 1
        return s

    def stage(self, ctx):
        self.side, self.taken = 1 - self.side, 0
        self.nc.gpsimd.sem_clear(SEM_RANGES[self.side])
        return ctx.enter_context(self.nc.Block())


def bcast(ap, n):
    return ap.unsqueeze(0).broadcast_to([n] + list(ap.shape))


def load_inputs(core):
    nc, dram = core.nc, core.dram
    with ExitStack() as ctx:
        loaded = core.semaphore(ctx, "in_loaded")
        ident_ready = core.semaphore(ctx, "in_ident")
        zeros_ready, zeroed = core.semaphore(ctx, "in_zeros"), core.semaphore(ctx, "in_zeroed")
        block = core.stage(ctx)

        @block.sync
        def _(sp):
            sp.dma_start(core.x[:], dram["x"].rearrange("b (t p) d -> p (b t) d", p=P)).then_inc(loaded, 16)
            sp.dma_start(core.ident[:], dram["identity"]).then_inc(loaded, 16)
            sp.dma_start(core.ctxT[:], dram["ctxT"].rearrange("(k p) n -> p k n", p=P)).then_inc(loaded, 16)
            sp.wait_ge(zeros_ready, 1)
            all_rows = dram["scratch_rows"].rearrange("(n p) d -> p n d", p=P)
            for n in range(0, all_rows.shape[1], 8):
                sp.dma_start(all_rows[:, n:n + 8, :], core.xn[:, 0:8, :]).then_inc(zeroed, 16)
            sp.wait_ge(zeroed, 16 * (all_rows.shape[1] // 8))
            sp.wait_ge(loaded, 48)

        @block.vector
        def _(dve):
            dve.memset(core.xn[:, 0:8, :], 0.0).then_inc(zeros_ready, 1)
            dve.wait_ge(loaded, 48)
            dve.tensor_copy(core.ident_bf[:], core.ident[:]).then_inc(ident_ready, 1)
            dve.wait_ge(ident_ready, 1)


def layer_norm(core, name, src, dst, dstT=None, gainT=None, shiftT=None, gain=None, shift=None, absmax=None):
    nc = core.nc
    with ExitStack() as ctx:
        sb = lambda n, shape, dt=F32: ctx.enter_context(nc.sbuf_tensor(f"{name}_{n}", shape, dt))
        sem = lambda n: core.semaphore(ctx, f"{name}_{n}")
        stats, moments = sb("stats", [P, NT, 6]), sb("moments", [P, NT, 2])
        std, rstd = sb("std", [P, NT]), sb("rstd", [P, NT])
        stats_done, moments_done, std_done, rstd_done = sem("stats"), sem("moments"), sem("std"), sem("rstd")
        tile_normed, transposed, evacuated, gains_in = sem("normed"), sem("transposed"), sem("evac"), sem("gains")
        affine_done = sem("affine")
        if gainT is not None:
            gT, sT = sb("gainT", [P, KD]), sb("shiftT", [P, KD])
        if gain is not None:
            g_bc, s_bc = sb("gain", [P, D]), sb("shift", [P, D])
        block = core.stage(ctx)

        @block.sync
        def _(sp):
            if gainT is not None:
                sp.dma_start(gT[:], gainT).then_inc(gains_in, 16)
                sp.dma_start(sT[:], shiftT).then_inc(gains_in, 16)
                sp.wait_ge(gains_in, 32)
            if gain is not None:
                sp.dma_start(g_bc[:], bcast(gain, P)).then_inc(gains_in, 16)
                sp.dma_start(s_bc[:], bcast(shift, P)).then_inc(gains_in, 16)
                sp.wait_ge(gains_in, 32)

        def evacuate(eng, is_act, g, k):
            out, in_ = dstT[:, k, g * CH:(g + 1) * CH], core.ps[:, 2 * g + k, :]
            if gainT is not None:
                if is_act:
                    return eng.activation(out, in_, ACT.Identity, bias=sT[:, k:k + 1], scale=gT[:, k:k + 1])
                return eng.tensor_scalar(out, in_, gT[:, k:k + 1], sT[:, k:k + 1], ALU.mult, ALU.add)
            return eng.copy(out, in_) if is_act else eng.tensor_copy(out, in_)

        @block.vector
        def _(dve):
            for t in range(NT):
                dve.bn_stats(stats[:, t, :], src[:, t, :]).then_inc(stats_done, 1)
            for t in range(NT):
                dve.wait_ge(stats_done, t + 1)
                dve.bn_aggr(moments[:, t, :], stats[:, t, :]).then_inc(moments_done, 1)
            dve.wait_ge(moments_done, NT)
            dve.tensor_scalar(moments[:, :, 1], moments[:, :, 1], EPS, None, ALU.add).then_inc(moments_done, 1)
            dve.wait_ge(std_done, 1)
            dve.reciprocal(rstd[:], std[:]).then_inc(rstd_done, 1)
            dve.wait_ge(rstd_done, 1)
            for t in range(NT):
                dve.tensor_scalar(dst[:, t, :], src[:, t, :], moments[:, t, 0:1], rstd[:, t:t + 1],
                                  ALU.subtract, ALU.mult).then_inc(tile_normed, 1)
            if gain is not None:
                dve.wait_ge(gains_in, 32)
                dve.wait_ge(tile_normed, NT)
                dve.tensor_tensor(dst[:], dst[:], g_bc[:].unsqueeze(1).broadcast_to([P, NT, D]), ALU.mult).then_inc(affine_done, 1)
                dve.wait_ge(affine_done, 1)
                dve.tensor_tensor(dst[:], dst[:], s_bc[:].unsqueeze(1).broadcast_to([P, NT, D]), ALU.add).then_inc(affine_done, 1)
            if absmax is not None:
                dve.wait_ge(tile_normed, NT)
                dve.tensor_reduce(absmax[:, 0:1], dst[:], mybir.AxisListType.XY, ALU.max, apply_absolute_value=True).then_inc(affine_done, 1)
            if dstT is not None:
                if gainT is not None:
                    dve.wait_ge(gains_in, 32)
                for g in range(NCH):
                    dve.wait_ge(transposed, 2 * g + 2)
                    evacuate(dve, False, g, 1).then_inc(evacuated, 1)

        @block.scalar
        def _(act):
            act.wait_ge(moments_done, NT + 1)
            act.activation(std[:], moments[:, :, 1], ACT.Sqrt).then_inc(std_done, 1)
            if dstT is not None:
                if gainT is not None:
                    act.wait_ge(gains_in, 32)
                for g in range(NCH):
                    act.wait_ge(transposed, 2 * g + 1)
                    evacuate(act, True, g, 0).then_inc(evacuated, 1)

        if dstT is not None:
            @block.tensor
            def _(pe):
                for g in range(NCH):
                    pe.wait_ge(tile_normed, 4 * g + 4)
                    for k in range(KD):
                        for j in range(4):
                            mm = pe.transpose(core.ps[:, 2 * g + k, j * P:(j + 1) * P],
                                              dst[:, 4 * g + j, k * P:(k + 1) * P], core.ident[:])
                        mm.then_inc(transposed, 1)


def transpose_tokens(core, name, src, dstT):
    nc = core.nc
    with ExitStack() as ctx:
        transposed = core.semaphore(ctx, f"{name}_transposed")
        evacuated = core.semaphore(ctx, f"{name}_evac")
        block = core.stage(ctx)

        @block.tensor
        def _(pe):
            for g in range(NCH):
                for k in range(KD):
                    for j in range(4):
                        mm = pe.transpose(core.ps[:, 2 * g + k, j * P:(j + 1) * P],
                                          src[:, 4 * g + j, k * P:(k + 1) * P], core.ident[:])
                    mm.then_inc(transposed, 1)

        @block.vector
        def _(dve):
            for g in range(NCH):
                dve.wait_ge(transposed, 2 * g + 2)
                dve.tensor_copy(dstT[:, 1, g * CH:(g + 1) * CH], core.ps[:, 2 * g + 1, :]).then_inc(evacuated, 1)

        @block.scalar
        def _(act):
            for g in range(NCH):
                act.wait_ge(transposed, 2 * g + 1)
                act.copy(dstT[:, 0, g * CH:(g + 1) * CH], core.ps[:, 2 * g, :]).then_inc(evacuated, 1)


def query_softmax_attention(core):
    nc, dram, ps = core.nc, core.dram, core.ps
    W = BATCH * KEYS
    SCALE = 64 ** -0.5
    with ExitStack() as ctx:
        sb = lambda n, shape, dt=F32: ctx.enter_context(nc.sbuf_tensor(f"a0_{n}", shape, dt))
        sem = lambda n: core.semaphore(ctx, f"a0_{n}")
        wkT, wvT = sb("wkT", [P, KD, FF]), sb("wvT", [P, KD, FF])
        wq, woT = sb("wq", [P, FB, D]), sb("woT", [P, FB, D])
        bq, bk, bv = sb("bq", [P, FB]), sb("bk", [P, FB]), sb("bv", [P, FB])
        bo = sb("bo", [P, D])
        kT, vT = sb("kT", [P, FB, W]), sb("vT", [P, FB, W])
        gT = sb("gT", [P, KD, W])
        cT = sb("cT", [KEYS, BATCH])
        vo = sb("vo", [KEYS, BATCH, D])
        ET = sb("ET", [KEYS, BATCH, SEQ])
        mx, tmp, nb = sb("mx", [KEYS, BATCH]), sb("tmp", [KEYS, BATCH]), sb("nb", [KEYS, BATCH])
        sums, rs = sb("sums", [KEYS, BATCH]), sb("rs", [KEYS, BATCH])
        loaded, kv_mm, k_sb, v_sb, g_mm, g_sb = sem("loaded"), sem("kv_mm"), sem("k_sb"), sem("v_sb"), sem("g_mm"), sem("g_sb")
        s_mm, chain, bias_ready, exp_done, v_ready, y_mm, y_sb = (
            sem("s_mm"), sem("chain"), sem("bias"), sem("exp"), sem("v"), sem("y_mm"), sem("y_sb"))
        block = core.stage(ctx)

        @block.sync
        def _(sp):
            for dst, key, pat in ((wkT, "L0_WkT", "(k p) f -> p k f"), (wvT, "L0_WvT", "(k p) f -> p k f"),
                                  (wq, "L0_Wq", "(f p) d -> p f d"), (woT, "L0_WoT", "(f p) d -> p f d")):
                sp.dma_start(dst[:], dram[key].rearrange(pat, p=P)).then_inc(loaded, 16)
            for dst, key in ((bq, "L0_bq"), (bk, "L0_bk"), (bv, "L0_bv")):
                sp.dma_start(dst[:], dram[key]).then_inc(loaded, 16)
            sp.dma_start(bo[:], bcast(dram["L0_bo"], P)).then_inc(loaded, 16)
            sp.wait_ge(loaded, 128)

        @block.tensor
        def _(pe):
            pe.wait_ge(loaded, 128)
            for i, w in enumerate((wkT, wvT)):
                for f in range(FB):
                    for k in range(KD):
                        mm = pe.matmul(ps[:, 4 * i + f // 2, (f % 2) * W:(f % 2 + 1) * W], w[:, k, f * P:(f + 1) * P],
                                       core.ctxT[:, k, :], start=(k == 0), stop=(k == KD - 1))
                mm.then_inc(kv_mm, 1)
            pe.wait_ge(k_sb, FB // 2)
            for m in range(KD):
                for f in range(FB):
                    mm = pe.matmul(ps[:, m, 0:W], wq[:, f, m * P:(m + 1) * P], kT[:, f, :], start=(f == 0), stop=(f == FB - 1))
            mm.then_inc(g_mm, 1)
            for b in range(BATCH):
                for f in range(FB):
                    mm = pe.matmul(ps[0:KEYS, 2 + b, 0:1], kT[:, f, b * KEYS:(b + 1) * KEYS], bq[:, f:f + 1],
                                   start=(f == 0), stop=(f == FB - 1))
            mm.then_inc(g_mm, 1)
            pe.wait_ge(v_sb, FB // 2)
            for b in range(BATCH):
                for f in range(FB):
                    mm = pe.matmul(ps[0:KEYS, 4 + b, 0:D], vT[:, f, b * KEYS:(b + 1) * KEYS], woT[:, f, :],
                                   start=(f == 0), stop=(f == FB - 1))
            mm.then_inc(g_mm, 1)
            pe.wait_ge(g_sb, 3)
            for b in range(BATCH):
                for c in range(2):
                    for k in range(KD):
                        mm = pe.matmul(ps[0:KEYS, 2 * b + c, :], gT[:, k, b * KEYS:(b + 1) * KEYS],
                                       core.xnT[:, k, b * SEQ + c * CH:b * SEQ + (c + 1) * CH], start=(k == 0), stop=(k == KD - 1))
                mm.then_inc(s_mm, 1)
            for b in range(BATCH):
                pe.wait_ge(exp_done, b + 1)
                pe.wait_ge(v_ready, b + 1)
                for t in range(NT // BATCH):
                    n = b * 8 + t
                    if n >= 4:
                        pe.wait_ge(y_sb, n - 3)
                    pe.matmul(ps[:, 4 + n % 4, 0:D], ET[:, b, t * P:(t + 1) * P], vo[:, b, :], start=True, stop=True).then_inc(y_mm, 1)

        @block.scalar
        def _(act):
            act.wait_ge(kv_mm, 1)
            for f in range(FB):
                ins = act.activation(kT[:, f, :], ps[:, f // 2, (f % 2) * W:(f % 2 + 1) * W], ACT.Identity, bias=bk[:, f:f + 1])
                if f % 2:
                    ins.then_inc(k_sb, 1)
            for b in range(BATCH):
                act.wait_ge(bias_ready, b + 1)
                act.activation(ET[:, b, :], ps[0:KEYS, 2 * b:2 * b + 2, :], ACT.Exp, bias=nb[:, b:b + 1], scale=SCALE,
                               accum_out=sums[:, b:b + 1]).then_inc(exp_done, 1)

        @block.vector
        def _(dve):
            count = [0]

            def link(ins):
                count[0] += 1
                ins.then_inc(chain, 1)
                dve.wait_ge(chain, count[0])

            dve.wait_ge(loaded, 128)
            link(dve.tensor_tensor(core.x[:], core.x[:], bo[:].unsqueeze(1).broadcast_to([P, NT, D]), ALU.add))
            dve.wait_ge(kv_mm, 2)
            for f in range(FB):
                ins = dve.tensor_scalar(vT[:, f, :], ps[:, 4 + f // 2, (f % 2) * W:(f % 2 + 1) * W], bv[:, f:f + 1], None, ALU.add)
                if f % 2:
                    ins.then_inc(v_sb, 1)
            dve.wait_ge(g_mm, 1)
            dve.tensor_copy(gT[:], ps[:, 0:KD, 0:W]).then_inc(g_sb, 1)
            dve.wait_ge(g_mm, 2)
            dve.tensor_copy(cT[:], ps[0:KEYS, 2:4, 0]).then_inc(g_sb, 1)
            dve.wait_ge(g_mm, 3)
            dve.tensor_copy(vo[:], ps[0:KEYS, 4:6, 0:D]).then_inc(g_sb, 1)
            dve.wait_ge(g_sb, 3)
            for b in range(BATCH):
                col = slice(b, b + 1)
                dve.wait_ge(s_mm, b + 1)
                link(dve.tensor_reduce(mx[:, col], ps[0:KEYS, 2 * b:2 * b + 2, :], mybir.AxisListType.XY, ALU.max))
                link(dve.tensor_scalar(tmp[:, col], mx[:, col], cT[:, col], -1.0, ALU.add, ALU.mult))
                link(dve.tensor_scalar(tmp[:, col], tmp[:, col], cT[:, col], None, ALU.add))
                dve.tensor_scalar(nb[:, col], tmp[:, col], SCALE, None, ALU.mult).then_inc(bias_ready, 1)
            for b in range(BATCH):
                dve.wait_ge(exp_done, b + 1)
                link(dve.reciprocal(rs[:, b:b + 1], sums[:, b:b + 1]))
                dve.tensor_scalar(vo[:, b, :], vo[:, b, :], rs[:, b:b + 1], None, ALU.mult).then_inc(v_ready, 1)
            for n in range(NT):
                dve.wait_ge(y_mm, n + 1)
                dve.tensor_tensor(core.x[:, n, :], core.x[:, n, :], ps[:, 4 + n % 4, 0:D], ALU.add).then_inc(y_sb, 1)


def quantised_ffn(core, xmax):
    nc, dram, ps = core.nc, core.dram, core.ps
    with ExitStack() as ctx:
        sb = lambda n, shape, dt=F32: ctx.enter_context(nc.sbuf_tensor(f"q_{n}", shape, dt))
        sem = lambda n: core.semaphore(ctx, f"q_{n}")
        w_inT = sb("w_inT", [P, FB, D])
        w_out = sb("w_out", [P, FB, D])
        w_in = sb("w_in", [P, KD, FF])
        b_in, b_out = sb("b_in", [P, FB]), sb("b_out", [P, D])
        amax, scale, inv = sb("amax", [P, 2 * FB]), sb("scale", [P, 2 * FB]), sb("inv", [P, 2 * FB])
        xs, hs = sb("xs", [P, 4]), sb("hs", [P, 4])
        hid = sb("hid", [P, FB, TOK])
        hmaxes, hmax = sb("hmaxes", [P, FB * NCH]), sb("hmax", [P, 1])
        loaded, chain, wq_done, wT_mm, wT_sb, xq_done = sem("loaded"), sem("chain"), sem("wq"), sem("wT_mm"), sem("wT_sb"), sem("xq")
        xT_mm, xT_sb, h_mm, h_sb, xred, hred, hmax_done, hq_done, y_mm, y_sb, scales_done = (
            sem("xT_mm"), sem("xT_sb"), sem("h_mm"), sem("h_sb"), sem("xred"), sem("hred"), sem("hmax"),
            sem("hq"), sem("y_mm"), sem("y_sb"), sem("scales"))
        block = core.stage(ctx)

        @block.sync
        def _(sp):
            sp.dma_start(w_inT[:], dram["L0_WinT"].rearrange("(f p) d -> p f d", p=P)).then_inc(loaded, 16)
            sp.dma_start(w_out[:], dram["L0_Wout"].rearrange("(f p) d -> p f d", p=P)).then_inc(loaded, 16)
            sp.dma_start(b_in[:], dram["L0_bin"]).then_inc(loaded, 16)
            sp.dma_start(b_out[:], bcast(dram["L0_bout"], P)).then_inc(loaded, 16)
            sp.wait_ge(loaded, 64)

        @block.gpsimd
        def _(pool):
            pool.partition_all_reduce(xs[:, 0:1], xmax[:, 0:1], P, bass.bass_isa.ReduceOp.max).then_inc(xred, 1)
            pool.wait_ge(hmax_done, FB * NCH + 1)
            pool.partition_all_reduce(hs[:, 0:1], hmax[:, 0:1], P, bass.bass_isa.ReduceOp.max).then_inc(hred, 1)

        @block.vector
        def _(dve):
            count = [0]

            def link(ins):
                count[0] += 1
                ins.then_inc(chain, 1)
                dve.wait_ge(chain, count[0])

            def scales_of(s, top):
                link(dve.tensor_scalar(s[:, 0:1], s[:, 0:1], 1e-8, None, ALU.max))
                link(dve.reciprocal(s[:, 1:2], s[:, 0:1]))
                link(dve.tensor_scalar(s[:, 2:3], s[:, 1:2], top, None, ALU.mult))
                link(dve.tensor_scalar(s[:, 3:4], s[:, 0:1], 1.0 / top, None, ALU.mult))

            def quantise(v, s):
                link(dve.tensor_scalar(v, v, s, 32767.0, ALU.mult, ALU.min))
                link(dve.tensor_scalar(v, v, -32768.0, ROUND, ALU.max, ALU.add))
                return dve.tensor_scalar(v, v, ROUND, None, ALU.subtract)

            dve.wait_ge(loaded, 64)
            link(dve.tensor_tensor(core.x[:], core.x[:], b_out[:].unsqueeze(1).broadcast_to([P, NT, D]), ALU.add))
            for i, w in enumerate((w_inT, w_out)):
                link(dve.tensor_reduce(amax[:, i * FB:(i + 1) * FB], w[:], AX, ALU.max, apply_absolute_value=True))
            link(dve.tensor_scalar(amax[:], amax[:], 1e-8, None, ALU.max))
            link(dve.reciprocal(scale[:], amax[:]))
            link(dve.tensor_scalar(scale[:], scale[:], 127.0, None, ALU.mult))
            link(dve.tensor_scalar(inv[:], amax[:], 1.0 / 127.0, None, ALU.mult))
            for i, w in enumerate((w_inT, w_out)):
                for f in range(FB):
                    n = i * FB + f
                    link(dve.tensor_scalar(w[:, f, :], w[:, f, :], scale[:, n:n + 1], 127.0, ALU.mult, ALU.min))
                    link(dve.tensor_scalar(w[:, f, :], w[:, f, :], -128.0, ROUND, ALU.max, ALU.add))
                    if i == 0:
                        dve.tensor_scalar(w[:, f, :], w[:, f, :], ROUND, None, ALU.subtract).then_inc(wq_done, 1)
                    else:
                        dve.tensor_scalar(w[:, f, :], w[:, f, :], ROUND, inv[:, n:n + 1], ALU.subtract, ALU.mult).then_inc(wq_done, 1)
            dve.wait_ge(xred, 1)
            scales_of(xs, 32767.0)
            quantise(core.xn[:], xs[:, 2:3]).then_inc(xq_done, 1)
            dve.tensor_scalar(scale[:, 0:FB], inv[:, 0:FB], xs[:, 3:4], None, ALU.mult).then_inc(scales_done, 1)
            for k in range(KD):
                dve.wait_ge(wT_mm, k + 1)
                dve.tensor_copy(w_in[:, k, :].rearrange("p (c n) -> p c n", n=CH), ps[:, 2 * k:2 * k + 2, :]).then_inc(wT_sb, 1)
            for g in range(NCH):
                dve.wait_ge(xT_mm, g + 1)
                dve.tensor_copy(core.xnT[:, :, g * CH:(g + 1) * CH], ps[:, 4 + 2 * (g % 2):6 + 2 * (g % 2), :]).then_inc(xT_sb, 1)
            for n in range(FB * NCH):
                c, f = n // FB, n % FB
                dve.wait_ge(h_sb, n + 1)
                dve.tensor_reduce(hmaxes[:, n:n + 1], hid[:, f, c * CH:(c + 1) * CH], AX, ALU.max, apply_absolute_value=True).then_inc(hmax_done, 1)
            dve.wait_ge(hmax_done, FB * NCH)
            dve.tensor_reduce(hmax[:], hmaxes[:], AX, ALU.max).then_inc(hmax_done, 1)
            dve.wait_ge(hred, 1)
            scales_of(hs, 32767.0)
            for c in range(NCH):
                quantise(hid[:, :, c * CH:(c + 1) * CH], hs[:, 2:3]).then_inc(hq_done, 1)
            for t in range(NT):
                dve.wait_ge(y_mm, t + 1)
                dve.scalar_tensor_tensor(core.x[:, t, :], ps[:, 4 + t % 4, 0:D], hs[:, 3:4], core.x[:, t, :],
                                         ALU.mult, ALU.add).then_inc(y_sb, 1)

        @block.tensor
        def _(pe):
            pe.wait_ge(wq_done, FB)
            for k in range(KD):
                for f in range(FB):
                    mm = pe.transpose(ps[:, 2 * k + f // 4, (f % 4) * P:(f % 4 + 1) * P], w_inT[:, f, k * P:(k + 1) * P], core.ident[:])
                mm.then_inc(wT_mm, 1)
            pe.wait_ge(xq_done, 1)
            for g in range(NCH):
                if g >= 2:
                    pe.wait_ge(xT_sb, g - 1)
                for k in range(KD):
                    for j in range(4):
                        mm = pe.transpose(ps[:, 4 + 2 * (g % 2) + k, j * P:(j + 1) * P],
                                          core.xn[:, 4 * g + j, k * P:(k + 1) * P], core.ident[:])
                mm.then_inc(xT_mm, 1)
            pe.wait_ge(wT_sb, KD)
            for n in range(FB * NCH):
                c, f = n // FB, n % FB
                pe.wait_ge(xT_sb, c + 1)
                if n >= 4:
                    pe.wait_ge(h_sb, n - 3)
                for k in range(KD):
                    mm = pe.matmul(ps[:, n % 4, :], w_in[:, k, f * P:(f + 1) * P], core.xnT[:, k, c * CH:(c + 1) * CH],
                                   start=(k == 0), stop=(k == KD - 1))
                mm.then_inc(h_mm, 1)
            pe.wait_ge(wq_done, 2 * FB)
            for t in range(NT):
                pe.wait_ge(hq_done, t // 4 + 1)
                if t >= 4:
                    pe.wait_ge(y_sb, t - 3)
                for f in range(FB):
                    mm = pe.matmul(ps[:, 4 + t % 4, 0:D], hid[:, f, t * P:(t + 1) * P], w_out[:, f, :], start=(f == 0), stop=(f == FB - 1))
                mm.then_inc(y_mm, 1)

        @block.scalar
        def _(act):
            act.wait_ge(scales_done, 1)
            act.wait_ge(loaded, 64)
            for n in range(FB * NCH):
                c, f = n // FB, n % FB
                act.wait_ge(h_mm, n + 1)
                act.activation(hid[:, f, c * CH:(c + 1) * CH], ps[:, n % 4, :], ACT.Gelu, bias=b_in[:, f:f + 1],
                               scale=scale[:, f:f + 1]).then_inc(h_sb, 1)


def headed_cross_attention(core, name, wqT, wkT, wvT, woT, out, bias=None, mask=None, bq=None, bk=None, bv=None):
    nc, dram, ps = core.nc, core.dram, core.ps
    W = BATCH * KEYS
    HW = 4 * KEYS
    with ExitStack() as ctx:
        sb = lambda n, shape, dt=F32: ctx.enter_context(nc.sbuf_tensor(f"{name}_{n}", shape, dt))
        sem = lambda n: core.semaphore(ctx, f"{name}_{n}")
        w = {n: sb(n, [P, KD, D]) for n in ("wq", "wk", "wv", "wo")}
        qT, kT = sb("qT", [P, KD, TOK]), sb("kT", [P, KD, W])
        kbd = sb("kbd", [P, BATCH, KD, 8, KEYS])
        vh = sb("vh", [KEYS, BATCH, HEADS, DK + 1])
        head_of = sb("head_of", [P, 8])
        s = sb("s", [P, 2, HEADS, KEYS])
        mx = sb("mx", [P, 2, HEADS])
        pT = sb("pT", [KEYS, 2, HEADS, P])
        rs, on, oT = sb("rs", [P, 2, HEADS]), sb("on", [P, 2, D]), sb("oT", [P, 2, KD, P])
        if bias is not None:
            bt = sb("bt", [P, 3, HEADS, KEYS])
        else:
            mt, bt = sb("mt", [P, NT, KEYS], U8), sb("bt", [P, NT, KEYS])
        if bq is not None:
            bqT, bkT, bv_bc = sb("bqT", [P, KD]), sb("bkT", [P, KD]), sb("bv", [KEYS, D])
        loaded, bias_in = sem("loaded"), [sem(f"bias{i}") for i in range(3)]
        q_mm, q_sb, kv_mm, k_sb, kbd_done, v_sb, ones_done, limit_done = (
            sem("q_mm"), sem("q_sb"), sem("kv_mm"), sem("k_sb"), sem("kbd"), sem("v_sb"), sem("ones"), sem("limit"))
        s_mm, s_sb, chain, s_ready, exp_done, pT_mm, pT_sb, o_mm, o_sb, oT_mm, oT_sb, y_mm, y_sb = (
            sem(x) for x in ("s_mm", "s_sb", "chain", "s_ready", "exp", "pT_mm", "pT_sb", "o_mm", "o_sb", "oT_mm", "oT_sb", "y_mm", "y_sb"))
        loads = 5 + (3 if bq is not None else 0) + (1 if mask is not None else 0)
        block = core.stage(ctx)

        @block.sync
        def _(sp):
            for n, a in (("wq", wqT), ("wk", wkT), ("wv", wvT), ("wo", woT)):
                sp.dma_start(w[n][:], a.rearrange("(k p) d -> p k d", p=P)).then_inc(loaded, 16)
            sp.dma_start(head_of[:], dram["head_of"]).then_inc(loaded, 16)
            if bq is not None:
                sp.dma_start(bqT[:], bq).then_inc(loaded, 16)
                sp.dma_start(bkT[:], bk).then_inc(loaded, 16)
                sp.dma_start(bv_bc[:], bcast(bv, KEYS)).then_inc(loaded, 16)
            if mask is not None:
                sp.dma_start(mt[:], mask.rearrange("(t p) k -> p t k", p=P)).then_inc(loaded, 16)
            sp.wait_ge(loaded, 16 * loads)
            if bias is not None:
                for t in range(NT):
                    if t >= 3:
                        sp.wait_ge(s_sb, t - 2)
                    sp.dma_start(bt[:, t % 3, :, :], bias[t]).then_inc(bias_in[t % 3], 16)

        @block.gpsimd
        def _(pool):
            pool.memset(vh[:, :, :, DK:DK + 1], 1.0).then_inc(ones_done, 1)

        @block.vector
        def _(dve):
            count = [0]

            def link(ins):
                count[0] += 1
                ins.then_inc(chain, 1)
                dve.wait_ge(chain, count[0])

            dve.wait_ge(loaded, 16 * loads)
            if mask is not None:
                link(dve.tensor_scalar(bt[:], mt[:], -3e38, 3e38, ALU.mult, ALU.add))
                link(dve.scalar_tensor_tensor(bt[:], mt[:], NEG, bt[:], ALU.mult, ALU.add))
            dve.wait_ge(kv_mm, 1)
            for k in range(KD):
                if bk is not None:
                    link(dve.tensor_scalar(kT[:, k, :], ps[:, k, 0:W], bkT[:, k:k + 1], 0.25, ALU.add, ALU.mult))
                else:
                    link(dve.tensor_scalar(kT[:, k, :], ps[:, k, 0:W], 0.25, None, ALU.mult))
            for b in range(BATCH):
                for k in range(KD):
                    for h in range(8):
                        dve.tensor_scalar(kbd[:, b, k, h, :], kT[:, k, b * KEYS:(b + 1) * KEYS], head_of[:, h:h + 1], None,
                                          ALU.mult).then_inc(kbd_done, 1)
            dve.wait_ge(kv_mm, 2)
            for b in range(BATCH):
                vin = ps[0:KEYS, 2 + b, 0:D].rearrange("p (h d) -> p h d", d=DK)
                if bv is not None:
                    dve.tensor_tensor(vh[:, b, :, 0:DK], vin, bv_bc[:].rearrange("p (h d) -> p h d", d=DK), ALU.add).then_inc(v_sb, 1)
                else:
                    dve.tensor_copy(vh[:, b, :, 0:DK], vin).then_inc(v_sb, 1)

            def scores(t):
                i = t % 2
                dve.wait_ge(s_mm, t + 1)
                if t >= 2:
                    dve.wait_ge(pT_mm, 4 * (t - 1))
                raw = ps[:, 0:4, 0:HW].rearrange("p c (h k) -> p c h k", k=KEYS)
                si = s[:, i, :, :].rearrange("p (c h) k -> p c h k", c=4)
                if bias is not None:
                    dve.wait_ge(bias_in[t % 3], 16 * (t // 3 + 1))
                    ins = dve.tensor_tensor(si, raw, bt[:, t % 3, :, :].rearrange("p (c h) k -> p c h k", c=4), ALU.add)
                else:
                    ins = dve.tensor_tensor(si, raw, bt[:, t, :].unsqueeze(1).unsqueeze(1).broadcast_to([P, 4, 4, KEYS]), ALU.min)
                ins.then_inc(s_sb, 1)
                dve.wait_ge(s_sb, t + 1)
                link(dve.tensor_reduce(mx[:, i, :], s[:, i, :, :], AX, ALU.max))
                dve.tensor_tensor(s[:, i, :, :], s[:, i, :, :], mx[:, i, :].unsqueeze(2).broadcast_to([P, HEADS, KEYS]),
                                  ALU.subtract).then_inc(s_ready, 1)

            def outputs(t):
                i = t % 2
                dve.wait_ge(o_mm, t + 1)
                o = ps[:, 6, 0:HEADS * (DK + 1)].rearrange("p (h d) -> p h d", d=DK + 1)
                link(dve.reciprocal(rs[:, i, :], o[:, :, DK]))
                if t >= 2:
                    dve.wait_ge(oT_mm, t - 1)
                dve.tensor_tensor(on[:, i, :].rearrange("p (h d) -> p h d", d=DK), o[:, :, 0:DK],
                                  rs[:, i, :].unsqueeze(2).broadcast_to([P, HEADS, DK]), ALU.mult).then_inc(o_sb, 1)
                dve.wait_ge(y_mm, t + 1)
                dve.tensor_tensor(out[:, t, :], out[:, t, :], ps[:, 7, 0:D], ALU.add).then_inc(y_sb, 1)

            for t in range(NT):
                scores(t)
                if t:
                    outputs(t - 1)
            outputs(NT - 1)

        @block.scalar
        def _(act):
            act.wait_ge(loaded, 16 * loads)
            for n in range(KD * NCH):
                act.wait_ge(q_mm, n + 1)
                out_, in_ = qT[:, n // NCH, (n % NCH) * CH:(n % NCH + 1) * CH], ps[:, 4 + n % 4, :]
                if bq is not None:
                    act.activation(out_, in_, ACT.Identity, bias=bqT[:, n // NCH:n // NCH + 1]).then_inc(q_sb, 1)
                else:
                    act.copy(out_, in_).then_inc(q_sb, 1)
            for t in range(NT):
                i = t % 2
                act.wait_ge(s_ready, t + 1)
                act.activation(s[:, i, :, :], s[:, i, :, :], ACT.Exp).then_inc(exp_done, 1)
                if t >= 2:
                    act.wait_ge(o_mm, t - 1)
                for q in range(4):
                    act.wait_ge(pT_mm, 4 * t + q + 1)
                    act.copy(pT[:, i, 4 * q:4 * q + 4, :], ps[0:KEYS, 4 + q % 2, :].rearrange("p (h n) -> p h n", n=P)).then_inc(pT_sb, 1)
                act.wait_ge(oT_mm, t + 1)
                act.copy(oT[:, i, :, :], ps[:, 7, D:2 * D].rearrange("p (k n) -> p k n", n=P)).then_inc(oT_sb, 1)

        @block.tensor
        def _(pe):
            pe.wait_ge(loaded, 16 * loads)
            for k2 in range(KD):
                for k in range(KD):
                    mm = pe.matmul(ps[:, k2, 0:W], w["wk"][:, k, k2 * P:(k2 + 1) * P], core.ctxT[:, k, :], start=(k == 0), stop=(k == KD - 1))
            mm.then_inc(kv_mm, 1)
            for b in range(BATCH):
                for k in range(KD):
                    mm = pe.matmul(ps[0:KEYS, 2 + b, 0:D], core.ctxT[:, k, b * KEYS:(b + 1) * KEYS], w["wv"][:, k, :], start=(k == 0), stop=(k == KD - 1))
            mm.then_inc(kv_mm, 1)
            for n in range(KD * NCH):
                k2, c = n // NCH, n % NCH
                if n >= 4:
                    pe.wait_ge(q_sb, n - 3)
                for k in range(KD):
                    mm = pe.matmul(ps[:, 4 + n % 4, :], w["wq"][:, k, k2 * P:(k2 + 1) * P], core.xnT[:, k, c * CH:(c + 1) * CH],
                                   start=(k == 0), stop=(k == KD - 1))
                mm.then_inc(q_mm, 1)
            pe.wait_ge(q_sb, KD * NCH)
            pe.wait_ge(kbd_done, BATCH * HEADS)
            pe.wait_ge(v_sb, BATCH)
            pe.wait_ge(ones_done, 1)

            def scores(t):
                if t:
                    pe.wait_ge(s_sb, t)
                for c in range(4):
                    mm = pe.matmul(ps[:, c, 0:HW], qT[:, c // 2, t * P:(t + 1) * P],
                                   kbd[:, t // 8, c // 2, 4 * (c % 2):4 * (c % 2) + 4, :], start=True, stop=True)
                mm.then_inc(s_mm, 1)

            scores(0)
            for t in range(NT):
                i = t % 2
                pe.wait_ge(exp_done, t + 1)
                for q in range(4):
                    if 4 * t + q >= 2:
                        pe.wait_ge(pT_sb, 4 * t + q - 1)
                    for j in range(4):
                        mm = pe.transpose(ps[0:KEYS, 4 + q % 2, j * P:(j + 1) * P], s[:, i, 4 * q + j, :], core.ident[:])
                    mm.then_inc(pT_mm, 1)
                if t + 1 < NT:
                    scores(t + 1)
                pe.wait_ge(pT_sb, 4 * t + 4)
                if t:
                    pe.wait_ge(o_sb, t)
                for h in range(HEADS):
                    mm = pe.matmul(ps[:, 6, h * (DK + 1):(h + 1) * (DK + 1)], pT[:, i, h, :], vh[:, t // 8, h, :], start=True, stop=True)
                mm.then_inc(o_mm, 1)
                pe.wait_ge(o_sb, t + 1)
                if t:
                    pe.wait_ge(y_sb, t)
                for k in range(KD):
                    mm = pe.transpose(ps[:, 7, D + k * P:D + (k + 1) * P], on[:, i, k * P:(k + 1) * P], core.ident[:])
                mm.then_inc(oT_mm, 1)
                pe.wait_ge(oT_sb, t + 1)
                for k in range(KD):
                    mm = pe.matmul(ps[:, 7, 0:D], oT[:, i, k, :], w["wo"][:, k, :], start=(k == 0), stop=(k == KD - 1))
                mm.then_inc(y_mm, 1)


def plain_cross_attention(core):
    nc, dram, ps = core.nc, core.dram, core.ps
    with ExitStack() as ctx:
        sb = lambda n, shape, dt=F32: ctx.enter_context(nc.sbuf_tensor(f"a2_{n}", shape, dt))
        sem = lambda n: core.semaphore(ctx, f"a2_{n}")
        ctx_sb = sb("ctx", [KEYS, BATCH, D])
        mi, mf = sb("mi", [P, BATCH, KEYS], I32), sb("mf", [P, BATCH, KEYS])
        s, p = sb("s", [P, NT, KEYS]), sb("p", [P, NT, KEYS])
        mx, sums, rs = sb("mx", [P, NT]), sb("sums", [P, NT]), sb("rs", [P, NT])
        pT = sb("pT", [KEYS, NT, P])
        loaded, s_mm, chain, s_ready, exp_done, rs_done, pT_mm, pT_sb, y_mm, y_sb = (
            sem(x) for x in ("loaded", "s_mm", "chain", "s_ready", "exp", "rs", "pT_mm", "pT_sb", "y_mm", "y_sb"))
        block = core.stage(ctx)
        PER = 4

        @block.sync
        def _(sp):
            sp.dma_start(ctx_sb[:], dram["ctx"].rearrange("b k d -> k b d")).then_inc(loaded, 16)
            sp.dma_start(mi[:], bcast(dram["mask_ik"], P)).then_inc(loaded, 16)
            sp.wait_ge(loaded, 32)

        @block.tensor
        def _(pe):
            for t in range(NT):
                for k in range(KD):
                    mm = pe.matmul(ps[:, t // PER, (t % PER) * KEYS:(t % PER + 1) * KEYS], core.xnT[:, k, t * P:(t + 1) * P],
                                   core.ctxT[:, k, (t // 8) * KEYS:(t // 8 + 1) * KEYS], start=(k == 0), stop=(k == KD - 1))
                if t % PER == PER - 1:
                    mm.then_inc(s_mm, 1)
            pe.wait_ge(loaded, 32)
            pe.wait_ge(exp_done, NT)
            for g in range(NT // 4):
                for j in range(4):
                    mm = pe.transpose(ps[0:KEYS, 4 + g, j * P:(j + 1) * P], p[:, 4 * g + j, :], core.ident[:])
                mm.then_inc(pT_mm, 1)
            for t in range(NT):
                pe.wait_ge(pT_sb, t // 4 + 1)
                if t >= 4:
                    pe.wait_ge(y_sb, t - 3)
                pe.matmul(ps[:, t % 4, 0:D], pT[:, t, :], ctx_sb[:, t // 8, :], start=True, stop=True).then_inc(y_mm, 1)

        @block.scalar
        def _(act):
            for t in range(NT):
                act.wait_ge(s_ready, t // 8 + 1)
                act.activation(p[:, t, :], s[:, t, :], ACT.Exp, accum_out=sums[:, t:t + 1]).then_inc(exp_done, 1)
            for g in range(NT // 4):
                act.wait_ge(pT_mm, g + 1)
                act.copy(pT[:, 4 * g:4 * g + 4, :], ps[0:KEYS, 4 + g, :].rearrange("p (t n) -> p t n", n=P)).then_inc(pT_sb, 1)

        @block.vector
        def _(dve):
            count = [0]

            def link(ins):
                count[0] += 1
                ins.then_inc(chain, 1)
                dve.wait_ge(chain, count[0])

            dve.wait_ge(loaded, 32)
            link(dve.tensor_scalar(mf[:], mi[:], NEG, None, ALU.mult))
            for b in range(BATCH):
                dve.wait_ge(s_mm, 2 * b + 2)
                sb_ = s[:, 8 * b:8 * b + 8, :]
                for c in range(2):
                    link(dve.scalar_tensor_tensor(s[:, 8 * b + 4 * c:8 * b + 4 * c + 4, :],
                                                  ps[:, 2 * b + c, 0:PER * KEYS].rearrange("p (t k) -> p t k", k=KEYS),
                                                  D ** -0.5, mf[:, b, :].unsqueeze(1).broadcast_to([P, 4, KEYS]), ALU.mult, ALU.add))
                link(dve.tensor_reduce(mx[:, 8 * b:8 * b + 8], sb_, AX, ALU.max))
                dve.tensor_tensor(sb_, sb_, mx[:, 8 * b:8 * b + 8].unsqueeze(2).broadcast_to([P, 8, KEYS]), ALU.subtract).then_inc(s_ready, 1)
            dve.wait_ge(exp_done, NT)
            link(dve.reciprocal(rs[:], sums[:]))
            for t in range(NT):
                dve.wait_ge(y_mm, t + 1)
                dve.scalar_tensor_tensor(core.x[:, t, :], ps[:, t % 4, 0:D], rs[:, t:t + 1], core.x[:, t, :],
                                         ALU.mult, ALU.add).then_inc(y_sb, 1)


class Routing:

    def __init__(self, core, ctx, name, choices):
        sb = lambda n, shape, dt=F32: ctx.enter_context(core.nc.sbuf_tensor(f"{name}_{n}", shape, dt))
        self.choices = choices
        self.slots = choices * NT + EXPERTS
        self.place = sb("place", [P, choices, NT], I32)
        self.weight = sb("weight", [P, choices, NT])
        self.expert = sb("expert", [1, self.slots], I32)


def expert_weights(core, name, kind, wg, bg, ew, b2, acc, routing=None):
    nc, dram, ps = core.nc, core.dram, core.ps
    with ExitStack() as ctx:
        sb = lambda n, shape, dt=F32: ctx.enter_context(nc.sbuf_tensor(f"{name}_{n}", shape, dt))
        sem = lambda n: core.semaphore(ctx, f"{name}_{n}")
        wg_sb, bg_sb, b2_sb = sb("wg", [P, KD, EXPERTS]), sb("bg", [P, EXPERTS]), sb("b2", [EXPERTS, D])
        rank = sb("rank", [P, EXPERTS])
        lg, t1, t2 = (sb(n, [P, NT, EXPERTS]) for n in ("lg", "t1", "t2"))
        m1, m2, r1, e2 = (sb(n, [P, NT]) for n in ("m1", "m2", "r1", "e2"))
        w8 = sb("w8", [P, NT, EXPERTS])
        if b2 is not None:
            ewT = sb("ewT", [EXPERTS, NT, P])
        if routing is not None:
            before = sb("before", [P, P])
            ones = sb("ones", [P, P])
            chosen = sb("chosen", [P, NT, EXPERTS])
            base = sb("base", [P, NT + 1, EXPERTS])
            cum = [sb(f"cum{i}", [P, EXPERTS]) for i in range(2)]
            start = sb("start", [P, EXPERTS])
            pf = sb("pf", [P, NT])
            slot_ids = sb("slot_ids", [1, routing.slots])
            past = sb("past", [1, routing.slots, EXPERTS])
            ef = sb("ef", [1, routing.slots])
            chosen_done, rank_mm, place_done, rows_out = sem("chosen"), sem("rank_mm"), sem("place"), core.lasting_semaphore(f"{name}_rows_out")
        loaded, g_mm, chain, act_in, act_out, w_done, wT_mm, wT_sb, y_mm, y_sb = (
            sem(x) for x in ("loaded", "g_mm", "chain", "act_in", "act_out", "w", "wT_mm", "wT_sb", "y_mm", "y_sb"))
        loads = 3 + (b2 is not None) + 2 * (routing is not None)
        block = core.stage(ctx)
        per_token = lambda v: v[:].unsqueeze(2).broadcast_to([P, NT, EXPERTS])
        per_expert = lambda v: v[:].unsqueeze(1).broadcast_to([P, NT, EXPERTS])

        @block.sync
        def _(sp):
            sp.dma_start(wg_sb[:], wg.rearrange("(k p) e -> p k e", p=P)).then_inc(loaded, 16)
            sp.dma_start(bg_sb[:], bcast(bg, P)).then_inc(loaded, 16)
            sp.dma_start(rank[:], bcast(dram["rank"], P)).then_inc(loaded, 16)
            if b2 is not None:
                sp.dma_start(b2_sb[:], b2).then_inc(loaded, 16)
            if routing is not None:
                sp.dma_start(before[:], dram["before"]).then_inc(loaded, 16)
                sp.dma_start(slot_ids[:], dram["slot_ids"][0:routing.slots].unsqueeze(0)).then_inc(loaded, 16)
            sp.wait_ge(loaded, 16 * loads)

        if routing is not None:
            @block.gpsimd
            def _(pool):
                pool.memset(ones[:], 1.0).then_inc(chosen_done, 1)
                for k in range(routing.choices):
                    pool.wait_ge(place_done, k + 1)
                    for t in range(NT):
                        pool.indirect_dma_start(dram["scratch_rows"], bass.IndirectOffsetOnAxis(ap=routing.place[:, k, t:t + 1], axis=0),
                                                core.xn[:, t, :], None, bounds_check=(routing.slots - 1) * P + P - 1).then_inc(rows_out, 16)
                pool.wait_ge(rows_out, 16 * routing.choices * NT)

        @block.tensor
        def _(pe):
            pe.wait_ge(loaded, 16 * loads)
            for t in range(NT):
                for k in range(KD):
                    mm = pe.matmul(ps[:, 0, t * EXPERTS:(t + 1) * EXPERTS], core.xnT[:, k, t * P:(t + 1) * P], wg_sb[:, k, :],
                                   start=(k == 0), stop=(k == KD - 1))
            mm.then_inc(g_mm, 1)
            if routing is not None:
                pe.wait_ge(chosen_done, 2)
                pe.matmul(ps[:, 5, 0:NT * EXPERTS], before[:], chosen[:].rearrange("p t e -> p (t e)"), start=True, stop=True)
                pe.matmul(ps[:, 5, NT * EXPERTS:2 * NT * EXPERTS], ones[:], chosen[:].rearrange("p t e -> p (t e)"),
                          start=True, stop=True).then_inc(rank_mm, 1)
            if b2 is not None:
                pe.wait_ge(w_done, 1)
                for g in range(NT // 4):
                    for j in range(4):
                        mm = pe.transpose(ps[0:EXPERTS, 1 + g, j * P:(j + 1) * P], w8[:, 4 * g + j, :], core.ident[:])
                mm.then_inc(wT_mm, 1)
                pe.wait_ge(wT_sb, 1)
                for t in range(NT):
                    if t >= 2:
                        pe.wait_ge(y_sb, t - 1)
                    pe.matmul(ps[:, 6 + t % 2, 0:D], ewT[:, t, :], b2_sb[:], start=True, stop=True).then_inc(y_mm, 1)

        @block.scalar
        def _(act):
            act.wait_ge(act_in, 1)
            if kind == "top2":
                act.activation(e2[:], m2[:], ACT.Exp).then_inc(act_out, 1)
            else:
                act.activation(t1[:], lg[:], ACT.Sigmoid).then_inc(act_out, 1)

        @block.vector
        def _(dve):
            count = [0]

            def link(ins):
                count[0] += 1
                ins.then_inc(chain, 1)
                dve.wait_ge(chain, count[0])

            def first_best(values, best, onehot):
                link(dve.tensor_reduce(best[:], values[:], AX, ALU.max))
                link(dve.tensor_tensor(onehot[:], values[:], per_token(best), ALU.is_equal))
                link(dve.tensor_tensor(onehot[:], onehot[:], per_expert(rank), ALU.mult))
                link(dve.tensor_reduce(r1[:], onehot[:], AX, ALU.max))
                link(dve.tensor_tensor(onehot[:], onehot[:], per_token(r1), ALU.is_equal))

            dve.wait_ge(loaded, 16 * loads)
            dve.wait_ge(g_mm, 1)
            logits = ps[:, 0, 0:NT * EXPERTS].rearrange("p (t e) -> p t e", e=EXPERTS)
            link(dve.tensor_tensor(lg[:], logits, per_expert(bg_sb), ALU.add))
            if kind == "top2":
                first_best(lg, m1, t1)
                link(dve.scalar_tensor_tensor(lg[:], t1[:], -3e38, lg[:], ALU.mult, ALU.add))
                first_best(lg, m2, t2)
                dve.tensor_tensor(m2[:], m2[:], m1[:], ALU.subtract).then_inc(act_in, 1)
                dve.wait_ge(act_out, 1)
                link(dve.tensor_scalar(m1[:], e2[:], 1.0, None, ALU.add))
                link(dve.reciprocal(m1[:], m1[:]))
                link(dve.tensor_tensor(m2[:], e2[:], m1[:], ALU.mult))
                link(dve.tensor_tensor(chosen[:], t1[:], per_token(m1), ALU.mult))
                link(dve.tensor_tensor(lg[:], t2[:], per_token(m2), ALU.mult))
                dve.tensor_tensor(w8[:], chosen[:], lg[:], ALU.add).then_inc(w_done, 1)
                link(dve.tensor_copy(routing.weight[:, 0, :], m1[:]))
                link(dve.tensor_copy(routing.weight[:, 1, :], m2[:]))
                dve.wait_ge(w_done, 1)
                dve.tensor_tensor(chosen[:], t1[:], t2[:], ALU.add).then_inc(chosen_done, 1)
            elif kind == "threshold":
                dve.sem_inc(act_in, 1)
                dve.wait_ge(act_out, 1)
                dve.scalar_tensor_tensor(w8[:], t1[:], 0.5, t1[:], ALU.is_gt, ALU.mult).then_inc(w_done, 1)
            else:
                dve.sem_inc(act_in, 1)
                dve.wait_ge(act_out, 1)
                first_best(t1, m1, t2)
                link(dve.tensor_copy(routing.weight[:, 0, :], m1[:]))
                dve.tensor_copy(chosen[:], t2[:]).then_inc(chosen_done, 1)
            if routing is not None:
                link(dve.memset(base[:, 0, :], 0.0))
                dve.wait_ge(rank_mm, 1)
                counts = ps[:, 5, :].rearrange("p (i t e) -> p i t e", i=4, e=EXPERTS)
                for t in range(NT):
                    link(dve.tensor_tensor(base[:, t + 1, :], base[:, t, :], counts[:, 1, t, :], ALU.add))
                link(dve.tensor_scalar(cum[0][:], base[:, NT, :], 1.0 / P, (P - 1) / P - 0.5 + 0.5 / P, ALU.mult, ALU.add))
                link(dve.tensor_scalar(cum[0][:], cum[0][:], ROUND, ROUND, ALU.add, ALU.subtract))
                link(dve.tensor_copy(start[:], cum[0][:]))
                for i, n in enumerate((1, 2, 4)):
                    a, b = cum[i % 2], cum[1 - i % 2]
                    link(dve.tensor_copy(b[:, 0:n], a[:, 0:n]))
                    link(dve.tensor_tensor(b[:, n:], a[:, n:], a[:, 0:EXPERTS - n], ALU.add))
                ends = cum[1]
                link(dve.tensor_tensor(start[:], ends[:], start[:], ALU.subtract))
                link(dve.tensor_scalar(start[:], start[:], float(P), None, ALU.mult))
                link(dve.tensor_tensor(base[:, 0:NT, :], base[:, 0:NT, :], counts[:, 0], ALU.add))
                link(dve.tensor_tensor(base[:, 0:NT, :], base[:, 0:NT, :], per_expert(start), ALU.add))
                for k, onehot in enumerate((t1, t2) if kind == "top2" else (t2,)):
                    link(dve.tensor_tensor(onehot[:], onehot[:], base[:, 0:NT, :], ALU.mult))
                    link(dve.tensor_reduce(pf[:], onehot[:], AX, ALU.add))
                    dve.tensor_copy(routing.place[:, k, :], pf[:]).then_inc(place_done, 1)
                    dve.wait_ge(place_done, k + 1)
                link(dve.tensor_tensor(past[:], ends[0:1, :].unsqueeze(1).broadcast_to([1, routing.slots, EXPERTS]),
                                       slot_ids[:].unsqueeze(2).broadcast_to([1, routing.slots, EXPERTS]), ALU.is_le))
                link(dve.tensor_reduce(ef[:], past[:], AX, ALU.add))
                link(dve.tensor_scalar(ef[:], ef[:], EXPERTS - 1.0, None, ALU.min))
                link(dve.tensor_copy(routing.expert[:], ef[:]))
            else:
                dve.wait_ge(w_done, 1)
                dve.tensor_copy(ew[:].rearrange("p e t -> p t e"), w8[:]).then_inc(w_done, 1)
            if b2 is not None:
                dve.wait_ge(wT_mm, 1)
                dve.tensor_copy(ewT[:].rearrange("e (g t) p -> e g (t p)", g=4), ps[0:EXPERTS, 1:5, :]).then_inc(wT_sb, 1)
                for t in range(NT):
                    dve.wait_ge(y_mm, t + 1)
                    dve.tensor_tensor(acc[:, t, :], acc[:, t, :], ps[:, 6 + t % 2, 0:D], ALU.add).then_inc(y_sb, 1)


def feed_forward(core, name, experts, w1, b1, w2, func, acc, ew=None):
    nc, dram, ps = core.nc, core.dram, core.ps
    with ExitStack() as ctx:
        sb = lambda n, shape, dt=F32: ctx.enter_context(nc.sbuf_tensor(f"{name}_{n}", shape, dt))
        sem = lambda n: core.semaphore(ctx, f"{name}_{n}")
        B = min(2, experts)
        w1_sb = [sb(f"w1_{u}", [P, KD, FF]) for u in range(B)]
        w2_sb = [sb(f"w2_{u}", [P, FB, D]) for u in range(B)]
        b1_sb = [sb(f"b1_{u}", [P, FB]) for u in range(B)]
        hid = sb("hid", [P, FB, CH])
        w_in = [sem(f"w_in{u}") for u in range(B)]
        w_free, h_mm, h_sb, y_mm, y_sb = sem("w_free"), sem("h_mm"), sem("h_sb"), sem("y_mm"), sem("y_sb")
        HB, YB = 4, 4
        LOADS = 48 if b1 is not None else 32
        block = core.stage(ctx)

        @block.sync
        def _(sp):
            with sp.Fori(0, experts // B) as i:
                for u in range(B):
                    e = i * B + u
                    sp.wait_ge(w_free, e + 1)
                    sp.dma_start(w1_sb[u][:], w1[bass.ds(e, 1)].rearrange("e (k p) f -> p (e k) f", p=P)).then_inc(w_in[u], 16)
                    sp.dma_start(w2_sb[u][:], w2[bass.ds(e, 1)].rearrange("e (f p) d -> p (e f) d", p=P)).then_inc(w_in[u], 16)
                    if b1 is not None:
                        sp.dma_start(b1_sb[u][:], b1[:, bass.ds(e, 1), :].rearrange("p e f -> p (e f)")).then_inc(w_in[u], 16)

        @block.tensor
        def _(pe):
            pe.sem_inc(w_free, B)
            with pe.Fori(0, experts // B) as i:
                for u in range(B):
                    e = i * B + u
                    pe.wait_ge(w_in[u], LOADS * i + LOADS)
                    for c in range(NCH):
                        for f in range(FB):
                            pe.wait_ge(h_sb, e * (NCH * FB) + (c * FB + f + 1))
                            for k in range(KD):
                                mm = pe.matmul(ps[:, f % HB, :], w1_sb[u][:, k, f * P:(f + 1) * P],
                                               core.xnT[:, k, c * CH:(c + 1) * CH], start=(k == 0), stop=(k == KD - 1))
                            mm.then_inc(h_mm, 1)
                        pe.wait_ge(h_sb, e * (NCH * FB) + (c * FB + FB + HB))
                        for t in range(4):
                            pe.wait_ge(y_sb, e * NT + (4 * c + t + 1))
                            for f in range(FB):
                                mm = pe.matmul(ps[:, HB + t, 0:D], hid[:, f, t * P:(t + 1) * P], w2_sb[u][:, f, :],
                                               start=(f == 0), stop=(f == FB - 1))
                            mm.then_inc(y_mm, 1)
                    pe.wait_ge(y_mm, e * NT + NT)
                    pe.sem_inc(w_free, 1)

        @block.scalar
        def _(act):
            act.sem_inc(h_sb, HB)
            with act.Fori(0, experts // B) as i:
                for u in range(B):
                    e = i * B + u
                    act.wait_ge(w_in[u], LOADS * i + LOADS)
                    for c in range(NCH):
                        for f in range(FB):
                            act.wait_ge(h_mm, e * (NCH * FB) + (c * FB + f + 1))
                            bias = b1_sb[u][:, f:f + 1] if b1 is not None else 0.0
                            act.activation(hid[:, f, :], ps[:, f % HB, :], func, bias=bias).then_inc(h_sb, 1)

        @block.vector
        def _(dve):
            dve.sem_inc(y_sb, YB)
            with dve.Fori(0, experts // B) as i:
                for u in range(B):
                    e = i * B + u
                    for t in range(NT):
                        dve.wait_ge(y_mm, e * NT + (t + 1))
                        y = ps[:, HB + t % 4, 0:D]
                        if ew is not None:
                            ins = dve.scalar_tensor_tensor(acc[:, t, :], y, ew[:, bass.ds(e, 1), t], acc[:, t, :], ALU.mult, ALU.add)
                        else:
                            ins = dve.tensor_tensor(acc[:, t, :], acc[:, t, :], y, ALU.add)
                        ins.then_inc(y_sb, 1)


def load_experts(core, ctx, name, w1, b1, w2):
    nc = core.nc
    sb = lambda n, shape: ctx.enter_context(nc.sbuf_tensor(f"{name}_{n}", shape, F32))
    w1_sb, w2_sb = sb("w1", [P, EXPERTS, KD, FF]), sb("w2", [P, EXPERTS, FB, D])
    b1_sb = sb("b1", [P, EXPERTS, FB]) if b1 is not None else None
    arrived = core.lasting_semaphore(f"{name}_experts_in")
    for e in range(EXPERTS):
        nc.sync.dma_start(w1_sb[:, e, :, :], w1[e].rearrange("(k p) f -> p k f", p=P)).then_inc(arrived, 16)
        nc.sync.dma_start(w2_sb[:, e, :, :], w2[e].rearrange("(f p) d -> p f d", p=P)).then_inc(arrived, 16)
    if b1 is not None:
        nc.sync.dma_start(b1_sb[:], b1).then_inc(arrived, 16)
    return w1_sb, b1_sb, w2_sb, arrived, 16 * (2 * EXPERTS + (b1 is not None))


def routed_feed_forward(core, name, experts, routing, func, acc, gT=None, sT=None):
    nc, dram, ps = core.nc, core.dram, core.ps
    w1_sb, b1_sb, w2_sb, experts_in, experts_all = experts
    S = routing.slots
    with ExitStack() as ctx:
        sb = lambda n, shape, dt=F32: ctx.enter_context(nc.sbuf_tensor(f"{name}_{n}", shape, dt))
        sem = lambda n: core.semaphore(ctx, f"{name}_{n}")
        rows, rowsT = sb("rows", [P, 2, D]), sb("rowsT", [P, 2, KD, P])
        h, hT = sb("h", [P, FF]), sb("hT", [P, FB, P])
        y = sb("y", [P, 2, D])
        bias = sb("bias", [P, FB])
        if gT is not None:
            g_sb, s_sb = sb("gT", [P, KD]), sb("sT", [P, KD])
        rows_in, y_out = [sem("rows_in0"), sem("rows_in1")], [sem("y_out0"), sem("y_out1")]
        loaded, rT_mm, rT_sb, h_mm, h_sb, hT_mm, hT_sb, y_mm, y_sb, bias_in = (
            sem(n) for n in ("loaded", "rT_mm", "rT_sb", "h_mm", "h_sb", "hT_mm", "hT_sb", "y_mm", "y_sb", "bias"))
        block = core.stage(ctx)
        R_BANK, H_BANK, HT_BANK, Y_BANK = 0, 1, 3, 5

        def each_tile(eng, step):
            with eng.Fori(0, S // 2) as i:
                for u in range(2):
                    step(i * 2 + u, u)

        @block.sync
        def _(sp):
            if gT is not None:
                sp.dma_start(g_sb[:], gT).then_inc(loaded, 16)
                sp.dma_start(s_sb[:], sT).then_inc(loaded, 16)
                sp.wait_ge(loaded, 32)

            def load(s, u):
                sp.wait_ge(rT_mm, s + 1)
                sp.dma_start(rows[:, u, :], dram["scratch_rows"].rearrange("(s p) d -> p s d", p=P)[:, bass.ds(s, 1), :]
                             .rearrange("p s d -> p (s d)")).then_inc(rows_in[u], 16)

            each_tile(sp, load)

        @block.tensor
        def _(pe):
            def transpose_rows(s, u):
                pe.wait_ge(rows_in[u], (s - u) * 8 + 16)
                pe.wait_ge(rT_sb, s + 1)
                for k in range(KD):
                    mm = pe.transpose(ps[:, R_BANK, k * P:(k + 1) * P], rows[:, u, k * P:(k + 1) * P], core.ident[:])
                mm.then_inc(rT_mm, 1)

            def first(s, u):
                e = pe.value_load(routing.expert[0:1, bass.ds(s, 1)], min_val=0, max_val=EXPERTS - 1)
                pe.wait_ge(rT_sb, s + 2)
                pe.wait_ge(h_sb, s * 2 + 2)
                for c in range(2):
                    for k in range(KD):
                        mm = pe.matmul(ps[:, H_BANK + c, :], rowsT[:, u, k, :], w1_sb[:, bass.ds(e, 1), k, c * CH:(c + 1) * CH],
                                       start=(k == 0), stop=(k == KD - 1))
                    mm.then_inc(h_mm, 1)

            def turn(s, u):
                for c in range(2):
                    pe.wait_ge(h_sb, s * 2 + (c + 3))
                    for j in range(4):
                        f = 4 * c + j
                        mm = pe.transpose(ps[:, HT_BANK + c, j * P:(j + 1) * P], h[:, f * P:(f + 1) * P], core.ident[:])
                    mm.then_inc(hT_mm, 1)

            def second(s, u):
                e = pe.value_load(routing.expert[0:1, bass.ds(s, 1)], min_val=0, max_val=EXPERTS - 1)
                pe.wait_ge(hT_sb, s * 2 + 3)
                pe.wait_ge(y_sb, s + 2)
                for f in range(FB):
                    mm = pe.matmul(ps[:, Y_BANK, 0:D], hT[:, f, :], w2_sb[:, bass.ds(e, 1), f, :], start=(f == 0), stop=(f == FB - 1))
                mm.then_inc(y_mm, 1)

            pe.wait_ge(experts_in, experts_all)
            pe.sem_inc(rT_mm, 2)

            transpose_rows(0, 0)
            first(0, 0)
            transpose_rows(1, 1)
            turn(0, 0)
            with pe.Fori(0, (S - 2) // 2) as i:
                for s, u in ((i * 2 + 1, 1), (i * 2 + 2, 0)):
                    first(s, u)
                    second(s - 1, 1 - u)
                    transpose_rows(s + 1, 1 - u)
                    turn(s, u)
            first(S - 1, 1)
            second(S - 2, 0)
            turn(S - 1, 1)
            second(S - 1, 1)

        @block.vector
        def _(dve):
            if gT is not None:
                dve.wait_ge(loaded, 32)
            dve.sem_inc(rT_sb, 1)
            dve.sem_inc(h_sb, 2)

            def step(s, u):
                if b1_sb is not None:
                    e = dve.value_load(routing.expert[0:1, bass.ds(s, 1)], min_val=0, max_val=EXPERTS - 1)
                dve.wait_ge(rT_mm, s + 3)
                if gT is not None:
                    for k in range(KD):
                        ins = dve.tensor_scalar(rowsT[:, u, k, :], ps[:, R_BANK, k * P:(k + 1) * P], g_sb[:, k:k + 1], s_sb[:, k:k + 1],
                                                ALU.mult, ALU.add)
                    ins.then_inc(rT_sb, 1)
                else:
                    dve.tensor_copy(rowsT[:, u, :, :].rearrange("p k n -> p (k n)"), ps[:, R_BANK, 0:D]).then_inc(rT_sb, 1)
                if b1_sb is not None:
                    dve.wait_ge(hT_sb, s * 2 + 1)
                    dve.tensor_scalar(bias[:], b1_sb[:, bass.ds(e, 1), :].rearrange("p e f -> p (e f)"), 0.0, None, ALU.add).then_inc(bias_in, 1)
                for c in range(2):
                    dve.wait_ge(h_mm, s * 2 + (c + 1))
                    dve.tensor_copy(h[:, c * CH:(c + 1) * CH], ps[:, H_BANK + c, :]).then_inc(h_sb, 1)

            each_tile(dve, step)

        @block.scalar
        def _(act):
            act.sem_inc(y_sb, 2)
            for u in range(2):
                act.sem_inc(y_out[u], 16)
            act.sem_inc(hT_sb, 1)

            def step(s, u):
                if b1_sb is not None:
                    act.wait_ge(bias_in, s + 1)
                for c in range(2):
                    act.wait_ge(hT_mm, s * 2 + (c + 1))
                    if b1_sb is not None:
                        for j in range(4):
                            f = 4 * c + j
                            ins = act.activation(hT[:, f, :], ps[:, HT_BANK + c, j * P:(j + 1) * P], func, bias=bias[:, f:f + 1])
                    else:
                        ins = act.activation(hT[:, 4 * c:4 * c + 4, :].rearrange("p f n -> p (f n)"), ps[:, HT_BANK + c, :], func)
                    ins.then_inc(hT_sb, 1)
                act.wait_ge(y_mm, s + 1)
                act.wait_ge(y_out[u], (s - u) * 8 + 16)
                act.copy(y[:, u, :], ps[:, Y_BANK, 0:D]).then_inc(y_sb, 1)
                act.wait_ge(y_sb, s + 3)
                act.dma_start(dram["scratch_results"].rearrange("(s p) d -> p s d", p=P)[:, bass.ds(s, 1), :]
                              .rearrange("p s d -> p (s d)"), y[:, u, :]).then_inc(y_out[u], 16)

            each_tile(act, step)
            for u in range(2):
                act.wait_ge(y_out[u], 16 * (S // 2) + 16)

    with ExitStack() as ctx:
        sb = lambda n, shape, dt=F32: ctx.enter_context(nc.sbuf_tensor(f"{name}c_{n}", shape, dt))
        R = 4
        res = sb("res", [P, R, D])
        res_in, added = [core.lasting_semaphore(f"{name}_res_in{i}") for i in range(R)], core.semaphore(ctx, f"{name}_added")
        block = core.stage(ctx)

        @block.gpsimd
        def _(pool):
            for t in range(NT):
                for k in range(routing.choices):
                    n = t * routing.choices + k
                    if n >= R:
                        pool.wait_ge(added, n - R + 1)
                    pool.indirect_dma_start(res[:, n % R, :], None, dram["scratch_results"][0:S * P, :],
                                            bass.IndirectOffsetOnAxis(ap=routing.place[:, k, t:t + 1], axis=0),
                                            bounds_check=S * P - 1).then_inc(res_in[n % R], 16)

        @block.vector
        def _(dve):
            for t in range(NT):
                for k in range(routing.choices):
                    n = t * routing.choices + k
                    dve.wait_ge(res_in[n % R], 16 * (n // R + 1))
                    if k:
                        dve.wait_ge(added, n)
                    dve.scalar_tensor_tensor(acc[:, t, :], res[:, n % R, :], routing.weight[:, k, t:t + 1], acc[:, t, :],
                                             ALU.mult, ALU.add).then_inc(added, 1)


PARTS = 3
PROD = ((0, 0), (0, 1), (1, 0), (1, 1), (0, 2), (2, 0))
SR = len(PROD) * DK


def self_attention(core, acc):
    nc, dram, ps = core.nc, core.dram, core.ps
    KT = SEQ // P
    NP = BATCH * HEADS // 2
    with ExitStack() as ctx:
        sb = lambda n, shape, dt=F32: ctx.enter_context(nc.sbuf_tensor(f"sa_{n}", shape, dt))
        sem = lambda n: core.semaphore(ctx, f"sa_{n}")
        parts = dram["scratch_parts"]
        maxima = dram["scratch_max"]
        vh = sb("vh", [P, NT, HEADS, DK + 1])
        on = sb("on", [P, NT, D])

        with ExitStack() as c2:
            sb2 = lambda n, shape, dt=F32: c2.enter_context(nc.sbuf_tensor(f"sp_{n}", shape, dt))
            sem2 = lambda n: core.semaphore(c2, f"sp_{n}")
            wqkv = sb2("wqkv", [P, KD, 3 * D])
            bqk, bv = sb2("bqk", [P, 4]), sb2("bv", [P, D])
            q32 = sb2("q32", [P, 2, CH])
            r32 = sb2("r32", [P, 2, CH])
            part = [sb2(f"part{i}", [P, 2, CH], BF16) for i in range(PARTS)]
            loaded, mm_done, q_sb, chain, split, stored, v_mm, v_sb, ones = (
                sem2("loaded"), sem2("mm"), sem2("q_sb"), sem2("chain"), sem2("split"), [sem2("stored0"), sem2("stored1")], sem2("v_mm"), sem2("v_sb"), sem2("ones"))
            NQ = 4 * NCH
            block = core.stage(c2)

            @block.sync
            def _(sp):
                sp.dma_start(wqkv[:], dram["L1f_wqkv"].rearrange("(k p) d -> p k d", p=P)).then_inc(loaded, 16)
                sp.dma_start(bqk[:], dram["L1f_bqk"]).then_inc(loaded, 16)
                sp.dma_start(bv[:], bcast(dram["L1f_bv"], P)).then_inc(loaded, 16)
                for n in range(NQ):
                    j, c = n // NCH, n % NCH
                    sp.wait_ge(split, n + 1)
                    for i in range(PARTS):
                        sp.dma_start(parts[j // 2, i, (j % 2) * P:(j % 2 + 1) * P, c * CH:(c + 1) * CH], part[i][:, n % 2, :]).then_inc(stored[n % 2], 16)
                sp.wait_ge(loaded, 48)
                for u in range(2):
                    sp.wait_ge(stored[u], NQ // 2 * 48)

            @block.tensor
            def _(pe):
                pe.wait_ge(loaded, 48)
                for n in range(NQ):
                    j, c = n // NCH, n % NCH
                    if n >= 4:
                        pe.wait_ge(q_sb, n - 3)
                    for k in range(KD):
                        mm = pe.matmul(ps[:, n % 4, :], wqkv[:, k, j * P:(j + 1) * P], core.xnT[:, k, c * CH:(c + 1) * CH],
                                       start=(k == 0), stop=(k == KD - 1))
                    mm.then_inc(mm_done, 1)
                for t in range(NT):
                    if t >= 4:
                        pe.wait_ge(v_sb, t - 3)
                    for k in range(KD):
                        mm = pe.matmul(ps[:, 4 + t % 4, 0:D], core.xnT[:, k, t * P:(t + 1) * P], wqkv[:, k, 2 * D:3 * D],
                                       start=(k == 0), stop=(k == KD - 1))
                    mm.then_inc(v_mm, 1)

            @block.gpsimd
            def _(pool):
                pool.memset(vh[:, :, :, DK:DK + 1], 1.0).then_inc(ones, 1)

            @block.scalar
            def _(act):
                act.wait_ge(loaded, 48)
                for n in range(NQ):
                    j = n // NCH
                    act.wait_ge(mm_done, n + 1)
                    if n >= 2:
                        act.wait_ge(split, n - 1)
                    act.activation(q32[:, n % 2, :], ps[:, n % 4, :], ACT.Identity, bias=bqk[:, j:j + 1]).then_inc(q_sb, 1)

            @block.vector
            def _(dve):
                count = [0]

                def link(ins):
                    count[0] += 1
                    ins.then_inc(chain, 1)
                    dve.wait_ge(chain, count[0])

                for n in range(NQ):
                    u = n % 2
                    dve.wait_ge(q_sb, n + 1)
                    if n >= 2:
                        dve.wait_ge(stored[u], 48 * (n // 2))
                    link(dve.tensor_copy(part[0][:, u, :], q32[:, u, :]))
                    link(dve.tensor_tensor(r32[:, u, :], q32[:, u, :], part[0][:, u, :], ALU.subtract))
                    link(dve.tensor_copy(part[1][:, u, :], r32[:, u, :]))
                    dve.tensor_tensor(part[2][:, u, :], r32[:, u, :], part[1][:, u, :], ALU.subtract).then_inc(split, 1)
                dve.wait_ge(loaded, 48)
                for t in range(NT):
                    dve.wait_ge(v_mm, t + 1)
                    dve.tensor_tensor(vh[:, t, :, 0:DK], ps[:, 4 + t % 4, 0:D].rearrange("p (h d) -> p h d", d=DK),
                                      bv[:].rearrange("p (h d) -> p h d", d=DK), ALU.add).then_inc(v_sb, 1)

        with ExitStack() as c3:
            sb3 = lambda n, shape, dt=F32: c3.enter_context(nc.sbuf_tensor(f"sh_{n}", shape, dt))
            sem3 = lambda n: core.semaphore(c3, f"sh_{n}")
            qs = [sb3(f"qs{u}", [SR + PARTS, 2, SEQ], BF16) for u in range(2)]
            ks = [sb3(f"ks{u}", [SR + PARTS, 2, SEQ], BF16) for u in range(2)]
            mhalf, m32 = sb3("mhalf", [P, 2, 2 * KT]), sb3("m32", [P, 2 * KT])
            mpart = [sb3(f"mpart{i}", [P, 2 * KT]) for i in range(PARTS)]
            mbf = [sb3(f"mbf{i}", [P, 2 * KT], BF16) for i in range(2)]
            mT = sb3("mT", [2 * KT, PARTS, P], BF16)
            pT = sb3("pT", [P, 4, 2, CH])
            oT_sb_, rs = sb3("oT", [P, CH]), sb3("rs", [P, 4, 4])
            stack_in = [sem3("stack_in0"), sem3("stack_in1")]
            max_in, max_out, ones_in = [sem3("max_in0"), sem3("max_in1")], sem3("max_out"), sem3("ones_in")
            a_mm, a_max, chain, m_split, mT_mm, mT_sb, b_mm, exp_done, pv_mm, oT_done, on_mm, on_done, stack_free = (
                sem3(x) for x in ("a_mm", "a_max", "chain", "m_split", "mT_mm", "mT_sb", "b_mm", "exp", "pv_mm", "oT", "on_mm", "on", "stack_free"))
            block = core.stage(c3)
            A_BANK, B_BANK, O_BANK, T_BANK = 0, 2, 6, 7
            NA = 2 * KT * 2

            @block.sync
            def _(sp):
                def load_stack(s, u):
                    b, hp = s // (HEADS // 2), s % (HEADS // 2)
                    rows = lambda w_, i: parts[w_, i, hp * 2 * DK:(hp + 1) * 2 * DK, b * SEQ:(b + 1) * SEQ].rearrange("(h p) n -> p h n", p=DK)
                    if s >= 2:
                        sp.wait_ge(stack_free, s - 1)
                    for j, (i, k) in enumerate(PROD):
                        sp.dma_start(qs[u][j * DK:(j + 1) * DK, :, :], rows(0, i)).then_inc(stack_in[u], 16)
                        sp.dma_start(ks[u][j * DK:(j + 1) * DK, :, :], rows(1, k)).then_inc(stack_in[u], 16)

                load_stack(0, 0)
                for s in range(NP):
                    u = s % 2
                    if s + 1 < NP:
                        load_stack(s + 1, 1 - u)
                    sp.wait_ge(mT_sb, s + 1)
                    sp.dma_start(maxima[:, s].rearrange("i h (t n) -> (h t) i n", n=P), mT[:]).then_inc(max_out, 16)
                    sp.wait_ge(max_out, 16 * (s + 1))
                    sp.dma_start(qs[u][SR:SR + PARTS, :, :], maxima[:, s]).then_inc(max_in[u], 16)

            @block.gpsimd
            def _(pool):
                for u in range(2):
                    pool.memset(ks[u][SR:SR + PARTS, :, :], 1.0).then_inc(ones_in, 1)

            def first_pass(pe, s, c):
                u, h, t, half = s % 2, c // (2 * KT), c // 2 % KT, c % 2
                n = s * NA + c
                if n >= 2:
                    pe.wait_ge(a_max, n - 1)
                pe.matmul(ps[:, A_BANK + n % 2, :], qs[u][0:SR, h, t * P:(t + 1) * P], ks[u][0:SR, h, half * CH:(half + 1) * CH],
                          start=True, stop=True).then_inc(a_mm, 1)

            @block.tensor
            def _(pe):
                pe.wait_ge(ones_in, 2)
                pe.wait_ge(stack_in[0], 16 * 2 * len(PROD))
                for c in range(NA):
                    first_pass(pe, 0, c)
                for s in range(NP):
                    u = s % 2
                    pe.wait_ge(m_split, s + 1)
                    if s:
                        pe.wait_ge(on_done, s)
                    for i in range(PARTS):
                        mm = pe.transpose(ps[0:2 * KT, T_BANK, i * P:(i + 1) * P], mpart[i][:], core.ident[:])
                    mm.then_inc(mT_mm, 1)
                    pe.wait_ge(max_in[u], 16 * (s // 2 + 1))
                    if s + 1 < NP:
                        pe.wait_ge(stack_in[1 - u], 16 * 2 * len(PROD) * ((s + 1) // 2 + 1))

                    def weighted(k):
                        pe.wait_ge(exp_done, s * 2 * KT + 2 * k + 2)
                        if k == 0 and s:
                            pe.wait_ge(oT_done, s)
                        b = s // (HEADS // 2)
                        for h in range(2):
                            head = 2 * (s % (HEADS // 2)) + h
                            for half in range(2):
                                g = 2 * h + half
                                mm = pe.matmul(ps[32 * g:32 * g + DK + 1, O_BANK, :], vh[:, b * KT + k, head, :],
                                               pT[:, (2 * k + h) % 4, half, :], start=(k == 0), stop=(k == KT - 1))
                        mm.then_inc(pv_mm, 1)

                    for k in range(KT):
                        for h in range(2):
                            n = s * 2 * KT + 2 * k + h
                            if n >= 2:
                                pe.wait_ge(exp_done, n - 1)
                            for half in range(2):
                                mm = pe.matmul(ps[:, B_BANK + 2 * (n % 2) + half, :], ks[u][:, h, k * P:(k + 1) * P],
                                               qs[u][:, h, half * CH:(half + 1) * CH], start=True, stop=True)
                            mm.then_inc(b_mm, 1)
                            if s + 1 < NP:
                                for c in range(2):
                                    first_pass(pe, s + 1, (2 * k + h) * 2 + c)
                        if k:
                            weighted(k - 1)
                    weighted(KT - 1)
                    pe.wait_ge(pv_mm, (s + 1) * KT)
                    pe.sem_inc(stack_free, 1)
                    pe.wait_ge(oT_done, s + 1)
                    for j in range(4):
                        mm = pe.transpose(ps[:, T_BANK, j * P:(j + 1) * P], oT_sb_[:, j * P:(j + 1) * P], core.ident[:])
                    mm.then_inc(on_mm, 1)

            @block.scalar
            def _(act):
                for s in range(NP):
                    for n in range(s * 2 * KT, (s + 1) * 2 * KT):
                        act.wait_ge(b_mm, n + 1)
                        if n >= 4:
                            act.wait_ge(pv_mm, n // 2 - 1)
                        act.activation(pT[:, n % 4, :, :], ps[:, B_BANK + 2 * (n % 2):B_BANK + 2 * (n % 2) + 2, :], ACT.Exp,
                                       scale=DK ** -0.5).then_inc(exp_done, 1)
                    act.wait_ge(pv_mm, (s + 1) * KT)
                    act.copy(oT_sb_[:], ps[:, O_BANK, :]).then_inc(oT_done, 1)

            @block.vector
            def _(dve):
                count = [0]

                def link(ins):
                    count[0] += 1
                    ins.then_inc(chain, 1)
                    dve.wait_ge(chain, count[0])

                def maxima_of(s):
                    for c in range(NA):
                        n = s * NA + c
                        h, t, half = c // (2 * KT), c // 2 % KT, c % 2
                        dve.wait_ge(a_mm, n + 1)
                        dve.tensor_reduce(mhalf[:, half, h * KT + t:h * KT + t + 1], ps[:, A_BANK + n % 2, :], AX, ALU.max).then_inc(a_max, 1)
                    dve.wait_ge(a_max, (s + 1) * NA)
                    link(dve.tensor_tensor(m32[:], mhalf[:, 0, :], mhalf[:, 1, :], ALU.max))
                    link(dve.tensor_scalar(m32[:], m32[:], -1.0, None, ALU.mult))
                    link(dve.tensor_copy(mbf[0][:], m32[:]))
                    link(dve.tensor_copy(mpart[0][:], mbf[0][:]))
                    link(dve.tensor_tensor(m32[:], m32[:], mpart[0][:], ALU.subtract))
                    link(dve.tensor_copy(mbf[1][:], m32[:]))
                    link(dve.tensor_copy(mpart[1][:], mbf[1][:]))
                    dve.tensor_tensor(mpart[2][:], m32[:], mpart[1][:], ALU.subtract).then_inc(m_split, 1)

                def maxima_rows(s):
                    dve.wait_ge(mT_mm, s + 1)
                    if s:
                        dve.wait_ge(max_out, 16 * s)
                    dve.tensor_copy(mT[:], ps[0:2 * KT, T_BANK, 0:PARTS * P].rearrange("p (i n) -> p i n", n=P)).then_inc(mT_sb, 1)

                def finish(s):
                    b, hp = s // (HEADS // 2), s % (HEADS // 2)
                    dve.wait_ge(on_mm, s + 1)
                    o = ps[:, T_BANK, :].rearrange("p (j g d) -> p j g d", g=4, d=32)
                    link(dve.reciprocal(rs[:], o[:, :, :, DK]))
                    for h in range(2):
                        dst = on[:, b * KT:(b + 1) * KT, (2 * hp + h) * DK:(2 * hp + h + 1) * DK].rearrange("p (g j) d -> p j g d", g=2)
                        ins = dve.tensor_tensor(dst, o[:, :, 2 * h:2 * h + 2, 0:DK],
                                                rs[:, :, 2 * h:2 * h + 2].unsqueeze(3).broadcast_to([P, 4, 2, DK]), ALU.mult)
                    ins.then_inc(on_done, 1)

                maxima_of(0)
                maxima_rows(0)
                for s in range(NP):
                    if s + 1 < NP:
                        maxima_of(s + 1)
                    finish(s)
                    if s + 1 < NP:
                        maxima_rows(s + 1)
        transpose_tokens(core, "sat", on, core.xnT)
        token_projection(core, "sao", dram["L1f_wo"], dram["L1f_bo"], acc)


def token_projection(core, name, w, b, acc):
    nc, ps = core.nc, core.ps
    with ExitStack() as ctx:
        w_sb = ctx.enter_context(nc.sbuf_tensor(f"{name}_w", [P, KD, D], F32))
        b_sb = ctx.enter_context(nc.sbuf_tensor(f"{name}_b", [P, D], F32))
        loaded, bias_done, y_mm, y_sb = (core.semaphore(ctx, f"{name}_{n}") for n in ("loaded", "bias", "y_mm", "y_sb"))
        block = core.stage(ctx)

        @block.sync
        def _(sp):
            sp.dma_start(w_sb[:], w.rearrange("(k p) d -> p k d", p=P)).then_inc(loaded, 16)
            sp.dma_start(b_sb[:], bcast(b, P)).then_inc(loaded, 16)
            sp.wait_ge(loaded, 32)

        @block.tensor
        def _(pe):
            pe.wait_ge(loaded, 32)
            for t in range(NT):
                if t >= 4:
                    pe.wait_ge(y_sb, t - 3)
                for k in range(KD):
                    mm = pe.matmul(ps[:, t % 4, 0:D], core.xnT[:, k, t * P:(t + 1) * P], w_sb[:, k, :], start=(k == 0), stop=(k == KD - 1))
                mm.then_inc(y_mm, 1)

        @block.vector
        def _(dve):
            dve.wait_ge(loaded, 32)
            dve.tensor_tensor(acc[:], acc[:], b_sb[:].unsqueeze(1).broadcast_to([P, NT, D]), ALU.add).then_inc(bias_done, 1)
            dve.wait_ge(bias_done, 1)
            for t in range(NT):
                dve.wait_ge(y_mm, t + 1)
                dve.tensor_tensor(acc[:, t, :], acc[:, t, :], ps[:, t % 4, 0:D], ALU.add).then_inc(y_sb, 1)


def add_to(core, name, dst, src, row=None):
    nc = core.nc
    with ExitStack() as ctx:
        done = core.semaphore(ctx, f"{name}_done")
        if row is not None:
            row_sb = ctx.enter_context(nc.sbuf_tensor(f"{name}_row", [P, D], F32))
            src = row_sb[:].unsqueeze(1).broadcast_to([P, NT, D])
        loaded = core.semaphore(ctx, f"{name}_loaded")
        block = core.stage(ctx)

        @block.sync
        def _(sp):
            if row is not None:
                sp.dma_start(row_sb[:], bcast(row, P)).then_inc(loaded, 16)
                sp.wait_ge(loaded, 16)

        @block.vector
        def _(dve):
            if row is not None:
                dve.wait_ge(loaded, 16)
            dve.tensor_tensor(dst[:], dst[:], src if row is not None else src[:], ALU.add).then_inc(done, 1)


def store_output(core):
    nc = core.nc
    with ExitStack() as ctx:
        stored = core.semaphore(ctx, "out_stored")
        block = core.stage(ctx)

        @block.sync
        def _(sp):
            sp.dma_start(core.dram["out"].rearrange("b (t p) d -> p (b t) d", p=P), core.x[:]).then_inc(stored, 16)
            sp.wait_ge(stored, 16)


def program(nc, dram, stages=range(1, 9)):
    with ExitStack() as ctx:
        core = Core(nc, ctx, dram)
        x, xn, xnT = core.x, core.xn, core.xnT
        load_inputs(core)
        if 1 in stages:
            layer_norm(core, "n0", x, xn, xnT)
            query_softmax_attention(core)
        if 2 in stages:
            with nc.sbuf_tensor("xmax", [P, 1], F32) as xmax:
                layer_norm(core, "n1", x, xn, absmax=xmax)
                quantised_ffn(core, xmax)
        if 3 in stages:
            layer_norm(core, "n2", x, xn, xnT)
            headed_cross_attention(core, "a1", dram["L1_WqT"], dram["L1_WkT"], dram["L1_WvT"], dram["L1_WoT"], xn, bias=dram["bias"])
            with nc.sbuf_tensor("l1_h", [P, NT, D], F32) as h:
                layer_norm(core, "n3", xn, h, xnT, gainT=dram["L1_g1"], shiftT=dram["L1_be1"])
            add_to(core, "b2", xn, None, row=dram["L1_b2"])
            feed_forward(core, "f1", 1, dram["L1_W1T"], dram["L1_b1"], dram["L1_W2T"], ACT.Gelu, xn)
            layer_norm(core, "n4", xn, xn, gain=dram["L1_g2"], shift=dram["L1_be2"])
            add_to(core, "r1", x, xn)
        if 4 in stages:
            layer_norm(core, "n5", x, xn)
            with nc.sbuf_tensor("l1f_h", [P, NT, D], F32) as h:
                layer_norm(core, "n6", xn, h, xnT, gainT=dram["L1f_ln1_g"], shiftT=dram["L1f_ln1_b"])
            self_attention(core, xn)
            with ExitStack() as layer:
                experts = load_experts(core, layer, "e1", dram["L1f_W1"], dram["L1f_b1"], dram["L1f_W2"])
                routing = Routing(core, layer, "r1", 2)
                add_to(core, "r2", x, xn)
                layer_norm(core, "n7", xn, xn, xnT, gainT=dram["L1f_ln2_g"], shiftT=dram["L1f_ln2_b"])
                expert_weights(core, "g1", "top2", dram["L1f_gate_w"], dram["L1f_gate_b"], None, dram["L1f_b2"], x, routing)
                routed_feed_forward(core, "m1", experts, routing, ACT.Relu, x, dram["L1f_ln2_g"], dram["L1f_ln2_b"])
        if 5 in stages:
            layer_norm(core, "n8", x, xn, xnT)
            plain_cross_attention(core)
        if 6 in stages:
            layer_norm(core, "n9", x, xn, xnT)
            with nc.sbuf_tensor("ew2", [P, EXPERTS, NT], F32) as ew:
                expert_weights(core, "g2", "threshold", dram["L2_Wg"], dram["L2_bg"], ew, dram["L2_b2"], x)
                feed_forward(core, "m2", EXPERTS, dram["L2_W1"], dram["L2_b1"], dram["L2_W2"], ACT.Relu, x, ew)
        if 7 in stages:
            layer_norm(core, "n10", x, xn, xnT)
            add_to(core, "bo3", x, None, row=dram["L3_bo"])
            headed_cross_attention(core, "a3", dram["L3_wq"], dram["L3_wk"], dram["L3_wv"], dram["L3_wo"], x, mask=dram["mask_bf"],
                                   bq=dram["L3_bq"], bk=dram["L3_bk"], bv=dram["L3_bv"])
        if 8 in stages:
            with ExitStack() as layer:
                experts = load_experts(core, layer, "e3", dram["L3_W1"], None, dram["L3_W2"])
                routing = Routing(core, layer, "r3", 1)
                layer_norm(core, "n11", x, xn, xnT)
                expert_weights(core, "g3", "top1", dram["L3_Wr"], dram["L3_br"], None, None, x, routing)
                routed_feed_forward(core, "m3", experts, routing, ACT.Gelu, x)
        store_output(core)



def laid_out(inputs):
    import numpy as np

    g = lambda n: np.asarray(inputs[n])
    t = lambda n: np.ascontiguousarray(np.swapaxes(np.asarray(inputs[n]), -1, -2))
    a = {}
    a["x"] = g("x")
    a["ctx"] = g("ctx_1024")
    a["ctxT"] = np.ascontiguousarray(g("ctx_1024").reshape(BATCH * KEYS, D).T)
    a["bias"] = np.ascontiguousarray(g("fside_Bx16xSxS2_0").reshape(BATCH, HEADS, SEQ // P, P, KEYS).transpose(0, 2, 3, 1, 4)
                                     .reshape(NT, P, HEADS, KEYS))
    a["mask_ik"] = g("mask_Bx1xS2_ik0").reshape(BATCH, KEYS)
    a["mask_bf"] = g("mask_Bx1xSxS2_bf0").reshape(TOK, KEYS)
    for n in ("Wk", "Wv", "Wo"):
        a[f"L0_{n}T"] = t(f"L0_xattn_{n}")
    a["L0_Wq"] = g("L0_xattn_Wq")
    for n in ("bq", "bk", "bv", "bo"):
        a[f"L0_{n}"] = g(f"L0_xattn_{n}")
    a["L0_WinT"], a["L0_Wout"] = t("L0_ffn_W_in"), g("L0_ffn_W_out")
    a["L0_bin"], a["L0_bout"] = g("L0_ffn_b_in"), g("L0_ffn_b_out")
    for n in ("Wq", "Wk", "Wv", "Wo"):
        a[f"L1_{n}T"] = t(f"L1_xattn_{n}")
    a["L1_W1T"], a["L1_W2T"] = t("L1_xattn_W1")[None], t("L1_xattn_W2")[None]
    a["L1_b1"] = g("L1_xattn_b1")[None]
    for n in ("b2", "g1", "be1", "g2", "be2"):
        a[f"L1_{n}"] = g(f"L1_xattn_{n}")
    for n in ("ln1_g", "ln1_b", "ln2_g", "ln2_b", "gate_w", "gate_b", "W1", "b1", "W2", "b2"):
        a[f"L1f_{n}"] = g(f"L1_ffn_{n}")
    a["L1f_wqkv"], a["L1f_bqkv"], a["L1f_wo"], a["L1f_bo"] = (g(f"L1_ffn_{n}") for n in ("w_qkv", "b_qkv", "w_o", "b_o"))
    for n in ("Wg", "bg", "W1", "b1", "W2", "b2"):
        a[f"L2_{n}"] = g(f"L2_ffn_{n}")
    for n in ("wq", "wk", "wv", "wo", "bq", "bk", "bv", "bo"):
        a[f"L3_{n}"] = g(f"L3_xattn_{n}")
    for n in ("Wr", "br", "W1", "W2"):
        a[f"L3_{n}"] = g(f"L3_ffn_{n}")
    a["L1f_bqk"], a["L1f_bv"] = a["L1f_bqkv"][:2 * D], a.pop("L1f_bqkv")[2 * D:]
    for n in ("L0_bq", "L0_bk", "L0_bv", "L0_bin", "L1_g1", "L1_be1", "L1f_ln1_g", "L1f_ln1_b", "L1f_ln2_g", "L1f_ln2_b",
              "L1f_bqk", "L3_bq", "L3_bk"):
        a[n] = a[n].reshape(-1, P).T
    for n in ("L1_b1", "L1f_b1", "L2_b1"):
        a[n] = a[n].reshape(-1, FB, P).transpose(2, 0, 1)
    return {k: np.ascontiguousarray(v) for k, v in a.items()}


def constants():
    import numpy as np
    return {
        "identity": np.eye(P, dtype=np.float32),
        "head_of": (np.arange(P)[:, None] // DK == np.arange(8)[None]).astype(np.float32),
        "before": np.triu(np.ones((P, P), np.float32), 1),
        "slot_ids": np.arange(2 * NT + EXPERTS, dtype=np.float32),
        "rank": np.arange(EXPERTS, 0, -1).astype(np.float32),
    }


def scratch(nc, dram):
    dram["scratch_rows"] = nc.dram_tensor("scratch_rows", ((2 * NT + EXPERTS) * P, D), F32).ap()
    dram["scratch_results"] = nc.dram_tensor("scratch_results", ((2 * NT + EXPERTS) * P, D), F32).ap()
    dram["scratch_parts"] = nc.dram_tensor("scratch_parts", (2, PARTS, D, TOK), BF16).ap()
    dram["scratch_max"] = nc.dram_tensor("scratch_max", (PARTS, BATCH * HEADS // 2, 2, SEQ), BF16).ap()


def kernel(**inputs):
    import concourse.bacc as _bacc
    from concourse import mybir as _mybir
    from concourse.bass_utils import run_bass_kernel_spmd as _run

    nc = _bacc.Bacc("TRN2", target_bir_lowering=False, num_devices=1)
    arrays = {**laid_out(inputs), **constants()}
    dram = {n: nc.dram_tensor(n, a.shape, _mybir.dt.from_np(a.dtype), kind="ExternalInput").ap() for n, a in arrays.items()}
    dram["out"] = nc.dram_tensor("out", (BATCH, SEQ, D), F32, kind="ExternalOutput").ap()
    scratch(nc, dram)
    program(nc, dram)
    r = _run(nc, [arrays], core_ids=[0])
    return r.results[0]["out"]
```

```python
from contextlib import ExitStack

import concourse.bass as bass
from concourse import mybir

ALU = mybir.AluOpType
ACT = mybir.ActivationFunctionType
F32 = mybir.dt.float32
BF16 = mybir.dt.bfloat16
I32 = mybir.dt.int32
U8 = mybir.dt.uint8
AX = mybir.AxisListType.X

P = 128
BATCH, SEQ, D = 2, 1024, 256
TOK = BATCH * SEQ
NT = TOK // P
KD = D // P
KEYS = 77
MAIN = 64
REST = KEYS - MAIN
HEADS, DK = 16, 16
FF = 1024
FB = FF // P
EXPERTS = 8
CH = 512
NCH = TOK // CH
ROW = D + EXPERTS + 1
PLACES = (EXPERTS * NT + 2) * P
NOWHERE = 1e6
SEND_AHEAD = 3
EPS = 1e-5
NEG = -1e9
SEM_RANGES = (range(130, 175), range(175, 220))
LONG_SEMS = 220
ROUND = 12582912.0


class Core:

    def __init__(self, nc, ctx, dram):
        self.nc, self.dram = nc, dram
        sb = lambda name, shape, dt=F32: ctx.enter_context(nc.sbuf_tensor(name, shape, dt))
        self.x = sb("x_resid", [P, NT, D])
        self.rows = sb("x_norm", [P, NT, ROW])
        self.xn = self.rows[:, :, 0:D]
        self.xnT = sb("x_normT", [P, KD, TOK])
        self.ctxT = sb("ctxT_sb", [P, KD, BATCH * KEYS])
        self.ident = sb("ident", [P, P])
        self.ps = ctx.enter_context(nc.psum_tensor("banks", [P, 8, CH], F32))
        self.side, self.taken, self.long = 0, 0, LONG_SEMS

    def lasting_semaphore(self, name):
        self.long += 1
        return self.nc.alloc_semaphore(name=name, num=self.long - 1)

    def semaphore(self, ctx, name):
        s = self.nc.alloc_semaphore(name=name, num=SEM_RANGES[self.side][self.taken])
        ctx.callback(self.nc.release_semaphore, s)
        self.taken += 1
        return s

    def stage(self, ctx):
        self.side, self.taken = 1 - self.side, 0
        self.nc.gpsimd.sem_clear(SEM_RANGES[self.side])
        return ctx.enter_context(self.nc.Block())


def bcast(ap, n):
    return ap.unsqueeze(0).broadcast_to([n] + list(ap.shape))


def load_inputs(core):
    nc, dram = core.nc, core.dram
    with ExitStack() as ctx:
        loaded = core.semaphore(ctx, "in_loaded")
        block = core.stage(ctx)

        @block.sync
        def _(sp):
            sp.dma_start(core.x[:], dram["x"].rearrange("b (t p) d -> p (b t) d", p=P)).then_inc(loaded, 16)
            sp.dma_start(core.ident[:], dram["identity"]).then_inc(loaded, 16)
            sp.dma_start(core.ctxT[:], dram["ctxT"].rearrange("(k p) n -> p k n", p=P)).then_inc(loaded, 16)
            sp.wait_ge(loaded, 48)


class Loads:

    def __init__(self, core, ctx, name):
        self.core, self.ctx, self.name = core, ctx, name
        self.arrived, self.total = core.lasting_semaphore(f"{name}_in"), 0
        self.at = {}

    def load(self, n, shape, source, dt=F32):
        self.at[n] = self.ctx.enter_context(self.core.nc.sbuf_tensor(f"{self.name}_{n}", shape, dt))
        self.core.nc.sync.dma_start(self.at[n][:], source).then_inc(self.arrived, 16)
        self.total += 16

    def wait(self, eng):
        eng.wait_ge(self.arrived, self.total)

    def __getitem__(self, n):
        return self.at[n]


def load_affine(core, ctx, name, gain, shift):
    loads = Loads(core, ctx, name)
    loads.load("gain", [P, KD], gain)
    loads.load("shift", [P, KD], shift)
    return loads


def layer_norm(core, name, src, dst, dstT=None, affineT=None, gain=None, shift=None, absmax=None):
    nc = core.nc
    with ExitStack() as ctx:
        sb = lambda n, shape, dt=F32: ctx.enter_context(nc.sbuf_tensor(f"{name}_{n}", shape, dt))
        sem = lambda n: core.semaphore(ctx, f"{name}_{n}")
        stats, moments = sb("stats", [P, NT, 6]), sb("moments", [P, NT, 2])
        std, rstd = sb("std", [P, NT]), sb("rstd", [P, NT])
        stats_done, moments_done, std_done, rstd_done = sem("stats"), sem("moments"), sem("std"), sem("rstd")
        tile_normed, transposed, evacuated, gains_in = sem("normed"), sem("transposed"), sem("evac"), sem("gains")
        affine_done = sem("affine")
        if affineT is not None:
            gT, sT = affineT["gain"], affineT["shift"]
        if gain is not None:
            g_bc, s_bc = sb("gain", [P, D]), sb("shift", [P, D])
        block = core.stage(ctx)

        @block.sync
        def _(sp):
            if gain is not None:
                sp.dma_start(g_bc[:], bcast(gain, P)).then_inc(gains_in, 16)
                sp.dma_start(s_bc[:], bcast(shift, P)).then_inc(gains_in, 16)
                sp.wait_ge(gains_in, 32)

        def evacuate(eng, is_act, g, k):
            out, in_ = dstT[:, k, g * CH:(g + 1) * CH], core.ps[:, 2 * g + k, :]
            if affineT is not None:
                if is_act:
                    return eng.activation(out, in_, ACT.Identity, bias=sT[:, k:k + 1], scale=gT[:, k:k + 1])
                return eng.tensor_scalar(out, in_, gT[:, k:k + 1], sT[:, k:k + 1], ALU.mult, ALU.add)
            return eng.copy(out, in_) if is_act else eng.tensor_copy(out, in_)

        @block.vector
        def _(dve):
            for t in range(NT):
                dve.bn_stats(stats[:, t, :], src[:, t, :]).then_inc(stats_done, 1)
            for t in range(NT):
                dve.wait_ge(stats_done, t + 1)
                dve.bn_aggr(moments[:, t, :], stats[:, t, :]).then_inc(moments_done, 1)
            dve.wait_ge(moments_done, NT)
            dve.tensor_scalar(moments[:, :, 1], moments[:, :, 1], EPS, None, ALU.add).then_inc(moments_done, 1)
            dve.wait_ge(std_done, 1)
            dve.reciprocal(rstd[:], std[:]).then_inc(rstd_done, 1)
            dve.wait_ge(rstd_done, 1)
            for t in range(NT):
                dve.tensor_scalar(dst[:, t, :], src[:, t, :], moments[:, t, 0:1], rstd[:, t:t + 1],
                                  ALU.subtract, ALU.mult).then_inc(tile_normed, 1)
            if gain is not None:
                dve.wait_ge(gains_in, 32)
                dve.wait_ge(tile_normed, NT)
                dve.tensor_tensor(dst[:], dst[:], g_bc[:].unsqueeze(1).broadcast_to([P, NT, D]), ALU.mult).then_inc(affine_done, 1)
                dve.wait_ge(affine_done, 1)
                dve.tensor_tensor(dst[:], dst[:], s_bc[:].unsqueeze(1).broadcast_to([P, NT, D]), ALU.add).then_inc(affine_done, 1)
            if absmax is not None:
                dve.wait_ge(tile_normed, NT)
                dve.tensor_reduce(absmax[:, 0:1], dst[:], mybir.AxisListType.XY, ALU.max, apply_absolute_value=True).then_inc(affine_done, 1)
            if dstT is not None:
                if affineT is not None:
                    affineT.wait(dve)
                for g in range(NCH):
                    dve.wait_ge(transposed, 2 * g + 2)
                    evacuate(dve, False, g, 1).then_inc(evacuated, 1)

        @block.scalar
        def _(act):
            act.wait_ge(moments_done, NT + 1)
            act.activation(std[:], moments[:, :, 1], ACT.Sqrt).then_inc(std_done, 1)
            if dstT is not None:
                if affineT is not None:
                    affineT.wait(act)
                for g in range(NCH):
                    act.wait_ge(transposed, 2 * g + 1)
                    evacuate(act, True, g, 0).then_inc(evacuated, 1)

        if dstT is not None:
            @block.tensor
            def _(pe):
                for g in range(NCH):
                    pe.wait_ge(tile_normed, 4 * g + 4)
                    for k in range(KD):
                        for j in range(4):
                            mm = pe.transpose(core.ps[:, 2 * g + k, j * P:(j + 1) * P],
                                              dst[:, 4 * g + j, k * P:(k + 1) * P], core.ident[:])
                        mm.then_inc(transposed, 1)


def transpose_tokens(core, name, src, dstT):
    nc = core.nc
    with ExitStack() as ctx:
        transposed = core.semaphore(ctx, f"{name}_transposed")
        evacuated = core.semaphore(ctx, f"{name}_evac")
        block = core.stage(ctx)

        @block.tensor
        def _(pe):
            for g in range(NCH):
                for k in range(KD):
                    for j in range(4):
                        mm = pe.transpose(core.ps[:, 2 * g + k, j * P:(j + 1) * P],
                                          src[:, 4 * g + j, k * P:(k + 1) * P], core.ident[:])
                    mm.then_inc(transposed, 1)

        @block.vector
        def _(dve):
            for g in range(NCH):
                dve.wait_ge(transposed, 2 * g + 2)
                dve.tensor_copy(dstT[:, 1, g * CH:(g + 1) * CH], core.ps[:, 2 * g + 1, :]).then_inc(evacuated, 1)

        @block.scalar
        def _(act):
            for g in range(NCH):
                act.wait_ge(transposed, 2 * g + 1)
                act.copy(dstT[:, 0, g * CH:(g + 1) * CH], core.ps[:, 2 * g, :]).then_inc(evacuated, 1)


def query_softmax_attention(core):
    nc, dram, ps = core.nc, core.dram, core.ps
    W = BATCH * KEYS
    SCALE = 64 ** -0.5
    with ExitStack() as ctx:
        sb = lambda n, shape, dt=F32: ctx.enter_context(nc.sbuf_tensor(f"a0_{n}", shape, dt))
        sem = lambda n: core.semaphore(ctx, f"a0_{n}")
        wkT, wvT = sb("wkT", [P, KD, FF]), sb("wvT", [P, KD, FF])
        wq, woT = sb("wq", [P, FB, D]), sb("woT", [P, FB, D])
        bq, bk, bv = sb("bq", [P, FB]), sb("bk", [P, FB]), sb("bv", [P, FB])
        bo = sb("bo", [P, D])
        kT, vT = sb("kT", [P, FB, W]), sb("vT", [P, FB, W])
        gT = sb("gT", [P, KD, W])
        cT = sb("cT", [KEYS, BATCH])
        vo = sb("vo", [KEYS, BATCH, D])
        ET = sb("ET", [KEYS, BATCH, SEQ])
        mx, tmp, nb = sb("mx", [KEYS, BATCH]), sb("tmp", [KEYS, BATCH]), sb("nb", [KEYS, BATCH])
        sums, rs = sb("sums", [KEYS, BATCH]), sb("rs", [KEYS, BATCH])
        loaded, kv_mm, k_sb, v_sb, g_mm, g_sb = sem("loaded"), sem("kv_mm"), sem("k_sb"), sem("v_sb"), sem("g_mm"), sem("g_sb")
        s_mm, chain, bias_ready, exp_done, v_ready, y_mm, y_sb = (
            sem("s_mm"), sem("chain"), sem("bias"), sem("exp"), sem("v"), sem("y_mm"), sem("y_sb"))
        block = core.stage(ctx)

        @block.sync
        def _(sp):
            for dst, key, pat in ((wkT, "L0_WkT", "(k p) f -> p k f"), (wvT, "L0_WvT", "(k p) f -> p k f"),
                                  (wq, "L0_Wq", "(f p) d -> p f d"), (woT, "L0_WoT", "(f p) d -> p f d")):
                sp.dma_start(dst[:], dram[key].rearrange(pat, p=P)).then_inc(loaded, 16)
            for dst, key in ((bq, "L0_bq"), (bk, "L0_bk"), (bv, "L0_bv")):
                sp.dma_start(dst[:], dram[key]).then_inc(loaded, 16)
            sp.dma_start(bo[:], bcast(dram["L0_bo"], P)).then_inc(loaded, 16)
            sp.wait_ge(loaded, 128)

        @block.tensor
        def _(pe):
            pe.wait_ge(loaded, 128)
            for i, w in enumerate((wkT, wvT)):
                for f in range(FB):
                    for k in range(KD):
                        mm = pe.matmul(ps[:, 4 * i + f // 2, (f % 2) * W:(f % 2 + 1) * W], w[:, k, f * P:(f + 1) * P],
                                       core.ctxT[:, k, :], start=(k == 0), stop=(k == KD - 1))
                mm.then_inc(kv_mm, 1)
            pe.wait_ge(k_sb, FB // 2)
            for m in range(KD):
                for f in range(FB):
                    mm = pe.matmul(ps[:, m, 0:W], wq[:, f, m * P:(m + 1) * P], kT[:, f, :], start=(f == 0), stop=(f == FB - 1))
            mm.then_inc(g_mm, 1)
            for b in range(BATCH):
                for f in range(FB):
                    mm = pe.matmul(ps[0:KEYS, 2 + b, 0:1], kT[:, f, b * KEYS:(b + 1) * KEYS], bq[:, f:f + 1],
                                   start=(f == 0), stop=(f == FB - 1))
            mm.then_inc(g_mm, 1)
            pe.wait_ge(v_sb, FB // 2)
            for b in range(BATCH):
                for f in range(FB):
                    mm = pe.matmul(ps[0:KEYS, 4 + b, 0:D], vT[:, f, b * KEYS:(b + 1) * KEYS], woT[:, f, :],
                                   start=(f == 0), stop=(f == FB - 1))
            mm.then_inc(g_mm, 1)
            pe.wait_ge(g_sb, 3)
            for b in range(BATCH):
                for c in range(2):
                    for k in range(KD):
                        mm = pe.matmul(ps[0:KEYS, 2 * b + c, :], gT[:, k, b * KEYS:(b + 1) * KEYS],
                                       core.xnT[:, k, b * SEQ + c * CH:b * SEQ + (c + 1) * CH], start=(k == 0), stop=(k == KD - 1))
                mm.then_inc(s_mm, 1)
            for b in range(BATCH):
                pe.wait_ge(exp_done, b + 1)
                pe.wait_ge(v_ready, b + 1)
                for t in range(NT // BATCH):
                    n = b * 8 + t
                    if n >= 4:
                        pe.wait_ge(y_sb, n - 3)
                    pe.matmul(ps[:, 4 + n % 4, 0:D], ET[:, b, t * P:(t + 1) * P], vo[:, b, :], start=True, stop=True).then_inc(y_mm, 1)

        @block.scalar
        def _(act):
            act.wait_ge(kv_mm, 1)
            for f in range(FB):
                ins = act.activation(kT[:, f, :], ps[:, f // 2, (f % 2) * W:(f % 2 + 1) * W], ACT.Identity, bias=bk[:, f:f + 1])
                if f % 2:
                    ins.then_inc(k_sb, 1)
            for b in range(BATCH):
                act.wait_ge(bias_ready, b + 1)
                act.activation(ET[:, b, :], ps[0:KEYS, 2 * b:2 * b + 2, :], ACT.Exp, bias=nb[:, b:b + 1], scale=SCALE,
                               accum_out=sums[:, b:b + 1]).then_inc(exp_done, 1)

        @block.vector
        def _(dve):
            count = [0]

            def link(ins):
                count[0] += 1
                ins.then_inc(chain, 1)
                dve.wait_ge(chain, count[0])

            dve.wait_ge(loaded, 128)
            link(dve.tensor_tensor(core.x[:], core.x[:], bo[:].unsqueeze(1).broadcast_to([P, NT, D]), ALU.add))
            dve.wait_ge(kv_mm, 2)
            for f in range(FB):
                ins = dve.tensor_scalar(vT[:, f, :], ps[:, 4 + f // 2, (f % 2) * W:(f % 2 + 1) * W], bv[:, f:f + 1], None, ALU.add)
                if f % 2:
                    ins.then_inc(v_sb, 1)
            dve.wait_ge(g_mm, 1)
            dve.tensor_copy(gT[:], ps[:, 0:KD, 0:W]).then_inc(g_sb, 1)
            dve.wait_ge(g_mm, 2)
            dve.tensor_copy(cT[:], ps[0:KEYS, 2:4, 0]).then_inc(g_sb, 1)
            dve.wait_ge(g_mm, 3)
            dve.tensor_copy(vo[:], ps[0:KEYS, 4:6, 0:D]).then_inc(g_sb, 1)
            dve.wait_ge(g_sb, 3)
            for b in range(BATCH):
                col = slice(b, b + 1)
                dve.wait_ge(s_mm, b + 1)
                link(dve.tensor_reduce(mx[:, col], ps[0:KEYS, 2 * b:2 * b + 2, :], mybir.AxisListType.XY, ALU.max))
                link(dve.tensor_scalar(tmp[:, col], mx[:, col], cT[:, col], -1.0, ALU.add, ALU.mult))
                link(dve.tensor_scalar(tmp[:, col], tmp[:, col], cT[:, col], None, ALU.add))
                dve.tensor_scalar(nb[:, col], tmp[:, col], SCALE, None, ALU.mult).then_inc(bias_ready, 1)
            for b in range(BATCH):
                dve.wait_ge(exp_done, b + 1)
                link(dve.reciprocal(rs[:, b:b + 1], sums[:, b:b + 1]))
                dve.tensor_scalar(vo[:, b, :], vo[:, b, :], rs[:, b:b + 1], None, ALU.mult).then_inc(v_ready, 1)
            for n in range(NT):
                dve.wait_ge(y_mm, n + 1)
                dve.tensor_tensor(core.x[:, n, :], core.x[:, n, :], ps[:, 4 + n % 4, 0:D], ALU.add).then_inc(y_sb, 1)


def load_quantised_ffn(core, ctx):
    dram, loads = core.dram, Loads(core, ctx, "q")
    loads.load("w_inT", [P, FB, D], dram["L0_WinT"].rearrange("(f p) d -> p f d", p=P))
    loads.load("w_out", [P, FB, D], dram["L0_Wout"].rearrange("(f p) d -> p f d", p=P))
    loads.load("b_in", [P, FB], dram["L0_bin"])
    loads.load("b_out", [P, D], bcast(dram["L0_bout"], P))
    return loads


def quantised_ffn(core, inputs, xmax):
    nc, dram, ps = core.nc, core.dram, core.ps
    with ExitStack() as ctx:
        sb = lambda n, shape, dt=F32: ctx.enter_context(nc.sbuf_tensor(f"q_{n}", shape, dt))
        sem = lambda n: core.semaphore(ctx, f"q_{n}")
        w_inT, w_out, b_in, b_out = (inputs[n] for n in ("w_inT", "w_out", "b_in", "b_out"))
        w_in = sb("w_in", [P, KD, FF])
        amax, scale, inv = sb("amax", [P, 2 * FB]), sb("scale", [P, 2 * FB]), sb("inv", [P, 2 * FB])
        worth = sb("worth", [P, FB])
        xs, hs = sb("xs", [P, 4]), sb("hs", [P, 4])
        hid = sb("hid", [P, FB, TOK])
        hmaxes, hmax = sb("hmaxes", [P, FB * NCH]), sb("hmax", [P, 1])
        chain, wq_done, wT_mm, wT_sb, xq_done = sem("chain"), sem("wq"), sem("wT_mm"), sem("wT_sb"), sem("xq")
        xT_mm, xT_sb, h_mm, h_sb, xred, hred, hmax_done, hq_done, y_mm, y_sb, scales_done = (
            sem("xT_mm"), sem("xT_sb"), sem("h_mm"), sem("h_sb"), sem("xred"), sem("hred"), sem("hmax"),
            sem("hq"), sem("y_mm"), sem("y_sb"), sem("scales"))
        block = core.stage(ctx)

        @block.sync
        def _(sp):
            inputs.wait(sp)

        @block.gpsimd
        def _(pool):
            pool.partition_all_reduce(xs[:, 0:1], xmax[:, 0:1], P, bass.bass_isa.ReduceOp.max).then_inc(xred, 1)
            pool.wait_ge(hmax_done, FB * NCH + 1)
            pool.partition_all_reduce(hs[:, 0:1], hmax[:, 0:1], P, bass.bass_isa.ReduceOp.max).then_inc(hred, 1)

        @block.vector
        def _(dve):
            count = [0]

            def link(ins):
                count[0] += 1
                ins.then_inc(chain, 1)
                dve.wait_ge(chain, count[0])

            def scales_of(s, top):
                link(dve.tensor_scalar(s[:, 0:1], s[:, 0:1], 1e-8, None, ALU.max))
                link(dve.reciprocal(s[:, 1:2], s[:, 0:1]))
                link(dve.tensor_scalar(s[:, 2:3], s[:, 1:2], top, None, ALU.mult))
                link(dve.tensor_scalar(s[:, 3:4], s[:, 0:1], 1.0 / top, None, ALU.mult))

            def quantise(v, s):
                link(dve.tensor_scalar(v, v, s, 32767.0, ALU.mult, ALU.min))
                link(dve.tensor_scalar(v, v, -32768.0, ROUND, ALU.max, ALU.add))
                return dve.tensor_scalar(v, v, ROUND, None, ALU.subtract)

            def quantise_weights(i, w):
                half = slice(i * FB, (i + 1) * FB)
                link(dve.tensor_reduce(amax[:, half], w[:], AX, ALU.max, apply_absolute_value=True))
                link(dve.tensor_scalar(amax[:, half], amax[:, half], 1e-8, None, ALU.max))
                link(dve.reciprocal(scale[:, half], amax[:, half]))
                link(dve.tensor_scalar(scale[:, half], scale[:, half], 127.0, None, ALU.mult))
                link(dve.tensor_scalar(inv[:, half], amax[:, half], 1.0 / 127.0, None, ALU.mult))
                for f in range(FB):
                    n = i * FB + f
                    link(dve.tensor_scalar(w[:, f, :], w[:, f, :], scale[:, n:n + 1], 127.0, ALU.mult, ALU.min))
                    link(dve.tensor_scalar(w[:, f, :], w[:, f, :], -128.0, ROUND, ALU.max, ALU.add))
                    if i == 0:
                        dve.tensor_scalar(w[:, f, :], w[:, f, :], ROUND, None, ALU.subtract).then_inc(wq_done, 1)
                    else:
                        dve.tensor_scalar(w[:, f, :], w[:, f, :], ROUND, inv[:, n:n + 1], ALU.subtract, ALU.mult).then_inc(wq_done, 1)

            inputs.wait(dve)
            quantise_weights(0, w_inT)
            dve.wait_ge(xred, 1)
            scales_of(xs, 32767.0)
            quantise(core.xn[:], xs[:, 2:3]).then_inc(xq_done, 1)
            dve.tensor_scalar(worth[:], inv[:, 0:FB], xs[:, 3:4], None, ALU.mult).then_inc(scales_done, 1)
            for k in range(KD):
                dve.wait_ge(wT_mm, k + 1)
                dve.tensor_copy(w_in[:, k, :].rearrange("p (c n) -> p c n", n=CH), ps[:, 2 * k:2 * k + 2, :]).then_inc(wT_sb, 1)
            for g in range(NCH):
                dve.wait_ge(xT_mm, g + 1)
                dve.tensor_copy(core.xnT[:, :, g * CH:(g + 1) * CH], ps[:, 4 + 2 * (g % 2):6 + 2 * (g % 2), :]).then_inc(xT_sb, 1)
            quantise_weights(1, w_out)
            link(dve.tensor_tensor(core.x[:], core.x[:], b_out[:].unsqueeze(1).broadcast_to([P, NT, D]), ALU.add))
            for n in range(FB * NCH):
                c, f = n // FB, n % FB
                dve.wait_ge(h_sb, n + 1)
                dve.tensor_reduce(hmaxes[:, n:n + 1], hid[:, f, c * CH:(c + 1) * CH], AX, ALU.max, apply_absolute_value=True).then_inc(hmax_done, 1)
            dve.wait_ge(hmax_done, FB * NCH)
            dve.tensor_reduce(hmax[:], hmaxes[:], AX, ALU.max).then_inc(hmax_done, 1)
            dve.wait_ge(hred, 1)
            scales_of(hs, 32767.0)
            for c in range(NCH):
                quantise(hid[:, :, c * CH:(c + 1) * CH], hs[:, 2:3]).then_inc(hq_done, 1)
            for t in range(NT):
                dve.wait_ge(y_mm, t + 1)
                dve.scalar_tensor_tensor(core.x[:, t, :], ps[:, 4 + t % 4, 0:D], hs[:, 3:4], core.x[:, t, :],
                                         ALU.mult, ALU.add).then_inc(y_sb, 1)

        @block.tensor
        def _(pe):
            pe.wait_ge(wq_done, FB)
            for k in range(KD):
                for f in range(FB):
                    mm = pe.transpose(ps[:, 2 * k + f // 4, (f % 4) * P:(f % 4 + 1) * P], w_inT[:, f, k * P:(k + 1) * P], core.ident[:])
                mm.then_inc(wT_mm, 1)
            pe.wait_ge(xq_done, 1)
            for g in range(NCH):
                if g >= 2:
                    pe.wait_ge(xT_sb, g - 1)
                for k in range(KD):
                    for j in range(4):
                        mm = pe.transpose(ps[:, 4 + 2 * (g % 2) + k, j * P:(j + 1) * P],
                                          core.xn[:, 4 * g + j, k * P:(k + 1) * P], core.ident[:])
                mm.then_inc(xT_mm, 1)
            pe.wait_ge(wT_sb, KD)
            for n in range(FB * NCH):
                c, f = n // FB, n % FB
                pe.wait_ge(xT_sb, c + 1)
                if n >= 4:
                    pe.wait_ge(h_sb, n - 3)
                for k in range(KD):
                    mm = pe.matmul(ps[:, n % 4, :], w_in[:, k, f * P:(f + 1) * P], core.xnT[:, k, c * CH:(c + 1) * CH],
                                   start=(k == 0), stop=(k == KD - 1))
                mm.then_inc(h_mm, 1)
            pe.wait_ge(wq_done, 2 * FB)
            for t in range(NT):
                pe.wait_ge(hq_done, t // 4 + 1)
                if t >= 4:
                    pe.wait_ge(y_sb, t - 3)
                for f in range(FB):
                    mm = pe.matmul(ps[:, 4 + t % 4, 0:D], hid[:, f, t * P:(t + 1) * P], w_out[:, f, :], start=(f == 0), stop=(f == FB - 1))
                mm.then_inc(y_mm, 1)

        @block.scalar
        def _(act):
            act.wait_ge(scales_done, 1)
            inputs.wait(act)
            for n in range(FB * NCH):
                c, f = n // FB, n % FB
                act.wait_ge(h_mm, n + 1)
                act.activation(hid[:, f, c * CH:(c + 1) * CH], ps[:, n % 4, :], ACT.Gelu, bias=b_in[:, f:f + 1],
                               scale=worth[:, f:f + 1]).then_inc(h_sb, 1)


def load_headed_cross_attention(core, ctx, name, wqT, wkT, wvT, woT, mask=None, bq=None, bk=None, bv=None):
    loads = Loads(core, ctx, name)
    for n, a in (("wk", wkT), ("wv", wvT), ("wq", wqT), ("wo", woT)):
        loads.load(n, [P, KD, D], a.rearrange("(k p) d -> p k d", p=P))
    loads.load("head_of", [P, 8], core.dram["head_of"])
    loads.load("rest_of", [8 * REST, 8], core.dram["rest_of"])
    if bq is not None:
        loads.load("bq", [P, KD], bq)
        loads.load("bk", [P, KD], bk)
        loads.load("bv", [P, D], bcast(bv, P))
    if mask is not None:
        loads.load("mask", [P, NT, KEYS], mask.rearrange("(t p) k -> p t k", p=P), U8)
    return loads


def headed_cross_attention(core, name, w, out, bias=None):
    nc, dram, ps = core.nc, core.dram, core.ps
    W = BATCH * KEYS
    HW = 4 * KEYS
    with ExitStack() as ctx:
        sb = lambda n, shape, dt=F32: ctx.enter_context(nc.sbuf_tensor(f"{name}_{n}", shape, dt))
        sem = lambda n: core.semaphore(ctx, f"{name}_{n}")
        head_of = w["head_of"]
        qT, kT = sb("qT", [P, KD, TOK]), sb("kT", [P, KD, W])
        kbd = sb("kbd", [P, BATCH, KD, 8, KEYS])
        ctx_main, ctx_rest = sb("ctx_main", [P, KD, BATCH, 2, MAIN]), sb("ctx_rest", [P, KD, BATCH, 8, REST])
        v_main, v_rest = sb("v_main", [P, BATCH, 8, 2, DK + 1]), sb("v_rest", [8 * REST, BATCH, 3, 8, DK + 1])
        REST_AT = (0, 2)
        rest_of = w["rest_of"]
        s = sb("s", [P, 2, HEADS, KEYS])
        mx = sb("mx", [P, 2, HEADS])
        e = sb("e", [P, 2, HEADS * KEYS])
        pT = sb("pT", [P, 2, 10, P])
        rs, on, oT = sb("rs", [P, 2, HEADS]), sb("on", [P, 2, D]), sb("oT", [P, 2, KD, P])
        if bias is not None:
            bt = sb("bt", [P, 3, HEADS, KEYS])
        else:
            mt, bt = w["mask"], sb("bt", [P, NT, KEYS])
        projection_bias = "bq" in w.at
        if projection_bias:
            bqT, bkT, bv_bc = w["bq"], w["bk"], w["bv"]
        bias_in = [sem(f"bias{i}") for i in range(3)]
        q_mm, q_sb, kv_mm, kbd_done, v_sb, ones_done, ctx_done = (
            sem("q_mm"), sem("q_sb"), sem("kv_mm"), sem("kbd"), sem("v_sb"), sem("ones"), sem("ctx"))
        s_mm, s_sb, chain, s_ready, exp_done, pT_mm, pT_sb, o_mm, o_sb, oT_mm, oT_sb, y_mm, y_sb = (
            sem(x) for x in ("s_mm", "s_sb", "chain", "s_ready", "exp", "pT_mm", "pT_sb", "o_mm", "o_sb", "oT_mm", "oT_sb", "y_mm", "y_sb"))
        block = core.stage(ctx)

        @block.sync
        def _(sp):
            w.wait(sp)
            if bias is not None:
                for t in range(NT):
                    if t >= 3:
                        sp.wait_ge(s_sb, t - 2)
                    sp.dma_start(bt[:, t % 3, :, :], bias[t]).then_inc(bias_in[t % 3], 16)

        @block.gpsimd
        def _(pool):
            by_batch = core.ctxT[:].rearrange("p k (b n) -> p k b n", b=BATCH)
            for k in range(KD):
                pool.tensor_copy(ctx_main[:, k], by_batch[:, k, :, 0:MAIN].unsqueeze(2).broadcast_to([P, BATCH, 2, MAIN])).then_inc(ctx_done, 1)
                pool.tensor_copy(ctx_rest[:, k], by_batch[:, k, :, MAIN:KEYS].unsqueeze(2).broadcast_to([P, BATCH, 8, REST])).then_inc(ctx_done, 1)
            pool.memset(v_rest[:, :, 1], 0.0).then_inc(ones_done, 1)
            pool.memset(v_main[:], 0.0).then_inc(ones_done, 1)
            pool.wait_ge(ones_done, 2)
            for h in range(2):
                pool.memset(v_main[h * MAIN:(h + 1) * MAIN, :, :, h, DK:DK + 1], 1.0).then_inc(ones_done, 1)

        @block.vector
        def _(dve):
            count = [0]

            def link(ins):
                count[0] += 1
                ins.then_inc(chain, 1)
                dve.wait_ge(chain, count[0])

            w.wait(dve)
            if bias is None:
                link(dve.tensor_scalar(bt[:], mt[:], -3e38, 3e38, ALU.mult, ALU.add))
                link(dve.scalar_tensor_tensor(bt[:], mt[:], NEG, bt[:], ALU.mult, ALU.add))
            dve.wait_ge(kv_mm, 1)
            for k in range(KD):
                if projection_bias:
                    link(dve.tensor_scalar(kT[:, k, :], ps[:, k, 0:W], bkT[:, k:k + 1], 0.25, ALU.add, ALU.mult))
                else:
                    link(dve.tensor_scalar(kT[:, k, :], ps[:, k, 0:W], 0.25, None, ALU.mult))
            for b in range(BATCH):
                for k in range(KD):
                    for h in range(8):
                        dve.tensor_scalar(kbd[:, b, k, h, :], kT[:, k, b * KEYS:(b + 1) * KEYS], head_of[:, h:h + 1], None,
                                          ALU.mult).then_inc(kbd_done, 1)
            dve.wait_ge(kv_mm, 2)
            dve.wait_ge(ones_done, 4)
            for b in range(BATCH):
                for h in range(2):
                    rows = slice(h * MAIN, (h + 1) * MAIN)
                    v = ps[rows, 2 + b, 0:D].rearrange("p (j h d) -> p j h d", h=2, d=DK)[:, :, h, :]
                    if projection_bias:
                        link(dve.tensor_tensor(v_main[rows, b, :, h, 0:DK], v,
                                               bv_bc[rows].rearrange("p (j h d) -> p j h d", h=2, d=DK)[:, :, h, :], ALU.add))
                    else:
                        link(dve.tensor_copy(v_main[rows, b, :, h, 0:DK], v))
                v = ps[0:8 * REST, 2 + b, D:2 * D].rearrange("p (g h d) -> p g h d", g=2, d=DK)
                for g in range(2):
                    own = v_rest[:, b, REST_AT[g], :, 0:DK]
                    if projection_bias:
                        link(dve.tensor_tensor(own, v[:, g], bv_bc[0:8 * REST].rearrange("p (g h d) -> p g h d", g=2, d=DK)[:, g], ALU.add))
                    else:
                        link(dve.tensor_copy(own, v[:, g]))
                    link(dve.tensor_tensor(own, own, rest_of[:].unsqueeze(2).broadcast_to([8 * REST, 8, DK]), ALU.mult))
                    link(dve.tensor_copy(v_rest[:, b, REST_AT[g], :, DK], rest_of[:]))
            dve.sem_inc(v_sb, 1)

            def scores(t):
                i = t % 2
                dve.wait_ge(s_mm, t + 1)
                if t >= 2:
                    dve.wait_ge(exp_done, t - 1)
                raw = ps[:, 0:4, 0:HW].rearrange("p c (h k) -> p c h k", k=KEYS)
                si = s[:, i, :, :].rearrange("p (c h) k -> p c h k", c=4)
                if bias is not None:
                    dve.wait_ge(bias_in[t % 3], 16 * (t // 3 + 1))
                    ins = dve.tensor_tensor(si, raw, bt[:, t % 3, :, :].rearrange("p (c h) k -> p c h k", c=4), ALU.add)
                else:
                    ins = dve.tensor_tensor(si, raw, bt[:, t, :].unsqueeze(1).unsqueeze(1).broadcast_to([P, 4, 4, KEYS]), ALU.min)
                ins.then_inc(s_sb, 1)
                dve.wait_ge(s_sb, t + 1)
                link(dve.tensor_reduce(mx[:, i, :], s[:, i, :, :], AX, ALU.max))
                dve.tensor_tensor(s[:, i, :, :], s[:, i, :, :], mx[:, i, :].unsqueeze(2).broadcast_to([P, HEADS, KEYS]),
                                  ALU.subtract).then_inc(s_ready, 1)

            def normalise(t):
                i = t % 2
                dve.wait_ge(o_mm, t + 1)
                o = ps[:, 6, 0:HEADS * (DK + 1)].rearrange("p (h d) -> p h d", d=DK + 1)
                link(dve.reciprocal(rs[:, i, :], o[:, :, DK]))
                if t >= 2:
                    dve.wait_ge(oT_mm, t - 1)
                dve.tensor_tensor(on[:, i, :].rearrange("p (h d) -> p h d", d=DK), o[:, :, 0:DK],
                                  rs[:, i, :].unsqueeze(2).broadcast_to([P, HEADS, DK]), ALU.mult).then_inc(o_sb, 1)

            def add_projection(t):
                dve.wait_ge(y_mm, t + 1)
                dve.tensor_tensor(out[:, t, :], out[:, t, :], ps[:, 7, 0:D], ALU.add).then_inc(y_sb, 1)

            scores(0)
            for t in range(NT):
                if t + 1 < NT:
                    scores(t + 1)
                if t:
                    add_projection(t - 1)
                normalise(t)
            add_projection(NT - 1)

        @block.scalar
        def _(act):
            w.wait(act)
            for n in range(KD * NCH):
                act.wait_ge(q_mm, n + 1)
                out_, in_ = qT[:, n // NCH, (n % NCH) * CH:(n % NCH + 1) * CH], ps[:, 4 + n % 4, :]
                if projection_bias:
                    act.activation(out_, in_, ACT.Identity, bias=bqT[:, n // NCH:n // NCH + 1]).then_inc(q_sb, 1)
                else:
                    act.copy(out_, in_).then_inc(q_sb, 1)

            def exponential(t):
                act.wait_ge(s_ready, t + 1)
                if t >= 2:
                    act.wait_ge(pT_mm, 3 * (t - 1))
                main = e[:, t % 2, 0:HEADS * MAIN].rearrange("p (h k) -> p h k", k=MAIN)
                rest = e[:, t % 2, HEADS * MAIN:HEADS * KEYS].rearrange("p (h k) -> p h k", k=REST)
                act.activation(main, s[:, t % 2, :, 0:MAIN], ACT.Exp)
                act.activation(rest, s[:, t % 2, :, MAIN:KEYS], ACT.Exp).then_inc(exp_done, 1)

            def heads_transposed(t):
                act.wait_ge(oT_mm, t + 1)
                act.copy(oT[:, t % 2, :, :], ps[:, 7, D:2 * D].rearrange("p (k n) -> p k n", n=P)).then_inc(oT_sb, 1)

            exponential(0)
            for t in range(NT):
                if t:
                    heads_transposed(t - 1)
                if t >= 2:
                    act.wait_ge(o_mm, t - 1)
                for q in range(3):
                    act.wait_ge(pT_mm, 3 * t + q + 1)
                    rows, blocks, at = (P, 4, 4 * (q - 1)) if q else (8 * REST, 2, 8)
                    act.copy(pT[0:rows, t % 2, at:at + blocks, :],
                             ps[0:rows, 4 + (3 * t + q) % 2, 0:blocks * P].rearrange("p (h n) -> p h n", n=P)).then_inc(pT_sb, 1)
                if t + 1 < NT:
                    exponential(t + 1)
            heads_transposed(NT - 1)

        @block.tensor
        def _(pe):
            w.wait(pe)
            for k2 in range(KD):
                for k in range(KD):
                    mm = pe.matmul(ps[:, k2, 0:W], w["wk"][:, k, k2 * P:(k2 + 1) * P], core.ctxT[:, k, :], start=(k == 0), stop=(k == KD - 1))
            mm.then_inc(kv_mm, 1)
            pe.wait_ge(ctx_done, 2 * KD)
            for b in range(BATCH):
                for k in range(KD):
                    pe.matmul(ps[:, 2 + b, 0:D], ctx_main[:, k, b].rearrange("p h n -> p (h n)"), w["wv"][:, k, :],
                              start=(k == 0), stop=(k == KD - 1))
                for k in range(KD):
                    mm = pe.matmul(ps[0:8 * REST, 2 + b, D:2 * D], ctx_rest[:, k, b].rearrange("p h n -> p (h n)"), w["wv"][:, k, :],
                                   start=(k == 0), stop=(k == KD - 1))
            mm.then_inc(kv_mm, 1)
            for n in range(KD * NCH):
                k2, c = n // NCH, n % NCH
                if n >= 4:
                    pe.wait_ge(q_sb, n - 3)
                for k in range(KD):
                    mm = pe.matmul(ps[:, 4 + n % 4, :], w["wq"][:, k, k2 * P:(k2 + 1) * P], core.xnT[:, k, c * CH:(c + 1) * CH],
                                   start=(k == 0), stop=(k == KD - 1))
                mm.then_inc(q_mm, 1)
            pe.wait_ge(q_sb, KD * NCH)
            pe.wait_ge(kbd_done, BATCH * HEADS)
            pe.wait_ge(v_sb, 1)

            def scores(t):
                if t:
                    pe.wait_ge(s_sb, t)
                for c in range(4):
                    mm = pe.matmul(ps[:, c, 0:HW], qT[:, c // 2, t * P:(t + 1) * P],
                                   kbd[:, t // 8, c // 2, 4 * (c % 2):4 * (c % 2) + 4, :], start=True, stop=True)
                mm.then_inc(s_mm, 1)

            def transpose_heads(t):
                pe.wait_ge(o_sb, t + 1)
                if t:
                    pe.wait_ge(y_sb, t)
                for k in range(KD):
                    mm = pe.transpose(ps[:, 7, D + k * P:D + (k + 1) * P], on[:, t % 2, k * P:(k + 1) * P], core.ident[:])
                mm.then_inc(oT_mm, 1)

            def project(t):
                pe.wait_ge(oT_sb, t + 1)
                for k in range(KD):
                    mm = pe.matmul(ps[:, 7, 0:D], oT[:, t % 2, k, :], w["wo"][:, k, :], start=(k == 0), stop=(k == KD - 1))
                mm.then_inc(y_mm, 1)

            scores(0)
            for t in range(NT):
                i = t % 2
                if t + 1 < NT:
                    scores(t + 1)
                if t:
                    transpose_heads(t - 1)
                pe.wait_ge(exp_done, t + 1)
                for q in range(3):
                    n = 3 * t + q
                    if n >= 2:
                        pe.wait_ge(pT_sb, n - 1)
                    for j in range(4 if q else 2):
                        if q:
                            rows, at = P, (4 * (q - 1) + j) * P
                        else:
                            rows, at = 8 * REST, HEADS * MAIN + j * 8 * REST
                        mm = pe.transpose(ps[0:rows, 4 + n % 2, j * P:(j + 1) * P], e[:, i, at:at + rows], core.ident[:])
                    mm.then_inc(pT_mm, 1)
                if t:
                    project(t - 1)
                if t:
                    pe.wait_ge(o_sb, t)
                pe.wait_ge(pT_sb, 3 * t + 1)
                o, D1 = ps[:, 6, 0:HEADS * (DK + 1)], 8 * (DK + 1)
                pe.matmul(o, pT[0:8 * REST, i, 8, :], v_rest[:, t // 8, 0:2].rearrange("p g h d -> p (g h d)"), start=True, stop=False)
                pe.matmul(o[:, D1:2 * D1], pT[0:8 * REST, i, 9, :], v_rest[:, t // 8, 2].rearrange("p h d -> p (h d)"),
                          start=False, stop=False)
                for j in range(8):
                    if j % 4 == 0:
                        pe.wait_ge(pT_sb, 3 * t + 2 + j // 4)
                    mm = pe.matmul(o[:, j * D1 // 4:(j + 1) * D1 // 4], pT[:, i, j, :],
                                   v_main[:, t // 8, j].rearrange("p h d -> p (h d)"), start=False, stop=(j == 7))
                mm.then_inc(o_mm, 1)
            transpose_heads(NT - 1)
            project(NT - 1)


def load_plain_cross_attention(core, ctx):
    loads = Loads(core, ctx, "a2")
    loads.load("ctx", [KEYS, BATCH, D], core.dram["ctx"].rearrange("b k d -> k b d"))
    loads.load("mask", [P, BATCH, KEYS], bcast(core.dram["mask_ik"], P), I32)
    return loads


def plain_cross_attention(core, inputs):
    nc, dram, ps = core.nc, core.dram, core.ps
    with ExitStack() as ctx:
        sb = lambda n, shape, dt=F32: ctx.enter_context(nc.sbuf_tensor(f"a2_{n}", shape, dt))
        sem = lambda n: core.semaphore(ctx, f"a2_{n}")
        ctx_sb, mi = inputs["ctx"], inputs["mask"]
        mf = sb("mf", [P, BATCH, KEYS])
        s, p = sb("s", [P, NT, KEYS]), sb("p", [P, NT, KEYS])
        mx, sums, rs = sb("mx", [P, NT]), sb("sums", [P, NT]), sb("rs", [P, NT])
        pT = sb("pT", [KEYS, NT, P])
        s_mm, chain, s_ready, exp_done, rs_done, pT_mm, pT_sb, y_mm, y_sb = (
            sem(x) for x in ("s_mm", "chain", "s_ready", "exp", "rs", "pT_mm", "pT_sb", "y_mm", "y_sb"))
        block = core.stage(ctx)
        PER = 4

        @block.sync
        def _(sp):
            inputs.wait(sp)

        @block.tensor
        def _(pe):
            for t in range(NT):
                for k in range(KD):
                    mm = pe.matmul(ps[:, t // PER, (t % PER) * KEYS:(t % PER + 1) * KEYS], core.xnT[:, k, t * P:(t + 1) * P],
                                   core.ctxT[:, k, (t // 8) * KEYS:(t // 8 + 1) * KEYS], start=(k == 0), stop=(k == KD - 1))
                if t % PER == PER - 1:
                    mm.then_inc(s_mm, 1)
            inputs.wait(pe)
            pe.wait_ge(exp_done, NT)
            for g in range(NT // 4):
                for j in range(4):
                    mm = pe.transpose(ps[0:KEYS, 4 + g, j * P:(j + 1) * P], p[:, 4 * g + j, :], core.ident[:])
                mm.then_inc(pT_mm, 1)
            for t in range(NT):
                pe.wait_ge(pT_sb, t // 4 + 1)
                if t >= 4:
                    pe.wait_ge(y_sb, t - 3)
                pe.matmul(ps[:, t % 4, 0:D], pT[:, t, :], ctx_sb[:, t // 8, :], start=True, stop=True).then_inc(y_mm, 1)

        @block.scalar
        def _(act):
            for t in range(NT):
                act.wait_ge(s_ready, t // 8 + 1)
                act.activation(p[:, t, :], s[:, t, :], ACT.Exp, accum_out=sums[:, t:t + 1]).then_inc(exp_done, 1)
            for g in range(NT // 4):
                act.wait_ge(pT_mm, g + 1)
                act.copy(pT[:, 4 * g:4 * g + 4, :], ps[0:KEYS, 4 + g, :].rearrange("p (t n) -> p t n", n=P)).then_inc(pT_sb, 1)

        @block.vector
        def _(dve):
            count = [0]

            def link(ins):
                count[0] += 1
                ins.then_inc(chain, 1)
                dve.wait_ge(chain, count[0])

            inputs.wait(dve)
            link(dve.tensor_scalar(mf[:], mi[:], NEG, None, ALU.mult))
            for b in range(BATCH):
                dve.wait_ge(s_mm, 2 * b + 2)
                sb_ = s[:, 8 * b:8 * b + 8, :]
                for c in range(2):
                    link(dve.scalar_tensor_tensor(s[:, 8 * b + 4 * c:8 * b + 4 * c + 4, :],
                                                  ps[:, 2 * b + c, 0:PER * KEYS].rearrange("p (t k) -> p t k", k=KEYS),
                                                  D ** -0.5, mf[:, b, :].unsqueeze(1).broadcast_to([P, 4, KEYS]), ALU.mult, ALU.add))
                link(dve.tensor_reduce(mx[:, 8 * b:8 * b + 8], sb_, AX, ALU.max))
                dve.tensor_tensor(sb_, sb_, mx[:, 8 * b:8 * b + 8].unsqueeze(2).broadcast_to([P, 8, KEYS]), ALU.subtract).then_inc(s_ready, 1)
            dve.wait_ge(exp_done, NT)
            link(dve.reciprocal(rs[:], sums[:]))
            for t in range(NT):
                dve.wait_ge(y_mm, t + 1)
                dve.scalar_tensor_tensor(core.x[:, t, :], ps[:, t % 4, 0:D], rs[:, t:t + 1], core.x[:, t, :],
                                         ALU.mult, ALU.add).then_inc(y_sb, 1)


class Routing:

    def __init__(self, core, ctx, name, choices, by_expert=False):
        sb = lambda n, shape, dt=F32: ctx.enter_context(core.nc.sbuf_tensor(f"{name}_{n}", shape, dt))
        self.choices = choices
        self.core = core
        self.slots = min(choices * NT + EXPERTS, EXPERTS * NT)
        self.place = sb("place", [P, choices, NT], I32)
        self.padding = sb("padding", [P, EXPERTS + 2], I32)
        self.expert = sb("expert", [1, self.slots + 2], I32)
        self.by_expert = by_expert
        self.start_tile = sb("start_tile", [1, EXPERTS], I32)
        self.send_at = sb("send_at", [1, EXPERTS], I32)
        self.padding_out = core.lasting_semaphore(f"{name}_padding_out")
        self.rows_out = [core.lasting_semaphore(f"{name}_rows_out{k}") for k in range(choices)]
        self.last_pair = sb("last_pair", [1, 1], I32)

    def send(self, pool, k, tiles=range(NT)):
        for t in tiles:
            pool.indirect_dma_start(self.core.dram["scratch_rows"], bass.IndirectOffsetOnAxis(ap=self.place[:, k, t:t + 1], axis=0),
                                    self.core.rows[:, t, :], None, bounds_check=PLACES - 1, oob_is_err=False).then_inc(self.rows_out[k], 16)

    def wait_sent(self, pool, k):
        pool.wait_ge(self.rows_out[k], 16 * NT)


class Gate:

    def __init__(self, core, ctx, name, wg, bg, b2, routing):
        nc, dram = core.nc, core.dram
        sb = lambda n, shape, dt=F32: ctx.enter_context(nc.sbuf_tensor(f"{name}_{n}", shape, dt))
        self.wg, self.bg, self.has_b2 = sb("wg", [P, KD, EXPERTS]), sb("bg", [P, EXPERTS]), b2 is not None
        self.rank = sb("rank", [P, EXPERTS])
        self.b2 = sb("b2", [EXPERTS, D])
        self.before = sb("before", [P, P])
        self.ids, self.pad_ids, self.lane = sb("ids", [P, NT], I32), sb("pad_ids", [P, 1], I32), sb("lane", [P, 1])
        self.slot_ids = sb("slot_ids", [1, routing.slots + 2])
        self.loaded = core.lasting_semaphore(f"{name}_gate_in")
        loads = [(self.wg[:], wg.rearrange("(k p) e -> p k e", p=P)), (self.bg[:], bcast(bg, P)),
                 (self.rank[:], bcast(dram["rank"], P)), (self.before[:], dram["before"]), (self.ids[:], dram["token_ids"]),
                 (self.pad_ids[:], dram["pad_ids"]), (self.lane[:], dram["lane"]),
                 (self.slot_ids[:], dram["slot_ids"][0:routing.slots + 2].unsqueeze(0))]
        if b2 is not None:
            loads.append((self.b2[:], b2))
        for to, source in loads:
            nc.sync.dma_start(to, source).then_inc(self.loaded, 16)
        self.all_loaded = 16 * len(loads)


def route(core, name, kind, gate, routing, stream):
    acc = core.x
    nc, dram, ps = core.nc, core.dram, core.ps
    with ExitStack() as ctx:
        sb = lambda n, shape, dt=F32: ctx.enter_context(nc.sbuf_tensor(f"{name}_{n}", shape, dt))
        sem = lambda n: core.semaphore(ctx, f"{name}_{n}")
        wg_sb, bg_sb, b2_sb, rank, before = gate.wg, gate.bg, gate.b2, gate.rank, gate.before
        ids, pad_ids, lane, slot_ids = gate.ids, gate.pad_ids, gate.lane, gate.slot_ids
        lg, t1, t2 = (sb(n, [P, NT, EXPERTS]) for n in ("lg", "t1", "t2"))
        m1, m2, r1, e2 = (sb(n, [P, NT]) for n in ("m1", "m2", "r1", "e2"))
        w8 = core.rows[:, :, D:D + EXPERTS]
        if gate.has_b2:
            ewT = sb("ewT", [EXPERTS, NT, P])
        ones = sb("ones", [P, P])
        chosen = sb("chosen", [P, NT, EXPERTS])
        base = sb("base", [P, NT + 1, EXPERTS])
        cum = [sb(f"cum{i}", [P, EXPERTS]) for i in range(2)]
        start = sb("start", [P, EXPERTS])
        pf = sb("pf", [P, NT])
        pad_row = sb("pad_row", [P, ROW])
        pad_f, pad_ok = sb("pad_f", [P, EXPERTS + 2]), sb("pad_ok", [P, EXPERTS + 2])
        pad_done, acc_out, b2_done = sem("pad"), sem("acc_out"), sem("b2_done")
        past = sb("past", [1, routing.slots + 2, EXPERTS])
        ef = sb("ef", [1, routing.slots + 2])
        chosen_done, rank_mm, place_done = sem("chosen"), sem("rank_mm"), sem("place")
        g_mm, chain, act_in, act_out, w_done, wT_mm, wT_sb, y_mm, y_sb = (
            sem(x) for x in ("g_mm", "chain", "act_in", "act_out", "w", "wT_mm", "wT_sb", "y_mm", "y_sb"))
        block = core.stage(ctx)
        per_token = lambda v: v[:].unsqueeze(2).broadcast_to([P, NT, EXPERTS])
        per_expert = lambda v: v[:].unsqueeze(1).broadcast_to([P, NT, EXPERTS])

        @block.sync
        def _(sp):
            if gate.has_b2:
                sp.wait_ge(y_sb, NT)
            sp.dma_start(stream.rearrange("(t p) d -> p t d", p=P), core.x[:]).then_inc(acc_out, 16)
            sp.wait_ge(acc_out, 16)

        @block.gpsimd
        def _(pool):
            pool.memset(ones[:], 1.0).then_inc(chosen_done, 1)
            first_choices = 1 if routing.by_expert else routing.choices
            for k in range(first_choices):
                pool.wait_ge(place_done, k + 1)
                routing.send(pool, k)
            pool.wait_ge(pad_done, 2)
            for e in range(EXPERTS + 2):
                pool.indirect_dma_start(dram["scratch_rows"], bass.IndirectOffsetOnAxis(ap=routing.padding[:, e:e + 1], axis=0),
                                        pad_row[:], None, bounds_check=PLACES - 1, oob_is_err=False).then_inc(routing.padding_out, 16)
            for k in range(first_choices):
                routing.wait_sent(pool, k)
            pool.wait_ge(routing.padding_out, 16 * (EXPERTS + 2))

        @block.tensor
        def _(pe):
            pe.wait_ge(gate.loaded, gate.all_loaded)
            for t in range(NT):
                for k in range(KD):
                    mm = pe.matmul(ps[:, 0, t * EXPERTS:(t + 1) * EXPERTS], core.xnT[:, k, t * P:(t + 1) * P], wg_sb[:, k, :],
                                   start=(k == 0), stop=(k == KD - 1))
            mm.then_inc(g_mm, 1)
            pe.wait_ge(chosen_done, 2)
            pe.matmul(ps[:, 5, 0:NT * EXPERTS], before[:], chosen[:].rearrange("p t e -> p (t e)"), start=True, stop=True)
            pe.matmul(ps[:, 5, NT * EXPERTS:2 * NT * EXPERTS], ones[:], chosen[:].rearrange("p t e -> p (t e)"),
                      start=True, stop=True).then_inc(rank_mm, 1)
            if gate.has_b2:
                pe.wait_ge(w_done, 1)
                for g in range(NT // 4):
                    for j in range(4):
                        mm = pe.transpose(ps[0:EXPERTS, 1 + g, j * P:(j + 1) * P], w8[:, 4 * g + j, :], core.ident[:])
                mm.then_inc(wT_mm, 1)
                pe.wait_ge(wT_sb, 1)
                for t in range(NT):
                    if t >= 2:
                        pe.wait_ge(y_sb, t - 1)
                    pe.matmul(ps[:, 6 + t % 2, 0:D], ewT[:, t, :], b2_sb[:], start=True, stop=True).then_inc(y_mm, 1)

        @block.scalar
        def _(act):
            act.wait_ge(act_in, 1)
            if kind == "top2":
                act.activation(e2[:], m2[:], ACT.Exp).then_inc(act_out, 1)
            else:
                act.activation(t1[:], lg[:], ACT.Sigmoid).then_inc(act_out, 1)

        @block.vector
        def _(dve):
            count = [0]

            def link(ins):
                count[0] += 1
                ins.then_inc(chain, 1)
                dve.wait_ge(chain, count[0])

            def first_best(values, best, onehot):
                link(dve.tensor_reduce(best[:], values[:], AX, ALU.max))
                link(dve.tensor_tensor(onehot[:], values[:], per_token(best), ALU.is_equal))
                link(dve.tensor_tensor(onehot[:], onehot[:], per_expert(rank), ALU.mult))
                link(dve.tensor_reduce(r1[:], onehot[:], AX, ALU.max))
                link(dve.tensor_tensor(onehot[:], onehot[:], per_token(r1), ALU.is_equal))

            dve.wait_ge(gate.loaded, gate.all_loaded)
            dve.wait_ge(g_mm, 1)
            logits = ps[:, 0, 0:NT * EXPERTS].rearrange("p (t e) -> p t e", e=EXPERTS)
            link(dve.tensor_tensor(lg[:], logits, per_expert(bg_sb), ALU.add))
            if kind == "top2":
                first_best(lg, m1, t1)
                link(dve.scalar_tensor_tensor(lg[:], t1[:], -3e38, lg[:], ALU.mult, ALU.add))
                first_best(lg, m2, t2)
                dve.tensor_tensor(m2[:], m2[:], m1[:], ALU.subtract).then_inc(act_in, 1)
                dve.wait_ge(act_out, 1)
                link(dve.tensor_scalar(m1[:], e2[:], 1.0, None, ALU.add))
                link(dve.reciprocal(m1[:], m1[:]))
                link(dve.tensor_tensor(m2[:], e2[:], m1[:], ALU.mult))
                link(dve.tensor_tensor(chosen[:], t1[:], per_token(m1), ALU.mult))
                link(dve.tensor_tensor(lg[:], t2[:], per_token(m2), ALU.mult))
                dve.tensor_tensor(w8, chosen[:], lg[:], ALU.add).then_inc(w_done, 1)
                dve.wait_ge(w_done, 1)
                dve.tensor_tensor(chosen[:], t1[:], t2[:], ALU.add).then_inc(chosen_done, 1)
            elif kind == "threshold":
                dve.sem_inc(act_in, 1)
                dve.wait_ge(act_out, 1)
                dve.scalar_tensor_tensor(w8, t1[:], 0.5, t1[:], ALU.is_gt, ALU.mult).then_inc(w_done, 1)
                dve.tensor_scalar(chosen[:], t1[:], 0.5, None, ALU.is_gt).then_inc(chosen_done, 1)
            else:
                dve.sem_inc(act_in, 1)
                dve.wait_ge(act_out, 1)
                first_best(t1, m1, t2)
                dve.tensor_tensor(w8, t2[:], per_token(m1), ALU.mult).then_inc(w_done, 1)
                dve.tensor_copy(chosen[:], t2[:]).then_inc(chosen_done, 1)
            link(dve.memset(base[:, 0, :], 0.0))
            dve.wait_ge(rank_mm, 1)
            counts = ps[:, 5, :].rearrange("p (i t e) -> p i t e", i=4, e=EXPERTS)
            for t in range(NT):
                link(dve.tensor_tensor(base[:, t + 1, :], base[:, t, :], counts[:, 1, t, :], ALU.add))
            link(dve.tensor_scalar(cum[0][:], base[:, NT, :], 1.0 / P, (P - 1) / P - 0.5 + 0.5 / P, ALU.mult, ALU.add))
            link(dve.tensor_scalar(cum[0][:], cum[0][:], ROUND, ROUND, ALU.add, ALU.subtract))
            link(dve.tensor_copy(start[:], cum[0][:]))
            for i, n in enumerate((1, 2, 4)):
                a, b = cum[i % 2], cum[1 - i % 2]
                link(dve.tensor_copy(b[:, 0:n], a[:, 0:n]))
                link(dve.tensor_tensor(b[:, n:], a[:, n:], a[:, 0:EXPERTS - n], ALU.add))
            ends = cum[1]
            link(dve.tensor_tensor(start[:], ends[:], start[:], ALU.subtract))
            if routing.by_expert:
                link(dve.tensor_scalar(pad_f[:, 0:EXPERTS], start[:], 0.5, -0.25 - SEND_AHEAD, ALU.mult, ALU.add))
                link(dve.tensor_scalar(pad_f[:, 0:EXPERTS], pad_f[:, 0:EXPERTS], ROUND, ROUND, ALU.add, ALU.subtract))
                link(dve.tensor_scalar(pad_f[:, 0:EXPERTS], pad_f[:, 0:EXPERTS], 0.0, None, ALU.max))
                link(dve.tensor_copy(routing.send_at[:], pad_f[0:1, 0:EXPERTS]))
                link(dve.tensor_copy(routing.start_tile[:], start[0:1, :]))
            link(dve.tensor_scalar(start[:], start[:], float(P), None, ALU.mult))
            link(dve.tensor_tensor(pad_f[:, 0:EXPERTS], start[:], base[:, NT, :], ALU.add))
            link(dve.tensor_tensor(base[:, 0:NT, :], base[:, 0:NT, :], counts[:, 0], ALU.add))
            link(dve.tensor_tensor(base[:, 0:NT, :], base[:, 0:NT, :], per_expert(start), ALU.add))
            dve.tensor_copy(core.rows[:, :, D + EXPERTS].bitcast(I32), ids[:]).then_inc(w_done, 1)
            dve.wait_ge(w_done, 2)
            if kind == "threshold":
                link(dve.scalar_tensor_tensor(base[:, 0:NT, :], base[:, 0:NT, :], -NOWHERE, chosen[:], ALU.add, ALU.mult))
                link(dve.tensor_scalar(base[:, 0:NT, :], base[:, 0:NT, :], NOWHERE, None, ALU.add))
                dve.tensor_copy(routing.place[:].rearrange("p e t -> p t e"), base[:, 0:NT, :]).then_inc(place_done, EXPERTS)
            for k, onehot in enumerate({"top2": (t1, t2), "top1": (t2,), "threshold": ()}[kind]):
                link(dve.tensor_tensor(onehot[:], onehot[:], base[:, 0:NT, :], ALU.mult))
                link(dve.tensor_reduce(pf[:], onehot[:], AX, ALU.add))
                dve.tensor_copy(routing.place[:, k, :], pf[:]).then_inc(place_done, 1)
                dve.wait_ge(place_done, k + 1)
            link(dve.tensor_scalar(pad_f[:, 0:EXPERTS], pad_f[:, 0:EXPERTS], lane[:], None, ALU.add))
            link(dve.tensor_scalar(start[:], ends[:], float(P), None, ALU.mult))
            link(dve.tensor_tensor(pad_ok[:, 0:EXPERTS], pad_f[:, 0:EXPERTS], start[:], ALU.is_lt))
            link(dve.scalar_tensor_tensor(pad_f[:, 0:EXPERTS], pad_f[:, 0:EXPERTS], -NOWHERE, pad_ok[:, 0:EXPERTS], ALU.add, ALU.mult))
            link(dve.tensor_scalar(pad_f[:, 0:EXPERTS], pad_f[:, 0:EXPERTS], NOWHERE, None, ALU.add))
            for n in range(2):
                link(dve.tensor_scalar(pad_f[:, EXPERTS + n:EXPERTS + n + 1], start[:, EXPERTS - 1:EXPERTS], lane[:], float(n * P), ALU.add, ALU.add))
            link(dve.memset(pad_row[:], 0.0))
            dve.tensor_copy(pad_row[:, D + EXPERTS:ROW].bitcast(I32), pad_ids[:]).then_inc(pad_done, 1)
            dve.tensor_copy(routing.padding[:], pad_f[:]).then_inc(pad_done, 1)
            link(dve.tensor_tensor(past[:], ends[0:1, :].unsqueeze(1).broadcast_to([1, routing.slots + 2, EXPERTS]),
                                   slot_ids[:].unsqueeze(2).broadcast_to([1, routing.slots + 2, EXPERTS]), ALU.is_le))
            link(dve.tensor_reduce(ef[:], past[:], AX, ALU.add))
            link(dve.tensor_scalar(ef[:], ef[:], EXPERTS - 1.0, None, ALU.min))
            link(dve.tensor_copy(routing.expert[:], ef[:]))
            link(dve.tensor_scalar(ef[:, 0:1], ends[0:1, EXPERTS - 1:EXPERTS], 0.5, -0.75, ALU.mult, ALU.add))
            link(dve.tensor_scalar(ef[:, 0:1], ef[:, 0:1], ROUND, ROUND, ALU.add, ALU.subtract))
            link(dve.tensor_scalar(ef[:, 0:1], ef[:, 0:1], 0.0, None, ALU.max))
            link(dve.tensor_copy(routing.last_pair[:], ef[:, 0:1]))
            if gate.has_b2:
                dve.wait_ge(wT_mm, 1)
                dve.tensor_copy(ewT[:].rearrange("e (g t) p -> e g (t p)", g=4), ps[0:EXPERTS, 1:5, :]).then_inc(wT_sb, 1)
                for t in range(NT):
                    dve.wait_ge(y_mm, t + 1)
                    dve.tensor_tensor(acc[:, t, :], acc[:, t, :], ps[:, 6 + t % 2, 0:D], ALU.add).then_inc(y_sb, 1)


def load_feed_forward(core, ctx, name, w1, b1, w2):
    loads = Loads(core, ctx, name)
    loads.load("w1", [P, KD, FF], w1.rearrange("(k p) f -> p k f", p=P))
    loads.load("b1", [P, FB], b1)
    loads.load("w2", [P, FB, D], w2.rearrange("(f p) d -> p f d", p=P))
    return loads


def feed_forward(core, name, w, func, acc):
    nc, ps = core.nc, core.ps
    with ExitStack() as ctx:
        sem = lambda n: core.semaphore(ctx, f"{name}_{n}")
        hid = ctx.enter_context(nc.sbuf_tensor(f"{name}_hid", [P, 2, FB, CH], F32))
        h_mm, h_sb, y_mm, y_sb = sem("h_mm"), sem("h_sb"), sem("y_mm"), sem("y_sb")
        HB, YB = 4, 4
        block = core.stage(ctx)

        @block.tensor
        def _(pe):
            w.wait(pe)
            def first(c):
                for f in range(FB):
                    n = c * FB + f
                    if n >= HB:
                        pe.wait_ge(h_sb, n - HB + 1)
                    for k in range(KD):
                        mm = pe.matmul(ps[:, f % HB, :], w["w1"][:, k, f * P:(f + 1) * P],
                                       core.xnT[:, k, c * CH:(c + 1) * CH], start=(k == 0), stop=(k == KD - 1))
                    mm.then_inc(h_mm, 1)

            def second(c):
                pe.wait_ge(h_sb, (c + 1) * FB)
                for j in range(YB):
                    if c:
                        pe.wait_ge(y_sb, (c - 1) * YB + j + 1)
                    for f in range(FB):
                        mm = pe.matmul(ps[:, HB + j, 0:D], hid[:, c % 2, f, j * P:(j + 1) * P], w["w2"][:, f, :],
                                       start=(f == 0), stop=(f == FB - 1))
                    mm.then_inc(y_mm, 1)

            first(0)
            for c in range(NCH):
                if c + 1 < NCH:
                    first(c + 1)
                second(c)

        @block.scalar
        def _(act):
            w.wait(act)
            for c in range(NCH):
                if c >= 2:
                    act.wait_ge(y_mm, (c - 1) * YB)
                for f in range(FB):
                    act.wait_ge(h_mm, c * FB + f + 1)
                    act.activation(hid[:, c % 2, f, :], ps[:, f % HB, :], func, bias=w["b1"][:, f:f + 1]).then_inc(h_sb, 1)

        @block.vector
        def _(dve):
            for t in range(NT):
                dve.wait_ge(y_mm, t + 1)
                dve.tensor_tensor(acc[:, t, :], acc[:, t, :], ps[:, HB + t % YB, 0:D], ALU.add).then_inc(y_sb, 1)


def load_experts(core, ctx, name, w1, b1, w2):
    nc = core.nc
    sb = lambda n, shape: ctx.enter_context(nc.sbuf_tensor(f"{name}_{n}", shape, F32))
    w1_sb, w2_sb = sb("w1", [P, EXPERTS, KD, FF]), sb("w2", [P, EXPERTS, FB, D])
    b1_sb = sb("b1", [P, EXPERTS, FB]) if b1 is not None else None
    arrived = core.lasting_semaphore(f"{name}_experts_in")
    for e in range(EXPERTS):
        nc.sync.dma_start(w1_sb[:, e, :, :], w1[e].rearrange("(k p) f -> p k f", p=P)).then_inc(arrived, 16)
        nc.sync.dma_start(w2_sb[:, e, :, :], w2[e].rearrange("(f p) d -> p f d", p=P)).then_inc(arrived, 16)
    if b1 is not None:
        nc.sync.dma_start(b1_sb[:], b1).then_inc(arrived, 16)
    return w1_sb, b1_sb, w2_sb, arrived, 16 * (2 * EXPERTS + (b1 is not None))


def routed_feed_forward(core, name, experts, routing, func, stream, affineT=None, last=False):
    nc, dram, ps = core.nc, core.dram, core.ps
    w1_sb, b1_sb, w2_sb, experts_in, experts_all = experts
    S = routing.slots
    with ExitStack() as ctx:
        sb = lambda n, shape, dt=F32: ctx.enter_context(nc.sbuf_tensor(f"{name}_{n}", shape, dt))
        sem = lambda n: core.semaphore(ctx, f"{name}_{n}")
        rows, rowsT = sb("rows", [P, 2, ROW]), sb("rowsT", [P, 2, KD, P])
        w1_tile = core.xnT[:].rearrange("p u (k f) -> p u k f", k=KD)
        hT = sb("hT", [P, 2, FB, P])
        y = sb("y", [P, 2, D])
        weight, ids = sb("weight", [P, 2]), sb("ids", [P, 2], I32)
        bias = sb("bias", [P, 2, FB])
        if affineT is not None:
            g_sb, s_sb = affineT["gain"], affineT["shift"]
        rows_in, y_out = [sem("rows_in0"), sem("rows_in1")], core.lasting_semaphore(f"{name}_y_out")
        tail_in, y_free, acc_in, x_in, y_taken = sem("tail"), sem("y_free"), sem("acc_in"), sem("x_in"), sem("y_taken")
        rT_mm, rT_sb, h_mm, hT_sb, y_mm, y_sb, w1_in = (
            sem(n) for n in ("rT_mm", "rT_sb", "h_mm", "hT_sb", "y_mm", "y_sb", "w1_in"))
        block = core.stage(ctx)
        R_BANK, H_BANK, Y_BANK = 0, 1, 3

        def each_pair(eng, last_pair, step):
            group = 8 if S // 2 > 32 and S // 2 % 8 == 0 else S // 2
            if group == S // 2:
                with eng.Fori(0, group) as i:
                    step(i)
            else:
                with eng.Fori(0, S // 2 // group) as g:
                    with eng.If(g * group <= last_pair):
                        with eng.Fori(0, group) as j:
                            step(g * group + j)

        def each_tile(eng, step):
            last_pair = eng.value_load(routing.last_pair[:], min_val=0, max_val=S // 2 - 1)

            def pair(i):
                with eng.If(i <= last_pair):
                    for u in range(2):
                        if eng is nc.gpsimd:
                            step(i * 2 + u, u, i)
                        else:
                            step(i * 2 + u, u)

            each_pair(eng, last_pair, pair)

        @block.sync
        def _(sp):
            starts = []
            if routing.by_expert:
                starts = [sp.value_load(routing.start_tile[0:1, k:k + 1], min_val=0, max_val=S) for k in range(1, EXPERTS)]

            def load(s, u):
                for k, start in enumerate(starts):
                    with sp.If(start == s):
                        sp.wait_ge(routing.rows_out[k + 1], 16 * NT)
                sp.wait_ge(rT_mm, s + 1)
                sp.wait_ge(tail_in, s + 1)
                sp.dma_start(rows[:, u, :], dram["scratch_rows"].rearrange("(s p) d -> p s d", p=P)[:, bass.ds(s, 1), :]
                             .rearrange("p s d -> p (s d)")).then_inc(rows_in[u], 16)

            each_tile(sp, load)
            sp.wait_ge(acc_in, 1)
            if not last:
                sp.dma_start(core.x[:], stream.rearrange("(t p) d -> p t d", p=P)).then_inc(x_in, 16)
                sp.wait_ge(x_in, 16)

        @block.gpsimd
        def _(pool):
            def add_rows(s, u, i):
                pool.wait_ge(y_sb, s + 3)
                pool.sem_inc(y_taken, 1)
                pool.indirect_dma_start(stream, bass.IndirectOffsetOnAxis(ap=ids[:, u:u + 1], axis=0), y[:, u, :], None,
                                        bounds_check=TOK - 1, oob_is_err=False, compute_op=ALU.add).then_inc(y_out, 16)
                if routing.by_expert:
                    send_rows(i, u)
                pool.wait_ge(y_out, s * 16 + 16)
                pool.sem_inc(y_free, 1)

            def send_rows(i, u):
                for k in range(1, EXPERTS):
                    with pool.If(send_at[k] == i + 1):
                        routing.send(pool, k, range(4 * u, 4 * u + 4))
                    with pool.If(send_at[k] == i):
                        with pool.If(send_at[k] > 0):
                            routing.send(pool, k, range(8 + 4 * u, 12 + 4 * u))

            if routing.by_expert:
                send_at = [pool.value_load(routing.send_at[0:1, k:k + 1], min_val=0, max_val=S // 2) for k in range(EXPERTS)]
                for k in range(1, EXPERTS):
                    with pool.If(send_at[k] == 0):
                        routing.send(pool, k)
            each_tile(pool, add_rows)
            if routing.by_expert:
                for k in range(1, EXPERTS):
                    routing.wait_sent(pool, k)
            pool.sem_inc(acc_in, 1)

        @block.tensor
        def _(pe):
            def transpose_rows(s, u):
                pe.wait_ge(rows_in[u], (s - u) * 8 + 16)
                pe.wait_ge(rT_sb, s + 1)
                for k in range(KD):
                    mm = pe.transpose(ps[:, R_BANK, k * P:(k + 1) * P], rows[:, u, k * P:(k + 1) * P], core.ident[:])
                mm.then_inc(rT_mm, 1)

            def first(s, u):
                pe.wait_ge(rT_sb, s + 2)
                pe.wait_ge(w1_in, s + 1)
                pe.wait_ge(hT_sb, s * 2 + 3)
                for f in range(FB):
                    for k in range(KD):
                        mm = pe.matmul(ps[:, H_BANK + f // 4, f % 4 * P:(f % 4 + 1) * P], w1_tile[:, u, k, f * P:(f + 1) * P],
                                       rowsT[:, u, k, :], start=(k == 0), stop=(k == KD - 1))
                    if f % 4 == 3:
                        mm.then_inc(h_mm, 1)

            def second(s, u):
                e = pe.value_load(routing.expert[0:1, bass.ds(s, 1)], min_val=0, max_val=EXPERTS - 1)
                pe.wait_ge(hT_sb, s * 2 + 5)
                pe.wait_ge(y_sb, s + 2)
                for f in range(FB):
                    mm = pe.matmul(ps[:, Y_BANK, 0:D], hT[:, u, f, :], w2_sb[:, bass.ds(e, 1), f, :], start=(f == 0), stop=(f == FB - 1))
                mm.then_inc(y_mm, 1)

            last_pair = pe.value_load(routing.last_pair[:], min_val=0, max_val=S // 2 - 1)
            pe.wait_ge(experts_in, experts_all)
            pe.sem_inc(rT_mm, 2)
            pe.sem_inc(h_mm, 3)

            transpose_rows(0, 0)
            first(0, 0)
            transpose_rows(1, 1)

            def pair(i):
                with pe.If(i < last_pair):
                    for s, u in ((i * 2 + 1, 1), (i * 2 + 2, 0)):
                        first(s, u)
                        transpose_rows(s + 1, 1 - u)
                        second(s - 1, 1 - u)

            each_pair(pe, last_pair, pair)
            s = last_pair * 2 + 1
            first(s, 1)
            second(s - 1, 0)
            second(s, 1)

        @block.vector
        def _(dve):
            if affineT is not None:
                affineT.wait(dve)
            dve.sem_inc(rT_sb, 1)
            dve.sem_inc(tail_in, 2)

            def weights(s, u):
                e = dve.value_load(routing.expert[0:1, bass.ds(s, 1)], min_val=0, max_val=EXPERTS - 1)
                dve.wait_ge(h_mm, s * 2 + 1)
                ins = dve.tensor_scalar(w1_tile[:, u, :, :], w1_sb[:, bass.ds(e, 1), :, :].rearrange("p e k f -> p (e k) f"), 0.0, None, ALU.add)
                if b1_sb is not None:
                    dve.wait_ge(hT_sb, s * 2 + 1)
                    ins = dve.tensor_scalar(bias[:, u, :], b1_sb[:, bass.ds(e, 1), :].rearrange("p e f -> p (e f)"), 0.0, None, ALU.add)
                ins.then_inc(w1_in, 1)

            def step(s, u):
                e = dve.value_load(routing.expert[0:1, bass.ds(s, 1)], min_val=0, max_val=EXPERTS - 1)
                dve.wait_ge(rT_mm, s + 3)
                if affineT is not None:
                    for k in range(KD):
                        ins = dve.tensor_scalar(rowsT[:, u, k, :], ps[:, R_BANK, k * P:(k + 1) * P], g_sb[:, k:k + 1], s_sb[:, k:k + 1],
                                                ALU.mult, ALU.add)
                    ins.then_inc(rT_sb, 1)
                else:
                    dve.tensor_copy(rowsT[:, u, :, :].rearrange("p k n -> p (k n)"), ps[:, R_BANK, 0:D]).then_inc(rT_sb, 1)
                weights(s + 1, 1 - u)
                dve.wait_ge(y_free, s + 1)
                dve.tensor_copy(ids[:, u:u + 1], rows[:, u, D + EXPERTS:ROW].bitcast(I32))
                dve.tensor_scalar(weight[:, u:u + 1], rows[:, u, D:D + EXPERTS][:, bass.ds(e, 1)], 0.0, None, ALU.add).then_inc(tail_in, 1)

            weights(0, 0)
            each_tile(dve, step)

        @block.scalar
        def _(act):
            act.sem_inc(y_sb, 2)
            act.sem_inc(y_free, 2)
            act.sem_inc(hT_sb, 3)

            def hidden(s, u):
                for c in range(2):
                    act.wait_ge(h_mm, s * 2 + (c + 4))
                    if b1_sb is not None:
                        for j in range(4):
                            f = 4 * c + j
                            ins = act.activation(hT[:, u, f, :], ps[:, H_BANK + c, j * P:(j + 1) * P], func, bias=bias[:, u, f:f + 1])
                    else:
                        ins = act.activation(hT[:, u, 4 * c:4 * c + 4, :].rearrange("p f n -> p (f n)"), ps[:, H_BANK + c, :], func)
                    ins.then_inc(hT_sb, 1)

            def weigh(s, u):
                act.wait_ge(y_mm, s + 1)
                act.wait_ge(y_free, s + 1)
                act.wait_ge(tail_in, s + 3)
                act.activation(y[:, u, :], ps[:, Y_BANK, 0:D], ACT.Copy, scale=weight[:, u:u + 1]).then_inc(y_sb, 1)

            last_pair = act.value_load(routing.last_pair[:], min_val=0, max_val=S // 2 - 1)
            hidden(0, 0)

            def pair(i):
                with act.If(i < last_pair):
                    for s, u in ((i * 2 + 1, 1), (i * 2 + 2, 0)):
                        hidden(s, u)
                        weigh(s - 1, 1 - u)

            each_pair(act, last_pair, pair)
            s = last_pair * 2 + 1
            hidden(s, 1)
            weigh(s - 1, 0)
            weigh(s, 1)


PARTS = 3
PROD = ((0, 0), (0, 1), (1, 0), (1, 1), (0, 2), (2, 0))
SR = len(PROD) * DK


def load_projections(core, ctx):
    loads = Loads(core, ctx, "sp")
    loads.load("wqkv", [P, KD, 3 * D], core.dram["L1f_wqkv"].rearrange("(k p) d -> p k d", p=P))
    loads.load("bqk", [P, 4], core.dram["L1f_bqk"])
    loads.load("bv", [P, D], bcast(core.dram["L1f_bv"], P))
    return loads


def self_attention(core, w, acc):
    nc, dram, ps = core.nc, core.dram, core.ps
    KT = SEQ // P
    NP = BATCH * HEADS // 2
    with ExitStack() as ctx:
        sb = lambda n, shape, dt=F32: ctx.enter_context(nc.sbuf_tensor(f"sa_{n}", shape, dt))
        sem = lambda n: core.semaphore(ctx, f"sa_{n}")
        parts = dram["scratch_parts"]
        maxima = dram["scratch_max"]
        vh = sb("vh", [P, NT, HEADS, DK + 1])
        on = sb("on", [P, NT, D])

        with ExitStack() as c2:
            sb2 = lambda n, shape, dt=F32: c2.enter_context(nc.sbuf_tensor(f"sp_{n}", shape, dt))
            sem2 = lambda n: core.semaphore(c2, f"sp_{n}")
            wqkv, bqk, bv = w["wqkv"], w["bqk"], w["bv"]
            q32 = sb2("q32", [P, 2, CH])
            r32 = sb2("r32", [P, 2, CH])
            part = [sb2(f"part{i}", [P, 2, CH], BF16) for i in range(PARTS)]
            mm_done, q_sb, chain, split, stored, v_mm, v_sb, ones = (
                sem2("mm"), sem2("q_sb"), sem2("chain"), sem2("split"), [sem2("stored0"), sem2("stored1")], sem2("v_mm"), sem2("v_sb"), sem2("ones"))
            NQ = 4 * NCH
            block = core.stage(c2)

            @block.sync
            def _(sp):
                w.wait(sp)
                for n in range(NQ):
                    j, c = n // NCH, n % NCH
                    sp.wait_ge(split, n + 1)
                    for i in range(PARTS):
                        sp.dma_start(parts[j // 2, i, (j % 2) * P:(j % 2 + 1) * P, c * CH:(c + 1) * CH], part[i][:, n % 2, :]).then_inc(stored[n % 2], 16)
                for u in range(2):
                    sp.wait_ge(stored[u], NQ // 2 * 48)

            @block.tensor
            def _(pe):
                w.wait(pe)
                for n in range(NQ):
                    j, c = n // NCH, n % NCH
                    if n >= 4:
                        pe.wait_ge(q_sb, n - 3)
                    for k in range(KD):
                        mm = pe.matmul(ps[:, n % 4, :], wqkv[:, k, j * P:(j + 1) * P], core.xnT[:, k, c * CH:(c + 1) * CH],
                                       start=(k == 0), stop=(k == KD - 1))
                    mm.then_inc(mm_done, 1)
                for t in range(NT):
                    if t >= 4:
                        pe.wait_ge(v_sb, t - 3)
                    for k in range(KD):
                        mm = pe.matmul(ps[:, 4 + t % 4, 0:D], core.xnT[:, k, t * P:(t + 1) * P], wqkv[:, k, 2 * D:3 * D],
                                       start=(k == 0), stop=(k == KD - 1))
                    mm.then_inc(v_mm, 1)

            @block.gpsimd
            def _(pool):
                pool.memset(vh[:, :, :, DK:DK + 1], 1.0).then_inc(ones, 1)

            @block.scalar
            def _(act):
                w.wait(act)
                for n in range(NQ):
                    j = n // NCH
                    act.wait_ge(mm_done, n + 1)
                    if n >= 2:
                        act.wait_ge(split, n - 1)
                    act.activation(q32[:, n % 2, :], ps[:, n % 4, :], ACT.Identity, bias=bqk[:, j:j + 1]).then_inc(q_sb, 1)

            @block.vector
            def _(dve):
                count = [0]

                def link(ins):
                    count[0] += 1
                    ins.then_inc(chain, 1)
                    dve.wait_ge(chain, count[0])

                for n in range(NQ):
                    u = n % 2
                    dve.wait_ge(q_sb, n + 1)
                    if n >= 2:
                        dve.wait_ge(stored[u], 48 * (n // 2))
                    link(dve.tensor_copy(part[0][:, u, :], q32[:, u, :]))
                    link(dve.tensor_tensor(r32[:, u, :], q32[:, u, :], part[0][:, u, :], ALU.subtract))
                    link(dve.tensor_copy(part[1][:, u, :], r32[:, u, :]))
                    dve.tensor_tensor(part[2][:, u, :], r32[:, u, :], part[1][:, u, :], ALU.subtract).then_inc(split, 1)
                w.wait(dve)
                for t in range(NT):
                    dve.wait_ge(v_mm, t + 1)
                    dve.tensor_tensor(vh[:, t, :, 0:DK], ps[:, 4 + t % 4, 0:D].rearrange("p (h d) -> p h d", d=DK),
                                      bv[:].rearrange("p (h d) -> p h d", d=DK), ALU.add).then_inc(v_sb, 1)

        with ExitStack() as c3:
            sb3 = lambda n, shape, dt=F32: c3.enter_context(nc.sbuf_tensor(f"sh_{n}", shape, dt))
            sem3 = lambda n: core.semaphore(c3, f"sh_{n}")
            U = 4
            qs = [sb3(f"qs{u}", [SR + PARTS, 2, SEQ], BF16) for u in range(U)]
            ks = [sb3(f"ks{u}", [SR + PARTS, 2, SEQ], BF16) for u in range(U)]
            mhalf, m32 = sb3("mhalf", [P, 2, 2 * KT]), sb3("m32", [P, 2 * KT])
            mpart = [sb3(f"mpart{i}", [P, 2 * KT]) for i in range(PARTS)]
            mbf = [sb3(f"mbf{i}", [P, 2 * KT], BF16) for i in range(2)]
            mT = sb3("mT", [2 * KT, PARTS, P], BF16)
            pT = sb3("pT", [P, 4, 2, CH])
            oT_sb_, rs = sb3("oT", [P, CH]), sb3("rs", [P, 4, 4])
            stack_in = [sem3(f"stack_in{u}") for u in range(U)]
            max_in, max_out, ones_in = [sem3(f"max_in{u}") for u in range(U)], sem3("max_out"), sem3("ones_in")
            a_mm, a_max, chain, m_split, mT_mm, mT_sb, b_mm, exp_done, pv_mm, oT_done, on_mm, on_done = (
                sem3(x) for x in ("a_mm", "a_max", "chain", "m_split", "mT_mm", "mT_sb", "b_mm", "exp", "pv_mm", "oT", "on_mm", "on"))
            block = core.stage(c3)
            A_BANK, B_BANK, O_BANK, T_BANK = 0, 2, 6, 7
            NA = 2 * KT * 2

            @block.sync
            def _(sp):
                def load_stack(s):
                    b, hp, u = s // (HEADS // 2), s % (HEADS // 2), s % U
                    rows = lambda w_, i: parts[w_, i, hp * 2 * DK:(hp + 1) * 2 * DK, b * SEQ:(b + 1) * SEQ].rearrange("(h p) n -> p h n", p=DK)
                    if s >= U:
                        sp.wait_ge(pv_mm, (s - U + 1) * KT)
                    for j, (i, k) in enumerate(PROD):
                        sp.dma_start(qs[u][j * DK:(j + 1) * DK, :, :], rows(0, i)).then_inc(stack_in[u], 16)
                        sp.dma_start(ks[u][j * DK:(j + 1) * DK, :, :], rows(1, k)).then_inc(stack_in[u], 16)

                def lay_maxima(s):
                    sp.wait_ge(mT_sb, s + 1)
                    sp.dma_start(maxima[:, s].rearrange("i h (t n) -> (h t) i n", n=P), mT[:]).then_inc(max_out, 16)
                    sp.wait_ge(max_out, 16 * (s + 1))
                    sp.dma_start(qs[s % U][SR:SR + PARTS, :, :], maxima[:, s]).then_inc(max_in[s % U], 16)

                for s in range(U - 1):
                    load_stack(s)
                lay_maxima(0)
                for s in range(NP):
                    if s + 1 < NP:
                        lay_maxima(s + 1)
                    if s + U - 1 < NP:
                        load_stack(s + U - 1)

            @block.gpsimd
            def _(pool):
                for u in range(U):
                    pool.memset(ks[u][SR:SR + PARTS, :, :], 1.0).then_inc(ones_in, 1)

            def first_pass(pe, s, c):
                u, h, t, half = s % U, c // (2 * KT), c // 2 % KT, c % 2
                n = s * NA + c
                if c == 0:
                    pe.wait_ge(stack_in[u], 16 * 2 * len(PROD) * (s // U + 1))
                if n >= 2:
                    pe.wait_ge(a_max, n - 1)
                pe.matmul(ps[:, A_BANK + n % 2, :], qs[u][0:SR, h, t * P:(t + 1) * P], ks[u][0:SR, h, half * CH:(half + 1) * CH],
                          start=True, stop=True).then_inc(a_mm, 1)

            @block.tensor
            def _(pe):
                pe.wait_ge(ones_in, U)

                def turn_maxima(s):
                    pe.wait_ge(m_split, s + 1)
                    if s >= 3:
                        pe.wait_ge(on_done, s - 2)
                    for i in range(PARTS):
                        mm = pe.transpose(ps[0:2 * KT, T_BANK, i * P:(i + 1) * P], mpart[i][:], core.ident[:])
                    mm.then_inc(mT_mm, 1)

                def turn_outputs(s):
                    pe.wait_ge(oT_done, s + 1)
                    pe.wait_ge(mT_sb, min(s + 3, NP))
                    if s:
                        pe.wait_ge(on_done, s)
                    for j in range(4):
                        mm = pe.transpose(ps[:, T_BANK, j * P:(j + 1) * P], oT_sb_[:, j * P:(j + 1) * P], core.ident[:])
                    mm.then_inc(on_mm, 1)

                for c in range(NA):
                    first_pass(pe, 0, c)
                turn_maxima(0)
                for c in range(NA):
                    first_pass(pe, 1, c)
                for s in range(NP):
                    u = s % U
                    pe.wait_ge(max_in[u], 16 * (s // U + 1))

                    def weighted(k):
                        pe.wait_ge(exp_done, s * 2 * KT + 2 * k + 2)
                        if k == 0 and s:
                            pe.wait_ge(oT_done, s)
                        b = s // (HEADS // 2)
                        for h in range(2):
                            head = 2 * (s % (HEADS // 2)) + h
                            for half in range(2):
                                g = 2 * h + half
                                mm = pe.matmul(ps[32 * g:32 * g + DK + 1, O_BANK, :], vh[:, b * KT + k, head, :],
                                               pT[:, (2 * k + h) % 4, half, :], start=(k == 0), stop=(k == KT - 1))
                        mm.then_inc(pv_mm, 1)

                    for k in range(KT):
                        for h in range(2):
                            n = s * 2 * KT + 2 * k + h
                            if n >= 2:
                                pe.wait_ge(exp_done, n - 1)
                            for half in range(2):
                                mm = pe.matmul(ps[:, B_BANK + 2 * (n % 2) + half, :], ks[u][:, h, k * P:(k + 1) * P],
                                               qs[u][:, h, half * CH:(half + 1) * CH], start=True, stop=True)
                            mm.then_inc(b_mm, 1)
                            if s + 2 < NP:
                                for c in range(2):
                                    first_pass(pe, s + 2, (2 * k + h) * 2 + c)
                        if k:
                            weighted(k - 1)
                        if k == 1 and s + 1 < NP:
                            turn_maxima(s + 1)
                        if k == 2 and s:
                            turn_outputs(s - 1)
                    weighted(KT - 1)
                turn_outputs(NP - 1)

            @block.scalar
            def _(act):
                for s in range(NP):
                    for n in range(s * 2 * KT, (s + 1) * 2 * KT):
                        act.wait_ge(b_mm, n + 1)
                        if n >= 4:
                            act.wait_ge(pv_mm, n // 2 - 1)
                        act.activation(pT[:, n % 4, :, :], ps[:, B_BANK + 2 * (n % 2):B_BANK + 2 * (n % 2) + 2, :], ACT.Exp,
                                       scale=DK ** -0.5).then_inc(exp_done, 1)
                    act.wait_ge(pv_mm, (s + 1) * KT)
                    if s:
                        act.wait_ge(on_mm, s)
                    act.copy(oT_sb_[:], ps[:, O_BANK, :]).then_inc(oT_done, 1)

            @block.vector
            def _(dve):
                count = [0]

                def link(ins):
                    count[0] += 1
                    ins.then_inc(chain, 1)
                    dve.wait_ge(chain, count[0])

                def reduce_scores(s, chunks):
                    for c in chunks:
                        n = s * NA + c
                        h, t, half = c // (2 * KT), c // 2 % KT, c % 2
                        dve.wait_ge(a_mm, n + 1)
                        dve.tensor_reduce(mhalf[:, half, h * KT + t:h * KT + t + 1], ps[:, A_BANK + n % 2, :], AX, ALU.max).then_inc(a_max, 1)

                def split_maxima(s):
                    dve.wait_ge(a_max, (s + 1) * NA)
                    link(dve.tensor_tensor(m32[:], mhalf[:, 0, :], mhalf[:, 1, :], ALU.max))
                    link(dve.tensor_scalar(m32[:], m32[:], -1.0, None, ALU.mult))
                    link(dve.tensor_copy(mbf[0][:], m32[:]))
                    link(dve.tensor_copy(mpart[0][:], mbf[0][:]))
                    link(dve.tensor_tensor(m32[:], m32[:], mpart[0][:], ALU.subtract))
                    link(dve.tensor_copy(mbf[1][:], m32[:]))
                    link(dve.tensor_copy(mpart[1][:], mbf[1][:]))
                    dve.tensor_tensor(mpart[2][:], m32[:], mpart[1][:], ALU.subtract).then_inc(m_split, 1)

                def maxima_rows(s):
                    dve.wait_ge(mT_mm, s + 1)
                    if s:
                        dve.wait_ge(max_out, 16 * s)
                    dve.tensor_copy(mT[:], ps[0:2 * KT, T_BANK, 0:PARTS * P].rearrange("p (i n) -> p i n", n=P)).then_inc(mT_sb, 1)

                def finish(s):
                    b, hp = s // (HEADS // 2), s % (HEADS // 2)
                    dve.wait_ge(on_mm, s + 1)
                    o = ps[:, T_BANK, :].rearrange("p (j g d) -> p j g d", g=4, d=32)
                    link(dve.reciprocal(rs[:], o[:, :, :, DK]))
                    for h in range(2):
                        dst = on[:, b * KT:(b + 1) * KT, (2 * hp + h) * DK:(2 * hp + h + 1) * DK].rearrange("p (g j) d -> p j g d", g=2)
                        ins = dve.tensor_tensor(dst, o[:, :, 2 * h:2 * h + 2, 0:DK],
                                                rs[:, :, 2 * h:2 * h + 2].unsqueeze(3).broadcast_to([P, 4, 2, DK]), ALU.mult)
                    ins.then_inc(on_done, 1)

                reduce_scores(0, range(NA))
                split_maxima(0)
                maxima_rows(0)
                reduce_scores(1, range(NA))
                split_maxima(1)
                for s in range(NP):
                    if s + 2 < NP:
                        reduce_scores(s + 2, range(0, 8))
                    if s + 1 < NP:
                        maxima_rows(s + 1)
                    if s + 2 < NP:
                        reduce_scores(s + 2, range(8, 12))
                    if s:
                        finish(s - 1)
                    if s + 2 < NP:
                        reduce_scores(s + 2, range(12, NA))
                        split_maxima(s + 2)
                finish(NP - 1)
        transpose_tokens(core, "sat", on, core.xnT)
        token_projection(core, "sao", dram["L1f_wo"], dram["L1f_bo"], acc)


def token_projection(core, name, w, b, acc):
    nc, ps = core.nc, core.ps
    with ExitStack() as ctx:
        w_sb = ctx.enter_context(nc.sbuf_tensor(f"{name}_w", [P, KD, D], F32))
        b_sb = ctx.enter_context(nc.sbuf_tensor(f"{name}_b", [P, D], F32))
        loaded, bias_done, y_mm, y_sb = (core.semaphore(ctx, f"{name}_{n}") for n in ("loaded", "bias", "y_mm", "y_sb"))
        block = core.stage(ctx)

        @block.sync
        def _(sp):
            sp.dma_start(w_sb[:], w.rearrange("(k p) d -> p k d", p=P)).then_inc(loaded, 16)
            sp.dma_start(b_sb[:], bcast(b, P)).then_inc(loaded, 16)
            sp.wait_ge(loaded, 32)

        @block.tensor
        def _(pe):
            pe.wait_ge(loaded, 32)
            for t in range(NT):
                if t >= 4:
                    pe.wait_ge(y_sb, t - 3)
                for k in range(KD):
                    mm = pe.matmul(ps[:, t % 4, 0:D], core.xnT[:, k, t * P:(t + 1) * P], w_sb[:, k, :], start=(k == 0), stop=(k == KD - 1))
                mm.then_inc(y_mm, 1)

        @block.vector
        def _(dve):
            dve.wait_ge(loaded, 32)
            dve.tensor_tensor(acc[:], acc[:], b_sb[:].unsqueeze(1).broadcast_to([P, NT, D]), ALU.add).then_inc(bias_done, 1)
            dve.wait_ge(bias_done, 1)
            for t in range(NT):
                dve.wait_ge(y_mm, t + 1)
                dve.tensor_tensor(acc[:, t, :], acc[:, t, :], ps[:, t % 4, 0:D], ALU.add).then_inc(y_sb, 1)


def add_to(core, name, dst, src, row=None):
    nc = core.nc
    with ExitStack() as ctx:
        done = core.semaphore(ctx, f"{name}_done")
        if row is not None:
            row_sb = ctx.enter_context(nc.sbuf_tensor(f"{name}_row", [P, D], F32))
            src = row_sb[:].unsqueeze(1).broadcast_to([P, NT, D])
        loaded = core.semaphore(ctx, f"{name}_loaded")
        block = core.stage(ctx)

        @block.sync
        def _(sp):
            if row is not None:
                sp.dma_start(row_sb[:], bcast(row, P)).then_inc(loaded, 16)
                sp.wait_ge(loaded, 16)

        @block.vector
        def _(dve):
            if row is not None:
                dve.wait_ge(loaded, 16)
            dve.tensor_tensor(dst[:], dst[:], src if row is not None else src[:], ALU.add).then_inc(done, 1)


def store_output(core):
    nc = core.nc
    with ExitStack() as ctx:
        stored = core.semaphore(ctx, "out_stored")
        block = core.stage(ctx)

        @block.sync
        def _(sp):
            sp.dma_start(core.dram["out"].rearrange("b (t p) d -> p (b t) d", p=P), core.x[:]).then_inc(stored, 16)
            sp.wait_ge(stored, 16)


def program(nc, dram, stages=range(1, 9)):
    with ExitStack() as ctx:
        core = Core(nc, ctx, dram)
        x, xn, xnT = core.x, core.xn, core.xnT
        load_inputs(core)
        if 1 in stages:
            layer_norm(core, "n0", x, xn, xnT)
            query_softmax_attention(core)
        if 2 in stages:
            with ExitStack() as layer:
                inputs = load_quantised_ffn(core, layer)
                xmax = layer.enter_context(nc.sbuf_tensor("xmax", [P, 1], F32))
                layer_norm(core, "n1", x, xn, absmax=xmax)
                quantised_ffn(core, inputs, xmax)
        if 3 in stages:
            with ExitStack() as layer:
                inputs = load_headed_cross_attention(core, layer, "a1", *(dram[f"L1_W{n}T"] for n in "qkvo"))
                layer_norm(core, "n2", x, xn, xnT)
                headed_cross_attention(core, "a1", inputs, xn, bias=dram["bias"])
            with ExitStack() as layer:
                affineT = load_affine(core, layer, "a3n", dram["L1_g1"], dram["L1_be1"])
                inputs = load_feed_forward(core, layer, "f1", dram["L1_W1T"], dram["L1_b1"], dram["L1_W2T"])
                with nc.sbuf_tensor("l1_h", [P, NT, D], F32) as h:
                    layer_norm(core, "n3", xn, h, xnT, affineT=affineT)
                add_to(core, "b2", xn, None, row=dram["L1_b2"])
                feed_forward(core, "f1", inputs, ACT.Gelu, xn)
            layer_norm(core, "n4", xn, xn, gain=dram["L1_g2"], shift=dram["L1_be2"])
            add_to(core, "r1", x, xn)
        if 4 in stages:
            with ExitStack() as layer:
                affineT = load_affine(core, layer, "a6n", dram["L1f_ln1_g"], dram["L1f_ln1_b"])
                projections = load_projections(core, layer)
                layer_norm(core, "n5", x, xn)
                with nc.sbuf_tensor("l1f_h", [P, NT, D], F32) as h:
                    layer_norm(core, "n6", xn, h, xnT, affineT=affineT)
                self_attention(core, projections, xn)
            with ExitStack() as layer:
                routing = Routing(core, layer, "r1", 2)
                affineT = load_affine(core, layer, "a7n", dram["L1f_ln2_g"], dram["L1f_ln2_b"])
                gate = Gate(core, layer, "g1", dram["L1f_gate_w"], dram["L1f_gate_b"], dram["L1f_b2"], routing)
                experts = load_experts(core, layer, "e1", dram["L1f_W1"], dram["L1f_b1"], dram["L1f_W2"])
                add_to(core, "r2", x, xn)
                layer_norm(core, "n7", xn, xn, xnT, affineT=affineT)
                route(core, "g1", "top2", gate, routing, dram["scratch_acc"])
                routed_feed_forward(core, "m1", experts, routing, ACT.Relu, dram["scratch_acc"], affineT)
        if 5 in stages:
            with ExitStack() as layer:
                inputs = load_plain_cross_attention(core, layer)
                layer_norm(core, "n8", x, xn, xnT)
                plain_cross_attention(core, inputs)
        if 6 in stages:
            with ExitStack() as layer:
                routing = Routing(core, layer, "r2", EXPERTS, by_expert=True)
                gate = Gate(core, layer, "g2", dram["L2_Wg"], dram["L2_bg"], dram["L2_b2"], routing)
                experts = load_experts(core, layer, "e2", dram["L2_W1"], dram["L2_b1"], dram["L2_W2"])
                layer_norm(core, "n9", x, xn, xnT)
                route(core, "g2", "threshold", gate, routing, dram["scratch_acc"])
                routed_feed_forward(core, "m2", experts, routing, ACT.Relu, dram["scratch_acc"])
        if 7 in stages:
            with ExitStack() as layer:
                inputs = load_headed_cross_attention(core, layer, "a3", *(dram[f"L3_w{n}"] for n in "qkvo"), mask=dram["mask_bf"],
                                                     bq=dram["L3_bq"], bk=dram["L3_bk"], bv=dram["L3_bv"])
                layer_norm(core, "n10", x, xn, xnT)
                add_to(core, "bo3", x, None, row=dram["L3_bo"])
                headed_cross_attention(core, "a3", inputs, x)
        if 8 in stages:
            with ExitStack() as layer:
                routing = Routing(core, layer, "r3", 1)
                gate = Gate(core, layer, "g3", dram["L3_Wr"], dram["L3_br"], None, routing)
                experts = load_experts(core, layer, "e3", dram["L3_W1"], None, dram["L3_W2"])
                layer_norm(core, "n11", x, xn, xnT)
                route(core, "g3", "top1", gate, routing, dram["out"].rearrange("b s d -> (b s) d"))
                routed_feed_forward(core, "m3", experts, routing, ACT.Gelu, dram["out"].rearrange("b s d -> (b s) d"), last=True)
        else:
            store_output(core)



def laid_out(inputs):
    import numpy as np

    g = lambda n: np.asarray(inputs[n])
    t = lambda n: np.ascontiguousarray(np.swapaxes(np.asarray(inputs[n]), -1, -2))
    a = {}
    a["x"] = g("x")
    a["ctx"] = g("ctx_1024")
    a["ctxT"] = np.ascontiguousarray(g("ctx_1024").reshape(BATCH * KEYS, D).T)
    a["bias"] = np.ascontiguousarray(g("fside_Bx16xSxS2_0").reshape(BATCH, HEADS, SEQ // P, P, KEYS).transpose(0, 2, 3, 1, 4)
                                     .reshape(NT, P, HEADS, KEYS))
    a["mask_ik"] = g("mask_Bx1xS2_ik0").reshape(BATCH, KEYS)
    a["mask_bf"] = g("mask_Bx1xSxS2_bf0").reshape(TOK, KEYS)
    for n in ("Wk", "Wv", "Wo"):
        a[f"L0_{n}T"] = t(f"L0_xattn_{n}")
    a["L0_Wq"] = g("L0_xattn_Wq")
    for n in ("bq", "bk", "bv", "bo"):
        a[f"L0_{n}"] = g(f"L0_xattn_{n}")
    a["L0_WinT"], a["L0_Wout"] = t("L0_ffn_W_in"), g("L0_ffn_W_out")
    a["L0_bin"], a["L0_bout"] = g("L0_ffn_b_in"), g("L0_ffn_b_out")
    for n in ("Wq", "Wk", "Wv", "Wo"):
        a[f"L1_{n}T"] = t(f"L1_xattn_{n}")
    a["L1_W1T"], a["L1_W2T"] = t("L1_xattn_W1"), t("L1_xattn_W2")
    a["L1_b1"] = g("L1_xattn_b1")
    for n in ("b2", "g1", "be1", "g2", "be2"):
        a[f"L1_{n}"] = g(f"L1_xattn_{n}")
    for n in ("ln1_g", "ln1_b", "ln2_g", "ln2_b", "gate_w", "gate_b", "W1", "b1", "W2", "b2"):
        a[f"L1f_{n}"] = g(f"L1_ffn_{n}")
    a["L1f_wqkv"], a["L1f_bqkv"], a["L1f_wo"], a["L1f_bo"] = (g(f"L1_ffn_{n}") for n in ("w_qkv", "b_qkv", "w_o", "b_o"))
    for n in ("Wg", "bg", "W1", "b1", "W2", "b2"):
        a[f"L2_{n}"] = g(f"L2_ffn_{n}")
    for n in ("wq", "wk", "wv", "wo", "bq", "bk", "bv", "bo"):
        a[f"L3_{n}"] = g(f"L3_xattn_{n}")
    for n in ("Wr", "br", "W1", "W2"):
        a[f"L3_{n}"] = g(f"L3_ffn_{n}")
    a["L1f_bqk"], a["L1f_bv"] = a["L1f_bqkv"][:2 * D], a.pop("L1f_bqkv")[2 * D:]
    for n in ("L0_bq", "L0_bk", "L0_bv", "L0_bin", "L1_b1", "L1_g1", "L1_be1", "L1f_ln1_g", "L1f_ln1_b", "L1f_ln2_g", "L1f_ln2_b",
              "L1f_bqk", "L3_bq", "L3_bk"):
        a[n] = a[n].reshape(-1, P).T
    for n in ("L1f_b1", "L2_b1"):
        a[n] = a[n].reshape(-1, FB, P).transpose(2, 0, 1)
    return {k: np.ascontiguousarray(v) for k, v in a.items()}


def constants():
    import numpy as np
    return {
        "identity": np.eye(P, dtype=np.float32),
        "head_of": (np.arange(P)[:, None] // DK == np.arange(8)[None]).astype(np.float32),
        "rest_of": (np.arange(8 * REST)[:, None] // REST == np.arange(8)[None]).astype(np.float32),
        "before": np.triu(np.ones((P, P), np.float32), 1),
        "slot_ids": np.arange(EXPERTS * NT + 2, dtype=np.float32),
        "token_ids": np.ascontiguousarray(np.arange(TOK, dtype=np.int32).reshape(NT, P).T),
        "pad_ids": np.arange(TOK, TOK + P, dtype=np.int32)[:, None],
        "lane": np.arange(P, dtype=np.float32)[:, None],
        "rank": np.arange(EXPERTS, 0, -1).astype(np.float32),
    }


def scratch(nc, dram):
    dram["scratch_rows"] = nc.dram_tensor("scratch_rows", (PLACES, ROW), F32).ap()
    dram["scratch_acc"] = nc.dram_tensor("scratch_acc", (TOK, D), F32).ap()
    dram["scratch_parts"] = nc.dram_tensor("scratch_parts", (2, PARTS, D, TOK), BF16).ap()
    dram["scratch_max"] = nc.dram_tensor("scratch_max", (PARTS, BATCH * HEADS // 2, 2, SEQ), BF16).ap()


def kernel(**inputs):
    import concourse.bacc as _bacc
    from concourse import mybir as _mybir
    from concourse.bass_utils import run_bass_kernel_spmd as _run

    nc = _bacc.Bacc("TRN2", target_bir_lowering=False, num_devices=1)
    arrays = {**laid_out(inputs), **constants()}
    dram = {n: nc.dram_tensor(n, a.shape, _mybir.dt.from_np(a.dtype), kind="ExternalInput").ap() for n, a in arrays.items()}
    dram["out"] = nc.dram_tensor("out", (BATCH, SEQ, D), F32, kind="ExternalOutput").ap()
    scratch(nc, dram)
    program(nc, dram)
    r = _run(nc, [arrays], core_ids=[0])
    return r.results[0]["out"]
```
